# Optimizing a Trainium2 kernel written in Bass

```python
import numpy as np
import jax
import jax.numpy as jnp

def _softmax(x, axis=-1):
    return jax.nn.softmax(x, axis=axis)

def _gelu(x):
    return jax.nn.gelu(x, approximate=True)

def _silu(x):
    return jax.nn.silu(x)

def _sigmoid(x):
    return jax.nn.sigmoid(x)

def _layernorm(x, axis=-1, eps=1e-05):
    m = jnp.mean(x, axis=axis, keepdims=True)
    v = jnp.var(x, axis=axis, keepdims=True)
    return (x - m) / jnp.sqrt(v + eps)

def _scatter_add(tgt, idx, src, axis=0):
    return tgt.at[idx].add(src)

def _segment_sum(src, seg, n):
    return jax.ops.segment_sum(src, seg, n)
kernel_name = 'mk_audio_tower_d1_tok_audfeat1024_r4_d98b23'

def setup_inputs(seed: int=0):
    np.random.seed(seed)
    _w = jnp.asarray

    def _rec_inputs():
        import jax
        import jax.numpy as jnp
        _rk = jax.random.key(seed)
        x = 0.00021031 + 1.00007 * jax.random.normal(jax.random.fold_in(_rk, 1), (32, 750, 256), jnp.float32)
        return x
    x = _rec_inputs()

    def _L0_tok_setup():
        import jax, jax.numpy as jnp
        import numpy as np
        DIM = 256
        SEGMENT_SIZE = 256
        DILATION_RATE = 2
        key = jax.random.key(seed)
        x = jax.random.normal(key, (4, 2048, DIM), dtype=jnp.float32)
        return {'x': x}
    _L0_tok_all = _L0_tok_setup()
    _L0_tok_in = {k: v for k, v in _L0_tok_all.items() if k in ()}
    del _L0_tok_all

    def _L0_attn_setup():
        import jax, jax.numpy as jnp
        import numpy as np
        B, L, H = (2, 512, 256)
        NH, DK, DV = (4, 64, 64)
        CONV_K, FIR_S, FIR_L = (4, 3, 63)
        GATE_IN = H + 4 * 2 * NH
        MLP_H = 2 * H
        CHUNK = 32

        def l2norm(x):
            return x * jax.lax.rsqrt(jnp.sum(x * x, -1, keepdims=True) + 1e-06)

        def causal_dwconv(x, w):
            k = w.shape[-1]
            xc = jnp.pad(jnp.transpose(x, (0, 2, 1)), ((0, 0), (0, 0), (k - 1, 0)))
            y = jax.lax.conv_general_dilated(xc, w[:, None, :], (1,), 'VALID', feature_group_count=w.shape[0], dimension_numbers=('NCH', 'OIH', 'NCH'))
            return jnp.transpose(y, (0, 2, 1))

        def delta_rule_chunkwise(q, k, v, beta, chunk=CHUNK):
            b, h, Lp, dk = q.shape
            dv = v.shape[-1]
            n = Lp // chunk
            q = l2norm(q)
            k = l2norm(k)
            v = v * beta[..., None]
            kb = k * beta[..., None]
            qc, kc, vc, kbc = (t.reshape(b, h, n, chunk, -1) for t in (q, k, v, kb))
            A = jnp.tril(jnp.einsum('bhnid,bhnjd->bhnij', kbc, kc), -1)
            T = jnp.linalg.inv(jnp.eye(chunk, dtype=q.dtype) + A)
            u = T @ vc
            w = T @ kbc

            def step(S, inp):
                qi, ki, ui, wi = inp
                attn = jnp.tril(qi @ jnp.swapaxes(ki, -1, -2))
                u2 = ui - wi @ S
                oi = qi @ S + attn @ u2
                return (S + jnp.swapaxes(ki, -1, -2) @ u2, oi)
            S0 = jnp.zeros((b, h, dk, dv), q.dtype)
            xs = tuple((jnp.moveaxis(t, 2, 0) for t in (qc, kc, u, w)))
            S, o = jax.lax.scan(step, S0, xs)
            o = jnp.moveaxis(o, 0, 2).reshape(b, h, Lp, dv)
            return (o, S)

        def branch_stats(x):
            m = x.mean(-1)
            s = jnp.sqrt(jnp.maximum(x.var(-1), 1e-06))
            return jnp.concatenate([m, s], -1)
        key = jax.random.key(seed)
        ks = jax.random.split(key, 16)
        f32 = jnp.float32

        def dirac(k_, shape):
            f = 0.01 * jax.random.normal(k_, shape, f32)
            return f.at[..., shape[-1] // 2].add(1.0)
        b2 = jnp.zeros((NH * 4,), f32).at[jnp.arange(NH) * 4 + 3].set(2.0)
        return {'hidden_states': jax.random.normal(ks[0], (B, L, H), f32), 'Wq': 0.02 * jax.random.normal(ks[1], (H, NH * DK), f32), 'Wk': 0.02 * jax.random.normal(ks[2], (H, NH * DK), f32), 'Wv': 0.02 * jax.random.normal(ks[3], (H, NH * DV), f32), 'Wb': 0.02 * jax.random.normal(ks[4], (H, NH), f32), 'conv_q_w': 0.2 * jax.random.normal(ks[5], (NH * DK, CONV_K), f32), 'conv_k_w': 0.2 * jax.random.normal(ks[6], (NH * DK, CONV_K), f32), 'conv_v_w': 0.2 * jax.random.normal(ks[7], (NH * DV, CONV_K), f32), 'fir_short_w': dirac(ks[8], (NH, DV, FIR_S)), 'fir_long_w': dirac(ks[9], (NH, DV, FIR_L)), 'mlp_w1': 0.02 * jax.random.normal(ks[10], (GATE_IN, MLP_H), f32), 'mlp_b1': jnp.zeros((MLP_H,), f32), 'mlp_w2': 0.02 * jax.random.normal(ks[11], (MLP_H, NH * 4), f32), 'mlp_b2': b2, 'gate_log_temp': jnp.full((NH,), np.log(1.2), f32), 'o_norm_w': jnp.ones((DV,), f32), 'Wo': 0.02 * jax.random.normal(ks[12], (NH * DV, H), f32)}
    _L0_attn_all = _L0_attn_setup()
    _L0_attn_in = {k: v for k, v in _L0_attn_all.items() if k in ('Wq', 'Wk', 'Wv', 'Wb', 'conv_q_w', 'conv_k_w', 'conv_v_w', 'fir_short_w', 'fir_long_w', 'mlp_w1', 'mlp_b1', 'mlp_w2', 'mlp_b2', 'gate_log_temp', 'o_norm_w', 'Wo')}
    del _L0_attn_all

    def _L0_ffn_setup():
        import jax, jax.numpy as jnp
        import numpy as np
        B, T, D_MODEL = (4, 512, 256)
        N_EXPERTS, TOP_K, D_EXPERT = (6, 2, 128)
        QUANT_TEMP = 0.3
        _ANCHOR_IDS = [63, 6, 0, 18, 45, 27]

        def _q6_idx_to_vertex(idx):
            bits = [idx >> 5 - b & 1 for b in range(6)]
            return [2.0 * b - 1.0 for b in bits]

        def _anchors():
            return jnp.asarray(np.array([_q6_idx_to_vertex(i) for i in _ANCHOR_IDS], dtype=np.float32))

        def _router(x, proj_w, anchors, routing_temp):
            z = jnp.einsum('btd,ed->bte', x, proj_w)
            q = jnp.tanh(z / QUANT_TEMP)
            dot = jnp.einsum('btd,ed->bte', q, anchors)
            hamming = (6.0 - dot) * 0.5
            logits = -hamming / jnp.clip(routing_temp, 0.1)
            topk_logits, topk_idx = jax.lax.top_k(logits, TOP_K)
            topk_w = jax.nn.softmax(topk_logits, axis=-1)
            onehot = jax.nn.one_hot(topk_idx, N_EXPERTS, dtype=x.dtype)
            expert_weights = jnp.einsum('btke,btk->bte', onehot, topk_w)
            return (expert_weights, q)
        key = jax.random.key(seed)
        k_x, k_p, k_w1, k_w2 = jax.random.split(key, 4)
        x = jax.random.normal(k_x, (B, T, D_MODEL), dtype=jnp.float32)
        proj_w = jax.random.normal(k_p, (6, D_MODEL), dtype=jnp.float32) * 0.02
        anchors = _anchors()
        routing_temp = jnp.array(1.0, dtype=jnp.float32)
        s1 = 1.0 / np.sqrt(D_MODEL)
        s2 = 1.0 / np.sqrt(D_EXPERT)
        w1 = jax.random.uniform(k_w1, (N_EXPERTS, D_MODEL, D_EXPERT), jnp.float32, -s1, s1)
        w2 = jax.random.uniform(k_w2, (N_EXPERTS, D_EXPERT, D_MODEL), jnp.float32, -s2, s2)
        return {'x': x, 'proj_w': proj_w, 'anchors': anchors, 'routing_temp': routing_temp, 'w1': w1, 'w2': w2}
    _L0_ffn_all = _L0_ffn_setup()
    _L0_ffn_in = {k: v for k, v in _L0_ffn_all.items() if k in ('proj_w', 'anchors', 'routing_temp', 'w1', 'w2')}
    del _L0_ffn_all
    return {'x': x, 'L0_attn_Wq': _L0_attn_in['Wq'], 'L0_attn_Wk': _L0_attn_in['Wk'], 'L0_attn_Wv': _L0_attn_in['Wv'], 'L0_attn_Wb': _L0_attn_in['Wb'], 'L0_attn_conv_q_w': _L0_attn_in['conv_q_w'], 'L0_attn_conv_k_w': _L0_attn_in['conv_k_w'], 'L0_attn_conv_v_w': _L0_attn_in['conv_v_w'], 'L0_attn_fir_short_w': _L0_attn_in['fir_short_w'], 'L0_attn_fir_long_w': _L0_attn_in['fir_long_w'], 'L0_attn_mlp_w1': _L0_attn_in['mlp_w1'], 'L0_attn_mlp_b1': _L0_attn_in['mlp_b1'], 'L0_attn_mlp_w2': _L0_attn_in['mlp_w2'], 'L0_attn_mlp_b2': _L0_attn_in['mlp_b2'], 'L0_attn_gate_log_temp': _L0_attn_in['gate_log_temp'], 'L0_attn_o_norm_w': _L0_attn_in['o_norm_w'], 'L0_attn_Wo': _L0_attn_in['Wo'], 'L0_ffn_proj_w': _L0_ffn_in['proj_w'], 'L0_ffn_anchors': _L0_ffn_in['anchors'], 'L0_ffn_routing_temp': _L0_ffn_in['routing_temp'], 'L0_ffn_w1': _L0_ffn_in['w1'], 'L0_ffn_w2': _L0_ffn_in['w2']}

def reference(x, L0_attn_Wq, L0_attn_Wk, L0_attn_Wv, L0_attn_Wb, L0_attn_conv_q_w, L0_attn_conv_k_w, L0_attn_conv_v_w, L0_attn_fir_short_w, L0_attn_fir_long_w, L0_attn_mlp_w1, L0_attn_mlp_b1, L0_attn_mlp_w2, L0_attn_mlp_b2, L0_attn_gate_log_temp, L0_attn_o_norm_w, L0_attn_Wo, L0_ffn_proj_w, L0_ffn_anchors, L0_ffn_routing_temp, L0_ffn_w1, L0_ffn_w2):
    import jax
    import jax.numpy as jnp

    def _L0_tok_ref(x):
        import jax, jax.numpy as jnp
        import numpy as np
        DIM = 256
        SEGMENT_SIZE = 256
        DILATION_RATE = 2
        B, S, D = x.shape
        pad = -S % SEGMENT_SIZE
        x = jnp.pad(x, ((0, 0), (0, pad), (0, 0)))
        x = x.reshape(B, -1, SEGMENT_SIZE, D)
        x = x[:, :, ::DILATION_RATE, :]
        q = k = v = x
        scale = 1.0 / jnp.sqrt(jnp.asarray(D, dtype=x.dtype))
        scores = jnp.einsum('bsqd,bskd->bsqk', q, k) * scale
        probs = jax.nn.softmax(scores, axis=-1)
        attn = jnp.einsum('bsqk,bskd->bsqd', probs, v)
        return attn.reshape(B, -1, D)

    def _L0_attn_ref(hidden_states, Wq, Wk, Wv, Wb, conv_q_w, conv_k_w, conv_v_w, fir_short_w, fir_long_w, mlp_w1, mlp_b1, mlp_w2, mlp_b2, gate_log_temp, o_norm_w, Wo):
        import jax, jax.numpy as jnp
        import numpy as np
        B, L, H = (2, 512, 256)
        NH, DK, DV = (4, 64, 64)
        CONV_K, FIR_S, FIR_L = (4, 3, 63)
        GATE_IN = H + 4 * 2 * NH
        MLP_H = 2 * H
        CHUNK = 32

        def l2norm(x):
            return x * jax.lax.rsqrt(jnp.sum(x * x, -1, keepdims=True) + 1e-06)

        def causal_dwconv(x, w):
            k = w.shape[-1]
            xc = jnp.pad(jnp.transpose(x, (0, 2, 1)), ((0, 0), (0, 0), (k - 1, 0)))
            y = jax.lax.conv_general_dilated(xc, w[:, None, :], (1,), 'VALID', feature_group_count=w.shape[0], dimension_numbers=('NCH', 'OIH', 'NCH'))
            return jnp.transpose(y, (0, 2, 1))

        def delta_rule_chunkwise(q, k, v, beta, chunk=CHUNK):
            b, h, Lp, dk = q.shape
            dv = v.shape[-1]
            n = Lp // chunk
            q = l2norm(q)
            k = l2norm(k)
            v = v * beta[..., None]
            kb = k * beta[..., None]
            qc, kc, vc, kbc = (t.reshape(b, h, n, chunk, -1) for t in (q, k, v, kb))
            A = jnp.tril(jnp.einsum('bhnid,bhnjd->bhnij', kbc, kc), -1)
            T = jnp.linalg.inv(jnp.eye(chunk, dtype=q.dtype) + A)
            u = T @ vc
            w = T @ kbc

            def step(S, inp):
                qi, ki, ui, wi = inp
                attn = jnp.tril(qi @ jnp.swapaxes(ki, -1, -2))
                u2 = ui - wi @ S
                oi = qi @ S + attn @ u2
                return (S + jnp.swapaxes(ki, -1, -2) @ u2, oi)
            S0 = jnp.zeros((b, h, dk, dv), q.dtype)
            xs = tuple((jnp.moveaxis(t, 2, 0) for t in (qc, kc, u, w)))
            S, o = jax.lax.scan(step, S0, xs)
            o = jnp.moveaxis(o, 0, 2).reshape(b, h, Lp, dv)
            return (o, S)

        def branch_stats(x):
            m = x.mean(-1)
            s = jnp.sqrt(jnp.maximum(x.var(-1), 1e-06))
            return jnp.concatenate([m, s], -1)
        x = hidden_states
        b, l, _ = x.shape
        q = jax.nn.silu(causal_dwconv(x @ Wq, conv_q_w)).reshape(b, l, NH, DK)
        k = jax.nn.silu(causal_dwconv(x @ Wk, conv_k_w)).reshape(b, l, NH, DK)
        v = jax.nn.silu(causal_dwconv(x @ Wv, conv_v_w)).reshape(b, l, NH, DV)
        beta = jax.nn.sigmoid(x @ Wb)
        delta_out, _S = delta_rule_chunkwise(jnp.transpose(q, (0, 2, 1, 3)), jnp.transpose(k, (0, 2, 1, 3)), jnp.transpose(v, (0, 2, 1, 3)), jnp.transpose(beta, (0, 2, 1)))
        delta_out = jnp.transpose(delta_out, (0, 2, 1, 3))
        vf = v.reshape(b, l, NH * DV)
        fir_short = causal_dwconv(vf, fir_short_w.reshape(NH * DV, FIR_S)).reshape(b, l, NH, DV)
        fir_long = causal_dwconv(vf, fir_long_w.reshape(NH * DV, FIR_L)).reshape(b, l, NH, DV)
        gate_in = jnp.concatenate([x, branch_stats(fir_short), branch_stats(fir_long), branch_stats(delta_out), branch_stats(v)], -1)
        logits = jax.nn.gelu(gate_in @ mlp_w1 + mlp_b1, approximate=False) @ mlp_w2 + mlp_b2
        temp = jax.nn.softplus(gate_log_temp) + 0.0001
        logits = logits.reshape(b, l, NH, 4) / temp[None, None, :, None]
        w = jax.nn.softmax(logits, -1)
        o = w[..., 0:1] * fir_short + w[..., 1:2] * fir_long + w[..., 2:3] * delta_out + w[..., 3:4] * v
        o = o * jax.lax.rsqrt(jnp.mean(o * o, -1, keepdims=True) + 1e-05) * o_norm_w
        return o.reshape(b, l, NH * DV) @ Wo

    def _L0_ffn_ref(x, proj_w, anchors, routing_temp, w1, w2):
        import jax, jax.numpy as jnp
        import numpy as np
        B, T, D_MODEL = (4, 512, 256)
        N_EXPERTS, TOP_K, D_EXPERT = (6, 2, 128)
        QUANT_TEMP = 0.3
        _ANCHOR_IDS = [63, 6, 0, 18, 45, 27]

        def _q6_idx_to_vertex(idx):
            bits = [idx >> 5 - b & 1 for b in range(6)]
            return [2.0 * b - 1.0 for b in bits]

        def _anchors():
            return jnp.asarray(np.array([_q6_idx_to_vertex(i) for i in _ANCHOR_IDS], dtype=np.float32))

        def _router(x, proj_w, anchors, routing_temp):
            z = jnp.einsum('btd,ed->bte', x, proj_w)
            q = jnp.tanh(z / QUANT_TEMP)
            dot = jnp.einsum('btd,ed->bte', q, anchors)
            hamming = (6.0 - dot) * 0.5
            logits = -hamming / jnp.clip(routing_temp, 0.1)
            topk_logits, topk_idx = jax.lax.top_k(logits, TOP_K)
            topk_w = jax.nn.softmax(topk_logits, axis=-1)
            onehot = jax.nn.one_hot(topk_idx, N_EXPERTS, dtype=x.dtype)
            expert_weights = jnp.einsum('btke,btk->bte', onehot, topk_w)
            return (expert_weights, q)
        expert_weights, q = _router(x, proj_w, anchors, routing_temp)
        h = jax.nn.gelu(jnp.einsum('btd,edh->bteh', x, w1))
        out = jnp.einsum('bteh,ehd,bte->btd', h, w2, expert_weights)
        return out
    h = _L0_tok_ref(x)
    h = h + _L0_attn_ref(_layernorm(h, axis=-1), L0_attn_Wq, L0_attn_Wk, L0_attn_Wv, L0_attn_Wb, L0_attn_conv_q_w, L0_attn_conv_k_w, L0_attn_conv_v_w, L0_attn_fir_short_w, L0_attn_fir_long_w, L0_attn_mlp_w1, L0_attn_mlp_b1, L0_attn_mlp_w2, L0_attn_mlp_b2, L0_attn_gate_log_temp, L0_attn_o_norm_w, L0_attn_Wo)
    h = h + _L0_ffn_ref(_layernorm(h, axis=-1), L0_ffn_proj_w, L0_ffn_anchors, L0_ffn_routing_temp, L0_ffn_w1, L0_ffn_w2)
    return h

_drawn_inputs = setup_inputs


def setup_inputs(seed=0):
    import zlib

    import numpy as np

    out = dict(_drawn_inputs(seed))
    spreads = {'L0_attn_mlp_b1': (0.0, 0.8),
     'L0_attn_gate_log_temp': (0.18232156336307526, 0.6),
     'L0_attn_o_norm_w': (1.0, 0.2)}
    factors = {'L0_attn_Wq': 3.491,
     'L0_attn_Wk': 3.453,
     'L0_attn_Wb': 8.0,
     'L0_attn_conv_q_w': 3.518,
     'L0_attn_conv_k_w': 3.372,
     'L0_attn_mlp_w1': 6.257,
     'L0_attn_mlp_w2': 6.189}
    for name, (base, spread) in spreads.items():
        noise = np.random.default_rng([zlib.crc32(name.encode()), seed]).standard_normal(out[name].shape)
        drawn = base * np.exp(spread * noise) if base else spread * noise
        out[name] = jnp.asarray(drawn.astype(out[name].dtype))
    for name, factor in factors.items():
        out[name] = (out[name] * factor).astype(out[name].dtype)
    return out
```

```python
from contextlib import ExitStack

import concourse.bass as bass
from concourse import mybir

F32 = mybir.dt.float32
ALU = mybir.AluOpType
ACT = mybir.ActivationFunctionType
AX = mybir.AxisListType

P = 128
D = 256
HALF = D // P
SEG, STEP = 256, 2
BLK = 3
T = BLK * P
NH, DH = 4, 64
NM = BLK * NH
CK, FS, FL = 4, 3, 63
TW = P + FL - 1
GATE_S = 8 * NH
MLP = 2 * D
NE, DE, ND = 6, 128, 6
SC = 32
NQ = P // SC

QT, KBT, KT, KTOK, VTOK = (n * HALF * T for n in range(5))
RQ = 5 * HALF * T
VBS = RQ + NM
AW = VBS + NM
HF, XNT, FSF = (n * HALF * T for n in range(3))
BW = 3 * HALF * T


class Signal:

    def __init__(self, sem, per, primed=1):
        self.sem, self.per, self.primed = sem, per, primed

    def now(self, it, k=None):
        return self.sem, (it + self.primed) * self.per + (self.per if k is None else k)

    def before(self, it, back=1):
        return self.sem, (it + (self.primed - back + 1)) * self.per


def even_heads_first(blk, h):
    return (h % 2) * (NM // 2) + blk * (NH // 2) + h // 2


def audio_tower(nc, x, w, out):
    NB = x.shape[0]
    NSYS = NB * NM * NQ // P
    with ExitStack() as ctx:
        def sem(name):
            return ctx.enter_context(nc.semaphore(name))

        def banks():
            return [c.enter_context(nc.psum_tensor(f"bank{n}", [P, 512], F32)) for n in range(8)]

        signals = []

        def signal(name, per=1, primed=1):
            signals.append(Signal(sem(name), per, primed))
            return signals[-1]

        dram = {
            "packa": nc.dram_tensor("packa", [NB, P, AW], F32, kind="Internal").ap(),
            "packb": nc.dram_tensor("packb", [NB, P, BW], F32, kind="Internal").ap(),
            "systems": nc.dram_tensor("systems", [NB * NM * NQ, SC, SC], F32, kind="Internal").ap(),
            "taps": nc.dram_tensor("taps", [D, 512], F32, kind="Internal").ap(),
            "toeplitz": nc.dram_tensor("toeplitz", [P, D, TW], F32, kind="Internal").ap(),
        }
        c = ctx
        bank = banks()

        def sb(name, shape):
            return ctx.enter_context(nc.sbuf_tensor(name, shape, F32))

        v_all = sb("v_all", [P, D, BLK * NB])
        ident = sb("ident", [P, P])
        upper = sb("upper", [P, 2 * P])
        expanded = ctx.enter_context(nc.semaphore("expanded"))
        shared = dict(expanded=expanded, NB=NB, NSYS=NSYS, dram=dram, bank=bank, v_all=v_all, ident=ident, upper=upper)
        make_constants(nc, ctx, ident, upper)
        first_phase(nc, x, w, shared)
        second_phase(nc, w, shared)
        third_phase(nc, w, out, shared)


def make_constants(nc, ctx, ident, upper):
    made = ctx.enter_context(nc.semaphore("made"))
    with nc.Block() as block:
        @block.gpsimd
        def _(pool):
            pool.memset(ident[:, :], 0.0).then_inc(made, 1)
            pool.memset(upper[:, 0:P], 1.0).then_inc(made, 1)
            pool.memset(upper[:, P:], -1.0).then_inc(made, 1)
            pool.wait_ge(made, 3)
            pool.affine_select(out=ident[:, :], in_=ident[:, :], compare_op=ALU.not_equal, fill=1.0,
                               base=0, pattern=[[-1, P]], channel_multiplier=1).then_inc(made, 1)
            pool.affine_select(out=upper[:, 0:P], in_=upper[:, 0:P], compare_op=ALU.is_ge, fill=0.0,
                               base=0, pattern=[[1, P]], channel_multiplier=-1).then_inc(made, 1)
            pool.affine_select(out=upper[:, P:], in_=upper[:, P:], compare_op=ALU.is_gt, fill=0.0,
                               base=0, pattern=[[1, P]], channel_multiplier=-1).then_inc(made, 1)
            pool.wait_ge(made, 6)


def prime(nc, signals):
    with nc.Block() as block:
        @block.sync
        def _(sp):
            for g in signals:
                sp.sem_inc(g.sem, g.per * g.primed)


def first_phase(nc, x, w, shared):
    NB, dram, bank, v_all, ident, upper, expanded = (
        shared[k] for k in ("NB", "dram", "bank", "v_all", "ident", "upper", "expanded"))
    with ExitStack() as c:
        def sb(name, shape):
            return c.enter_context(nc.sbuf_tensor(name, shape, F32))

        signals = []

        def signal(name, per=1, primed=1):
            signals.append(Signal(c.enter_context(nc.semaphore(name)), per, primed))
            return signals[-1]

        loaded = c.enter_context(nc.semaphore("p1_weights"))
        setup = c.enter_context(nc.semaphore("p1_setup"))
        started = c.enter_context(nc.semaphore("p1_started"))
        wqkv = sb("wqkv", [P, HALF, 3 * D])
        wb = sb("wb", [P, HALF, NH])
        convw = sb("convw", [P, 3 * HALF, CK])
        firw = sb("firw", [P, HALF, FS])
        flw = sb("flw", [P, HALF, FL])
        flr = sb("flr", [P, HALF, 512])
        headsel = sb("headsel", [P, 2])
        xs = [sb(f"x{s}", [P, BLK, D]) for s in range(2)]
        pa = [sb(f"pa{s}", [P, AW]) for s in range(2)]
        pb = [sb(f"pb{s}", [P, BW]) for s in range(2)]
        xT = sb("xT", [P, BLK, HALF, P])
        E = sb("E", [P, BLK, P])
        PT = sb("PT", [P, BLK, P])
        xn = sb("xn", [P, BLK, D])
        Y = sb("Y", [P, 3 * HALF, T])
        VT = sb("VT", [P, HALF, T])
        SQ = sb("SQ", [P, 2 * HALF, T])
        fsT = sb("fsT", [P, HALF, T])
        fst = sb("fst", [P, HALF, T])
        KB = sb("KB", [P, BLK, D])
        AT = sb("AT", [P, NM, P])
        mx, negmax, rs, rinv, veps, lnv, rstd = (sb(f"s{n}", [P, BLK]) for n in range(7))
        st = sb("st", [P, BLK, 6])
        mv = sb("mv", [P, BLK, 2])
        eb, b1, beta, kbs = (sb(f"t{n}", [P, NM]) for n in range(4))
        RS, LR, RR = (sb(f"r{n}", [P, BLK, 2, NH]) for n in range(3))

        def field(buf, at):
            return buf[:, at:at + HALF * T]

        def chans(buf, at):
            return field(buf, at).rearrange("p (a t) -> p a t", a=HALF)

        def toks(buf, at):
            return field(buf, at).rearrange("p (b c) -> p b c", b=BLK)

        x_loaded = [signal(f"x_loaded{s}", 32) for s in range(2)]
        packs_stored = [signal(f"packs_stored{s}", 32) for s in range(2)]
        at_stored = signal("at_stored", 16 * NQ)
        xT_ready = signal("xT_ready", 2)
        scores_ready = signal("scores_ready")
        probsT_ready = signal("probsT_ready")
        attn_ready = signal("attn_ready", 1, primed=2)
        xnT_ready = signal("xnT_ready", 2)
        beta_ready = signal("beta_ready")
        proj_ready = signal("proj_ready", 6)
        ssq_ready = signal("ssq_ready")
        ktok_ready = signal("ktok_ready")
        vtok_ready = signal("vtok_ready")
        fs_ready = signal("fs_ready")
        kbT_ready = signal("kbT_ready", 2)
        at_ready = signal("at_ready")
        xT01_copied = signal("xT01_copied")
        xT2_copied = signal("xT2_copied")
        max_found = signal("max_found")
        negmax_ready = signal("negmax_ready")
        probs_ready = signal("probs_ready", BLK)
        rinv_ready = signal("rinv_ready")
        probsT_copied = signal("probsT_copied")
        h_ready = signal("h_ready", BLK)
        stats_done = signal("stats_done", BLK)
        mv_ready = signal("mv_ready", BLK)
        veps_ready = signal("veps_ready")
        lnv_ready = signal("lnv_ready")
        rstd_ready = signal("rstd_ready")
        xn_ready = signal("xn_ready", BLK)
        xnT0_copied = signal("xnT0_copied")
        xnT1_copied = signal("xnT1_copied")
        eb_ready = signal("eb_ready")
        beta_step = signal("beta_step", 2)
        tap_done = signal("tap_done", 6)
        conv_step = signal("conv_step", 18)
        silu_done = signal("silu_done", 6)
        sq_ready = signal("sq_ready", 2)
        rs_ready = signal("rs_ready")
        lr_ready = signal("lr_ready")
        rr_ready = signal("rr_ready")
        vbs_ready = signal("vbs_ready")
        scales_ready = signal("scales_ready")
        ktok_copied = signal("ktok_copied")
        vtok_copied = signal("vtok_copied")
        fir_step = signal("fir_step", 5)
        fs_copied = signal("fs_copied")
        kb_ready = signal("kb_ready")
        kbT0_copied = signal("kbT0_copied")
        kbT1_copied = signal("kbT1_copied")
        at_copied = signal("at_copied")
        v_kept = signal("v_kept")
        prime(nc, signals)

        proj_bank = [bank[n] for n in (4, 5, 6, 7, 0, 1)]

        with nc.Block() as block:
            @block.vector
            def _(dve):
                for half in range(2):
                    for head in range(2):
                        dve.memset(headsel[half * DH:(half + 1) * DH, head:head + 1], float(half == head)).then_inc(started, 1)
                dve.wait_ge(started, 4)

            @block.sync
            def _(sp):
                for n, name in enumerate(("Wq", "Wk", "Wv")):
                    sp.dma_start(wqkv[:, :, n * D:(n + 1) * D],
                                 w[name].rearrange("(a p) n -> p a n", a=HALF)).then_inc(loaded, 16)
                    sp.dma_start(convw[:, n * HALF:(n + 1) * HALF, :],
                                 w[f"conv_{name[1]}_w"].rearrange("(a p) k -> p a k", a=HALF)).then_inc(loaded, 16)
                sp.dma_start(wb[:, :, :], w["Wb"].rearrange("(a p) n -> p a n", a=HALF)).then_inc(loaded, 16)
                sp.dma_start(firw[:, :, :], w["fir_short_w"].rearrange("(a g) v k -> (g v) a k", a=HALF)).then_inc(loaded, 16)
                sp.dma_start(flw[:, :, :], w["fir_long_w"].rearrange("(a g) v k -> (g v) a k", a=HALF)).then_inc(loaded, 16)
                sp.wait_ge(loaded, 16 * 9)
                sp.wait_ge(setup, 5)
                sp.dma_start(dram["taps"].rearrange("(a p) n -> p a n", a=HALF), flr[:, :, :]).then_inc(loaded, 16)
                sp.wait_ge(loaded, 16 * 10)
                tp = dram["taps"].tensor
                for h in range(HALF):
                    sp.dma_start(dram["toeplitz"][:, h * P:(h + 1) * P, :].rearrange("p c t -> c p t"),
                                 bass.AP(tp, 512 * P * h + P - 1, [[512, P], [-1, P], [1, TW]])).then_inc(expanded, 16)

            @block.gpsimd
            def _(pool):
                pool.memset(flr[:, :, :], 0.0).then_inc(setup, 1)
                pool.memset(xs[0][:, BLK - 1, :], 0.0).then_inc(setup, 1)
                pool.memset(xs[1][:, BLK - 1, :], 0.0).then_inc(setup, 1)
                pool.wait_ge(loaded, 16 * 9)
                pool.wait_ge(setup, 3)
                for a in range(HALF):
                    pool.tensor_copy(flr[:, a, P - 1:P - 1 + FL], flw[:, a, ::-1]).then_inc(setup, 1)
                pool.wait_ge(setup, 5)

        with nc.Block() as block:
            @block.sync
            def _(sp):
                def load_x(it, s):
                    sp.wait_ge(*attn_ready.before(it, 2))
                    sp.dma_start(xs[s][:, 0:2, :], x[it, 0:2 * SEG, :].rearrange(
                        "(b p two) n -> p b two n", b=2, two=STEP)[:, :, 0, :]).then_inc(x_loaded[s].sem, 16)
                    rows = (x.shape[1] - 2 * SEG) // STEP
                    sp.dma_start(xs[s][0:rows, 2, :], x[it, 2 * SEG:2 * SEG + rows * STEP, :].rearrange(
                        "(p two) n -> p two n", two=STEP)[:, 0, :]).then_inc(x_loaded[s].sem, 16)

                def store_packs(it, s):
                    sp.wait_ge(*fs_copied.now(it))
                    sp.wait_ge(*kbT0_copied.now(it))
                    sp.wait_ge(*kbT1_copied.now(it))
                    sp.wait_ge(*xnT1_copied.now(it))
                    sp.dma_start(dram["packa"][it], pa[s][:, :]).then_inc(packs_stored[s].sem, 16)
                    sp.dma_start(dram["packb"][it], pb[s][:, :]).then_inc(packs_stored[s].sem, 16)
                    sp.wait_ge(*at_copied.now(it))
                    sysv = dram["systems"].rearrange("(n m q) j i -> n q j m i", m=NM, q=NQ)
                    for q in range(NQ):
                        sp.dma_start(sysv[it, q], AT[q * SC:(q + 1) * SC, :, q * SC:(q + 1) * SC])\
                            .then_inc(at_stored.sem, 16)

                load_x(0, 0)
                with sp.Fori(0, NB // 2 - 1) as i:
                    load_x(2 * i + 1, 1)
                    store_packs(2 * i, 0)
                    load_x(2 * i + 2, 0)
                    store_packs(2 * i + 1, 1)
                load_x(NB - 1, 1)
                store_packs(NB - 2, 0)
                store_packs(NB - 1, 1)
                for s in range(2):
                    sp.wait_ge(*packs_stored[s].before(NB // 2))
                sp.wait_ge(*at_stored.before(NB))

            @block.tensor
            def _(pe):
                with pe.Fori(0, NB // 2) as i:
                    for s in range(2):
                        it = i * 2 + s
                        xnT, qT, kT, kbT = chans(pb[s], XNT), chans(pa[s], QT), chans(pa[s], KT), chans(pa[s], KBT)
                        pe.wait_ge(*x_loaded[s].now(i))
                        pe.wait_ge(*fs_copied.before(it))
                        for b in range(BLK):
                            for a in range(HALF):
                                o = (b % 2) * D + a * P
                                mm = pe.transpose(bank[b // 2][:, o:o + P], xs[s][:, b, a * P:(a + 1) * P], ident[:, :])
                            if b:
                                mm.then_inc(xT_ready.sem, 1)
                        pe.wait_ge(*xT01_copied.now(it))
                        pe.wait_ge(*xT2_copied.now(it))
                        pe.wait_ge(*kbT0_copied.before(it))
                        for b in range(BLK):
                            for a in range(HALF):
                                mm = pe.matmul(bank[2][:, b * P:(b + 1) * P], xT[:, b, a, :], xT[:, b, a, :],
                                               start=(a == 0), stop=(a == HALF - 1))
                        mm.then_inc(scores_ready.sem, 1)
                        pe.wait_ge(*probs_ready.now(it))
                        pe.wait_ge(*kbT1_copied.before(it))
                        for b in range(BLK):
                            mm = pe.transpose(bank[3][:, b * P:(b + 1) * P], E[:, b, :], ident[:, :])
                        mm.then_inc(probsT_ready.sem, 1)
                        pe.wait_ge(*probsT_copied.now(it))
                        pe.wait_ge(*at_copied.before(it))
                        for b in range(BLK):
                            mm = pe.matmul(bank[4 + b // 2][:, (b % 2) * D:(b % 2 + 1) * D], PT[:, b, :], xs[s][:, b, :],
                                           start=True, stop=True)
                        mm.then_inc(attn_ready.sem, 1)
                        pe.wait_ge(*xn_ready.now(it))
                        for a in range(HALF):
                            for b in range(BLK):
                                mm = pe.transpose(bank[a][:, b * P:(b + 1) * P], xn[:, b, a * P:(a + 1) * P], ident[:, :])
                            mm.then_inc(xnT_ready.sem, 1)
                        pe.wait_ge(*xnT0_copied.now(it))
                        pe.wait_ge(*xnT1_copied.now(it))
                        for b in range(BLK):
                            for a in range(HALF):
                                mm = pe.matmul(bank[2][:, b * NH:(b + 1) * NH], xnT[:, a, b * P:(b + 1) * P], wb[:, a, :],
                                               start=(a == 0), stop=(a == HALF - 1))
                        mm.then_inc(beta_ready.sem, 1)
                        for j in range(3 * HALF):
                            for a in range(HALF):
                                mm = pe.matmul(proj_bank[j][:, 0:T], wqkv[:, a, j * P:(j + 1) * P], xnT[:, a, :],
                                               start=(a == 0), stop=(a == HALF - 1))
                            mm.then_inc(proj_ready.sem, 1)
                        pe.wait_ge(*sq_ready.now(it))
                        pe.wait_ge(*eb_ready.now(it))
                        for b in range(BLK):
                            for n in range(2 * HALF):
                                o = b * 2 * NH + n * 2
                                mm = pe.matmul(bank[2][:, o:o + 2], SQ[:, n, b * P:(b + 1) * P], headsel[:, :],
                                               start=True, stop=True)
                        mm.then_inc(ssq_ready.sem, 1)
                        pe.wait_ge(*silu_done.now(it, 4))
                        for b in range(BLK):
                            for a in range(HALF):
                                o = (b % 2) * D + a * P
                                mm = pe.transpose(bank[4 + b // 2][:, o:o + P], kT[:, a, b * P:(b + 1) * P], ident[:, :])
                        mm.then_inc(ktok_ready.sem, 1)
                        pe.wait_ge(*silu_done.now(it, 6))
                        for b in range(BLK):
                            for a in range(HALF):
                                o = (b % 2) * D + a * P
                                mm = pe.transpose(bank[6 + b // 2][:, o:o + P], VT[:, a, b * P:(b + 1) * P], ident[:, :])
                        mm.then_inc(vtok_ready.sem, 1)
                        pe.wait_ge(*kb_ready.now(it))
                        for a in range(HALF):
                            for b in range(BLK):
                                mm = pe.transpose(bank[2 + a][:, b * P:(b + 1) * P], KB[:, b, a * P:(a + 1) * P], ident[:, :])
                            mm.then_inc(kbT_ready.sem, 1)
                        pe.wait_ge(*fir_step.now(it))
                        for b in range(BLK):
                            for a in range(HALF):
                                o = (b % 2) * D + a * P
                                mm = pe.transpose(bank[b // 2][:, o:o + P], fsT[:, a, b * P:(b + 1) * P], ident[:, :])
                        mm.then_inc(fs_ready.sem, 1)
                        pe.wait_ge(*kbT0_copied.now(it))
                        pe.wait_ge(*kbT1_copied.now(it))
                        pe.wait_ge(*ktok_copied.now(it))
                        pe.wait_ge(*vtok_copied.now(it))
                        for b in range(BLK):
                            for hh in range(NH // 2):
                                for odd in range(2):
                                    e = b * (NH // 2) + hh
                                    rows = slice(odd * DH, (odd + 1) * DH)
                                    mm = pe.matmul(bank[4 + 2 * (e // 4) + odd][:, (e % 4) * P:(e % 4 + 1) * P],
                                                   kT[rows, hh, b * P:(b + 1) * P], kbT[rows, hh, b * P:(b + 1) * P],
                                                   start=True, stop=True)
                        mm.then_inc(at_ready.sem, 1)

            @block.scalar
            def _(act):
                with act.Fori(0, NB // 2) as i:
                    for s in range(2):
                        it = i * 2 + s
                        H = toks(pb[s], HF)
                        act.wait_ge(*xT_ready.now(it, 1))
                        act.activation(xT[:, 0:2, :, :].rearrange("p b a t -> p (b a t)"), bank[0][:, :], ACT.Copy)\
                            .then_inc(xT01_copied.sem, 1)
                        act.wait_ge(*negmax_ready.now(it))
                        for b in range(BLK):
                            act.activation(E[:, b, :], bank[2][:, b * P:(b + 1) * P], ACT.Exp, bias=negmax[:, b:b + 1],
                                           scale=float(D) ** -0.5, accum_out=rs[:, b:b + 1]).then_inc(probs_ready.sem, 1)
                        act.wait_ge(*probsT_ready.now(it))
                        act.activation(PT[:, :, :].rearrange("p b t -> p (b t)"), bank[3][:, 0:T], ACT.Copy)\
                            .then_inc(probsT_copied.sem, 1)
                        act.wait_ge(*attn_ready.now(it))
                        act.wait_ge(*rinv_ready.now(it))
                        act.wait_ge(*packs_stored[s].before(i))
                        for b in range(BLK):
                            act.activation(H[:, b, :], bank[4 + b // 2][:, (b % 2) * D:(b % 2 + 1) * D], ACT.Copy,
                                           scale=rinv[:, b:b + 1]).then_inc(h_ready.sem, 1)
                        act.wait_ge(*veps_ready.now(it))
                        act.activation(lnv[:, :], veps[:, :], ACT.Ln).then_inc(lnv_ready.sem, 1)
                        act.wait_ge(*lnv_ready.now(it))
                        act.activation(rstd[:, :], lnv[:, :], ACT.Exp, scale=-0.5).then_inc(rstd_ready.sem, 1)
                        act.wait_ge(*xnT_ready.now(it, 1))
                        act.activation(chans(pb[s], XNT)[:, 0, :], bank[0][:, 0:T], ACT.Copy).then_inc(xnT0_copied.sem, 1)
                        act.wait_ge(*beta_ready.now(it))
                        act.activation(eb[:, :], bank[2][:, 0:NM], ACT.Exp, scale=-1.0).then_inc(eb_ready.sem, 1)
                        for j in range(3 * HALF):
                            act.wait_ge(*proj_ready.now(it, j + 1))
                            act.activation(Y[:, j, :], proj_bank[j][:, 0:T], ACT.Copy, scale=convw[:, j, CK - 1:CK])\
                                .then_inc(tap_done.sem, 1)
                        for j in range(3 * HALF):
                            dst = (chans(pa[s], QT), chans(pa[s], KT), VT)[j // 2]
                            act.wait_ge(*conv_step.now(it, 6 * (j // 2) + 5 + j % 2))
                            if j == 4:
                                act.wait_ge(*fir_step.before(it))
                            act.activation(dst[:, j % 2, :], Y[:, j, :], ACT.Silu).then_inc(silu_done.sem, 1)
                        act.wait_ge(*silu_done.now(it, 4))
                        for n in range(2):
                            act.activation(SQ[:, 2 * n:2 * n + 2, :].rearrange("p a t -> p (a t)"),
                                           field(pa[s], (QT, KT)[n]), ACT.Square).then_inc(sq_ready.sem, 1)
                        act.wait_ge(*rs_ready.now(it))
                        act.activation(LR[:, :, :, :], RS[:, :, :, :], ACT.Ln).then_inc(lr_ready.sem, 1)
                        act.wait_ge(*lr_ready.now(it))
                        act.activation(RR[:, :, :, :], LR[:, :, :, :], ACT.Exp, scale=-0.5).then_inc(rr_ready.sem, 1)
                        act.wait_ge(*ktok_ready.now(it))
                        act.activation(field(pa[s], KTOK)[:, 0:2 * D], bank[4][:, :], ACT.Copy)
                        act.activation(field(pa[s], KTOK)[:, 2 * D:], bank[5][:, 0:D], ACT.Copy).then_inc(ktok_copied.sem, 1)
                        act.wait_ge(*kbT_ready.now(it, 1))
                        act.activation(chans(pa[s], KBT)[:, 0, :], bank[2][:, 0:T], ACT.Copy).then_inc(kbT0_copied.sem, 1)
                        act.wait_ge(*fs_ready.now(it))
                        act.activation(field(pb[s], FSF)[:, 0:2 * D], bank[0][:, :], ACT.Copy)
                        act.activation(field(pb[s], FSF)[:, 2 * D:], bank[1][:, 0:D], ACT.Copy).then_inc(fs_copied.sem, 1)

            @block.vector
            def _(dve):
                with dve.Fori(0, NB // 2) as i:
                    for s in range(2):
                        it = i * 2 + s
                        H = toks(pb[s], HF)
                        dve.wait_ge(*xT_ready.now(it, 2))
                        dve.tensor_copy(xT[:, 2, :, :].rearrange("p a t -> p (a t)"), bank[1][:, 0:D]).then_inc(xT2_copied.sem, 1)
                        dve.wait_ge(*scores_ready.now(it))
                        dve.tensor_reduce(mx[:, :], bank[2][:, 0:T].rearrange("p (b t) -> p b t", b=BLK), AX.X, ALU.max)\
                            .then_inc(max_found.sem, 1)
                        dve.wait_ge(*max_found.now(it))
                        dve.tensor_scalar(negmax[:, :], mx[:, :], -float(D) ** -0.5, None, ALU.mult).then_inc(negmax_ready.sem, 1)
                        dve.wait_ge(*probs_ready.now(it))
                        dve.reciprocal(rinv[:, :], rs[:, :]).then_inc(rinv_ready.sem, 1)
                        for b in range(BLK):
                            dve.wait_ge(*h_ready.now(it, b + 1))
                            dve.bn_stats(st[:, b, :], H[:, b, :]).then_inc(stats_done.sem, 1)
                        dve.wait_ge(started, 1)
                        dve.wait_ge(*stats_done.now(it))
                        for b in range(BLK):
                            dve.bn_aggr(mv[:, b, :], st[:, b, :]).then_inc(mv_ready.sem, 1)
                        dve.wait_ge(*mv_ready.now(it))
                        dve.tensor_scalar(veps[:, :], mv[:, :, 1], 1e-5, None, ALU.add).then_inc(veps_ready.sem, 1)
                        dve.wait_ge(*rstd_ready.now(it))
                        for b in range(BLK):
                            dve.tensor_scalar(xn[:, b, :], H[:, b, :], mv[:, b, 0:1], rstd[:, b:b + 1],
                                              ALU.subtract, ALU.mult).then_inc(xn_ready.sem, 1)
                        dve.wait_ge(*xnT_ready.now(it, 2))
                        dve.tensor_copy(chans(pb[s], XNT)[:, 1, :], bank[1][:, 0:T]).then_inc(xnT1_copied.sem, 1)
                        dve.wait_ge(*eb_ready.now(it))
                        dve.tensor_scalar(b1[:, :], eb[:, :], 1.0, None, ALU.add).then_inc(beta_step.sem, 1)
                        dve.wait_ge(*beta_step.now(it, 1))
                        dve.reciprocal(beta[:, :], b1[:, :]).then_inc(beta_step.sem, 1)
                        for n in range(3):
                            for lag in range(1, CK):
                                for a in range(HALF):
                                    j = 2 * n + a
                                    if lag == 1:
                                        dve.wait_ge(*tap_done.now(it, j + 1))
                                    else:
                                        dve.wait_ge(*conv_step.now(it, 6 * n + 2 * (lag - 2) + a + 1))
                                    dve.scalar_tensor_tensor(out=Y[:, j, lag:T], in0=proj_bank[j][:, 0:T - lag],
                                                             scalar=convw[:, j, CK - 1 - lag:CK - lag], in1=Y[:, j, lag:T],
                                                             op0=ALU.mult, op1=ALU.add).then_inc(conv_step.sem, 1)
                        dve.wait_ge(*ssq_ready.now(it))
                        dve.tensor_scalar(RS[:, :, :, :].rearrange("p b n h -> p (b n h)"), bank[2][:, 0:2 * NM], 1e-6, None,
                                          ALU.add).then_inc(rs_ready.sem, 1)
                        dve.wait_ge(*rr_ready.now(it))
                        dve.wait_ge(*beta_step.now(it, 2))
                        vbs = pa[s][:, VBS:VBS + NM]
                        dve.tensor_tensor(vbs.rearrange("p (b h) -> p b h", b=BLK),
                                          beta[:, :].rearrange("p (b h) -> p b h", b=BLK), RR[:, :, 1, :], ALU.mult)\
                            .then_inc(vbs_ready.sem, 1)
                        dve.tensor_copy(pa[s][:, RQ:RQ + NM].rearrange("p (b h) -> p b h", b=BLK), RR[:, :, 0, :])
                        dve.wait_ge(*vbs_ready.now(it))
                        dve.tensor_tensor(kbs[:, :].rearrange("p (b h) -> p b h", b=BLK),
                                          vbs.rearrange("p (b h) -> p b h", b=BLK), RR[:, :, 1, :], ALU.mult)\
                            .then_inc(scales_ready.sem, 1)
                        dve.wait_ge(*vtok_ready.now(it))
                        dve.tensor_copy(field(pa[s], VTOK)[:, 0:2 * D], bank[6][:, :])
                        dve.tensor_copy(field(pa[s], VTOK)[:, 2 * D:], bank[7][:, 0:D]).then_inc(vtok_copied.sem, 1)
                        dve.wait_ge(*kbT_ready.now(it, 2))
                        dve.tensor_copy(chans(pa[s], KBT)[:, 1, :], bank[3][:, 0:T]).then_inc(kbT1_copied.sem, 1)
                        dve.wait_ge(*at_ready.now(it))
                        dve.wait_ge(*at_stored.before(it))
                        for n in range(4):
                            odd, far = n % 2, n // 2
                            m = 2 if far else 4
                            o = odd * NM // 2 + far * 4
                            ins = dve.tensor_tensor(AT[:, o:o + m, :], bank[4 + n][:, 0:m * P].rearrange("p (m t) -> p m t", m=m),
                                                    upper[:, P:].unsqueeze(1).broadcast_to([P, m, P]), ALU.mult)
                        ins.then_inc(at_copied.sem, 1)

            @block.gpsimd
            def _(pool):
                with pool.Fori(0, NB // 2) as i:
                    for s in range(2):
                        it = i * 2 + s
                        pool.wait_ge(*scales_ready.now(it))
                        pool.wait_ge(*ktok_copied.now(it))
                        pool.tensor_tensor(KB[:, :, :].rearrange("p b (h d) -> p (b h) d", h=NH),
                                           field(pa[s], KTOK).rearrange("p (m d) -> p m d", d=DH),
                                           kbs[:, :].unsqueeze(2).broadcast_to([P, NM, DH]), ALU.mult).then_inc(kb_ready.sem, 1)
                        pool.wait_ge(*silu_done.now(it, 6))
                        pool.tensor_tensor(fsT[:, :, :], VT[:, :, :], firw[:, :, FS - 1:FS].broadcast_to([P, HALF, T]), ALU.mult)\
                            .then_inc(fir_step.sem, 1)
                        for lag in range(1, FS):
                            pool.wait_ge(*fir_step.now(it, 2 * lag - 1))
                            pool.tensor_tensor(fst[:, :, :], VT[:, :, :],
                                               firw[:, :, FS - 1 - lag:FS - lag].broadcast_to([P, HALF, T]), ALU.mult)\
                                .then_inc(fir_step.sem, 1)
                            pool.wait_ge(*fir_step.now(it, 2 * lag))
                            pool.tensor_tensor(fsT[:, :, lag:T], fsT[:, :, lag:T], fst[:, :, 0:T - lag], ALU.add)\
                                .then_inc(fir_step.sem, 1)
                        pool.wait_ge(*vtok_copied.now(it))
                        for b in range(BLK):
                            keep = pool.tensor_copy(v_all[:, :, it + b * NB], toks(pa[s], VTOK)[:, b, :])
                        keep.then_inc(v_kept.sem, 1)


def second_phase(nc, w, shared):
    NB, NSYS, dram, bank, v_all, expanded = (shared[k] for k in ("NB", "NSYS", "dram", "bank", "v_all", "expanded"))
    CG = 8
    SG = 6 if NSYS % 6 == 0 else NSYS
    with ExitStack() as c:
        def sb(name, shape):
            return c.enter_context(nc.sbuf_tensor(name, shape, F32))

        signals = []

        def signal(name, per=1, primed=1):
            signals.append(Signal(c.enter_context(nc.semaphore(name)), per, primed))
            return signals[-1]

        toep = [sb(f"toep{s}", [P, CG, TW]) for s in range(2)]
        X = sb("X", [P, SG, SC, SC])
        prod = sb("prod", [P, SG * (SC // 2) * (SC // 2 - 1)])
        toep_loaded = [signal(f"toep_loaded{s}", 16) for s in range(2)]
        fl_ready = signal("fl_ready", 2, primed=2)
        fl_copied = signal("fl_copied", 2, primed=2)
        sys_loaded = c.enter_context(nc.semaphore("sys_loaded"))
        sys_stored = c.enter_context(nc.semaphore("sys_stored"))
        solve_step = c.enter_context(nc.semaphore("solve_step"))
        prime(nc, signals)
        systems = dram["systems"].rearrange("(p s) j i -> p s j i", s=NSYS)
        steps = 1 + 2 * (SC - 2)

        with nc.Block() as block:
            @block.sync
            def _(sp):
                sp.wait_ge(expanded, 16 * HALF)
                with sp.Fori(0, D // CG // 2) as i:
                    for s in range(2):
                        it = i * 2 + s
                        sp.wait_ge(*fl_ready.before(it, 2))
                        sp.dma_start(toep[s][:, :, :], dram["toeplitz"][:, bass.ds(it * CG, CG), :]).then_inc(toep_loaded[s].sem, 16)

            @block.tensor
            def _(pe):
                with pe.Fori(0, D // CG // 2) as i:
                    for s in range(2):
                        it = i * 2 + s
                        pe.wait_ge(*toep_loaded[s].now(i))
                        pe.wait_ge(*fl_copied.before(it, 2))
                        for ch in range(CG):
                            o = (ch % 4) * BLK * NB
                            acc = bank[2 * s + ch // 4]
                            pe.matmul(acc[:, o:o + BLK * NB], toep[s][:, ch, 0:P], v_all[:, it * CG + ch, :],
                                      start=True, stop=False, skip_group_check=True)
                            mm = pe.matmul(acc[0:TW - P, o + NB:o + BLK * NB], toep[s][:, ch, P:], v_all[:, it * CG + ch, 0:(BLK - 1) * NB],
                                           start=False, stop=True, skip_group_check=True)
                            if ch % 4 == 3:
                                mm.then_inc(fl_ready.sem, 1)

            @block.scalar
            def _(act):
                with act.Fori(0, D // CG // 2) as i:
                    for s in range(2):
                        it = i * 2 + s
                        for half in range(2):
                            act.wait_ge(*fl_ready.now(it, half + 1))
                            act.activation(v_all[:, bass.ds(it * CG + half * 4, 4), :].rearrange("p c n -> p (c n)"),
                                           bank[2 * s + half][:, 0:4 * BLK * NB], ACT.Copy).then_inc(fl_copied.sem, 1)

            @block.gpsimd
            def _(pool):
                for g in range(NSYS // SG):
                    pool.wait_ge(solve_step, steps * g)
                    if g:
                        pool.wait_ge(sys_stored, 16 * g)
                    pool.dma_start(X[:, :, :, :], systems[:, g * SG:(g + 1) * SG]).then_inc(sys_loaded, 16)
                    pool.wait_ge(solve_step, steps * (g + 1))
                    pool.dma_start(systems[:, g * SG:(g + 1) * SG], X[:, :, :, :]).then_inc(sys_stored, 16)
                pool.wait_ge(sys_stored, 16 * (NSYS // SG))

            @block.vector
            def _(dve):
                for g in range(NSYS // SG):
                    done = steps * g + 1
                    dve.wait_ge(sys_loaded, 16 * (g + 1))
                    dve.memset(X[:, :, :, :].rearrange("p s j i -> p s (j i)")[:, :, ::SC + 1], 1.0).then_inc(solve_step, 1)
                    dve.wait_ge(solve_step, done)
                    for j in range(1, SC - 1):
                        n = SC - 1 - j
                        pr = prod[:, 0:SG * j * n].rearrange("p (s j n) -> p s j n", s=SG, j=j)
                        dve.tensor_tensor(pr, X[:, :, 0:j, j:j + 1].broadcast_to([P, SG, j, n]),
                                          X[:, :, j:j + 1, j + 1:].broadcast_to([P, SG, j, n]), ALU.mult).then_inc(solve_step, 1)
                        done += 1
                        dve.wait_ge(solve_step, done)
                        dve.tensor_tensor(X[:, :, 0:j, j + 1:], X[:, :, 0:j, j + 1:], pr, ALU.add).then_inc(solve_step, 1)
                        done += 1
                        dve.wait_ge(solve_step, done)


def third_phase(nc, w, out, shared):
    NB, dram, bank, v_all, ident, upper = (shared[k] for k in ("NB", "dram", "bank", "v_all", "ident", "upper"))
    with ExitStack() as c:
        def sb(name, shape):
            return c.enter_context(nc.sbuf_tensor(name, shape, F32))

        signals = []

        def signal(name, per=1, primed=1):
            signals.append(Signal(c.enter_context(nc.semaphore(name)), per, primed))
            return signals[-1]

        loaded = c.enter_context(nc.semaphore("p3_weights"))
        setup = c.enter_context(nc.semaphore("p3_setup"))
        setup_act = c.enter_context(nc.semaphore("p3_setup_act"))
        MC = MLP // P
        w1g = sb("w1g", [P, HALF, MLP])
        w1s = sb("w1s", [GATE_S, MLP])
        b1g = sb("b1g", [P, MC])
        w2g = sb("w2g", [P, MC, 4 * NH])
        b2g = sb("b2g", [P, 4 * NH])
        wo = sb("wo", [P, HALF, D])
        onw = sb("onw", [P, 1])
        router = sb("router", [P, HALF, NE])
        anchors = sb("anchors", [P, NE, ND])
        before_e = sb("before_e", [P, NE, NE])
        rclip = sb("rclip", [P, 1])
        w1e = sb("w1e", [P, HALF, NE, DE])
        w2e = sb("w2e", [P, NE, D])
        temp = sb("temp", [P, 4, NH])
        itemp = sb("itemp", [P, NH])
        pa = [sb(f"qa{s}", [P, AW]) for s in range(2)]
        pb = sb("qb", [P, BW])
        ATM = sb("ATM", [P, NM, 2 * P])
        UF = sb("UF", [P, NM, P])
        TL = sb("TL", [P, NM, DH])
        P1 = sb("P1", [P, NM, SC])
        P1B = sb("P1B", [P, NM, DH])
        VB = sb("VB", [P, NM, DH])
        R = sb("R", [P, NH, DH])
        W = sb("W", [P, NH, DH])
        S = sb("S", [P, NH // 2, DH])
        DL = sb("DL", [P, NM, DH])
        ta = sb("ta", [P, BLK * D])
        tb = sb("tb", [P, BLK * D])
        NT = sb("NT", [P, HALF, T])
        HE = [P1B[:, n * 6:(n + 1) * 6, :].rearrange("p m d -> p (m d)") for n in range(2)]
        SGT = sb("SGT", [GATE_S, T])
        ST = sb("ST", [P, 4, NM, 6])
        SG = sb("SG", [P, BLK, 4, 2, NH])
        st1, st2, st3, st4 = (sb(f"st{n}", [P, 4, NM]) for n in range(4))
        L = sb("L", [P, NM, 4])
        WT = sb("WT", [P, NM, 4])
        m12, s12, r12 = (sb(f"m{n}", [P, NM]) for n in range(3))
        bst = sb("bst", [P, BLK, 6])
        bmv = sb("bmv", [P, BLK, 2])
        bv, bl, br = (sb(f"b{n}", [P, BLK]) for n in range(3))
        qr, lg, rank, ex, we = (sb(f"e{n}", [P, BLK, NE]) for n in range(5))
        cmp, eqs = (sb(f"c{n}", [P, BLK, NE, NE]) for n in range(2))
        me, se, re = (sb(f"g{n}", [P, BLK]) for n in range(3))

        def field(buf, at):
            return buf[:, at:at + HALF * T]

        def chans(buf, at):
            return field(buf, at).rearrange("p (a t) -> p a t", a=HALF)

        def toks(buf, at):
            return field(buf, at).rearrange("p (b c) -> p b c", b=BLK)

        def heads(buf, at):
            return field(buf, at).rearrange("p (m d) -> p m d", d=DH)

        H = toks(pb, HF)
        xnT = chans(pb, XNT)

        def gated(m):
            return ATM[:, BLK * m:BLK * (m + 1), P:]

        pa_loaded = [signal(f"pa_loaded{s}", 16) for s in range(2)]
        pb_loaded = signal("pb_loaded", 16)
        uf_loaded = signal("uf_loaded", 16 * NQ)
        out_stored = signal("out_stored", 16)
        qk_ready = signal("qk_ready", 6)
        masked = signal("masked", 6)
        tdiag_ready = signal("tdiag_ready")
        p1_ready, p1_copied = signal("p1_ready"), signal("p1_copied")
        u12_ready, u12_copied = signal("u12_ready"), signal("u12_copied")
        p1b_ready, p1b_copied = signal("p1b_ready"), signal("p1b_copied")
        u12b_ready, u12b_copied = signal("u12b_ready"), signal("u12b_copied")
        vb_ready = signal("vb_ready")
        r_ready, r_copied = signal("r_ready", 2), signal("r_copied", 2)
        w_ready, w_copied = signal("w_ready", 3), signal("w_copied", 3)
        s_ready, s_copied = signal("s_ready", 2), signal("s_copied", 2)
        o_ready, d_ready = signal("o_ready", 3), signal("d_ready", 3)
        branch_stats = signal("branch_stats")
        stat_step = signal("stat_step", 4)
        vmax_ready = signal("vmax_ready")
        lnv_ready, std_ready = signal("q_lnv_ready"), signal("std_ready")
        sgT_ready, sgT_copied = signal("sgT_ready"), signal("sgT_copied")
        mlp_ready, g1_ready = signal("mlp_ready", 4), signal("g1_ready", 4)
        logits_ready = signal("logits_ready")
        gate_step = signal("gate_step", 3)
        lg_ready, wexp_ready = signal("lg_ready"), signal("wexp_ready")
        wt_step = signal("wt_step", 3)
        fsw_ready, vw_ready = signal("fsw_ready"), signal("vw_ready")
        mix_step = signal("mix_step", 5)
        sq_ready, ss_ready, ms_ready = signal("q_sq_ready"), signal("ss_ready"), signal("ms_ready")
        lnr_ready, rr_ready = signal("lnr_ready"), signal("q_rr_ready")
        on_ready = signal("on_ready")
        onT_ready, onT0_copied, onT1_copied = signal("onT_ready", 2), signal("onT0_copied"), signal("onT1_copied")
        wo_ready, h2_ready = signal("wo_ready"), signal("h2_ready")
        bst_ready, bmv_ready, veps_ready = signal("bst_ready"), signal("bmv_ready"), signal("q_veps_ready")
        lny_ready, rstd_ready = signal("lny_ready"), signal("q_rstd_ready")
        y_ready = signal("y_ready", BLK)
        yT_ready, yT0_copied, yT1_copied = signal("yT_ready", 2), signal("yT0_copied"), signal("yT1_copied")
        z_ready, q_ready = signal("z_ready"), signal("q_ready", primed=2)
        route_step = signal("route_step", 9)
        lr_ready, er_ready = signal("q_lr_ready"), signal("er_ready")
        we_step = signal("we_step", 4)
        hid_ready, he_ready = signal("hid_ready", NE), signal("he_ready", NE)
        eo_ready = signal("eo_ready", NE)
        acc_done = signal("acc_done", NE * BLK)
        prime(nc, signals)

        with nc.Block() as block:
            @block.sync
            def _(sp):
                def load(dst, src):
                    sp.dma_start(dst, src).then_inc(loaded, 16)
                load(w1g[:, :, :], w["mlp_w1"][0:D].rearrange("(a p) n -> p a n", a=HALF))
                load(w1s[:, :], w["mlp_w1"][D:])
                load(w2g[:, :, :], w["mlp_w2"].rearrange("(m p) n -> p m n", m=MC))
                load(wo[:, :, :], w["Wo"].rearrange("(a p) n -> p a n", a=HALF))
                for e in range(NE):
                    load(w1e[:, :, e, :], w["ffn_w1"][e].rearrange("(a p) n -> p a n", a=HALF))
                load(w2e[:, :, :], w["ffn_w2"].rearrange("e p n -> p e n"))
                load(b2g[:, :], w["mlp_b2"].partition_broadcast(P))
                load(anchors[:, :, :].rearrange("p e d -> p (e d)"), w["ffn_anchors"].rearrange("e d -> (e d)").partition_broadcast(P))
                load(rclip[:, :], w["ffn_routing_temp"].partition_broadcast(P))
                load(itemp[:, :], w["gate_log_temp"].partition_broadcast(P))
                for half in range(2):
                    load(onw[half * DH:(half + 1) * DH, :], w["o_norm_w"].unsqueeze(1))
                with nc.allow_non_contiguous_dma(reason="a few columns, once"):
                    load(b1g[:, :], w["mlp_b1"].rearrange("(m p) -> p m", m=MC))
                    for a in range(HALF):
                        load(router[:, a, :], w["ffn_proj_w"][:, a * P:(a + 1) * P].rearrange("e p -> p e"))
                sp.wait_ge(loaded, 16 * 20)

            @block.scalar
            def _(act):
                act.wait_ge(loaded, 16 * 20)
                act.activation(s12[:, 0:NH], itemp[:, :], ACT.Abs).then_inc(setup_act, 1)
                act.wait_ge(setup_act, 1)
                act.activation(r12[:, 0:NH], s12[:, 0:NH], ACT.Exp, scale=-1.0).then_inc(setup_act, 1)
                act.wait_ge(setup, 1)
                act.activation(r12[:, NH:2 * NH], m12[:, 0:NH], ACT.Ln).then_inc(setup_act, 1)

            @block.vector
            def _(dve):
                dve.wait_ge(setup_act, 2)
                dve.tensor_scalar(m12[:, 0:NH], r12[:, 0:NH], 1.0, None, ALU.add).then_inc(setup, 1)
                dve.tensor_scalar(m12[:, NH:2 * NH], itemp[:, :], 0.0, 1e-4, ALU.max, ALU.add).then_inc(setup, 1)
                dve.wait_ge(setup_act, 3)
                dve.wait_ge(setup, 2)
                dve.tensor_tensor(s12[:, 0:NH], m12[:, NH:2 * NH], r12[:, NH:2 * NH], ALU.add).then_inc(setup, 1)
                dve.wait_ge(setup, 3)
                dve.reciprocal(itemp[:, :], s12[:, 0:NH]).then_inc(setup, 1)
                dve.tensor_scalar(bv[:, 0:1], rclip[:, :], 0.1, None, ALU.max).then_inc(setup, 1)
                dve.wait_ge(setup, 5)
                dve.reciprocal(rclip[:, :], bv[:, 0:1]).then_inc(setup, 1)
                dve.memset(TL[:, :, :], 0.0).then_inc(setup, 1)
                dve.memset(UF[:, :, :], 0.0).then_inc(setup, 1)
                dve.memset(before_e[:, :, :], 0.0).then_inc(setup, 1)
                dve.wait_ge(setup, 9)
                for e in range(1, NE):
                    dve.memset(before_e[:, e, 0:e], 1.0).then_inc(setup, 1)
                dve.tensor_scalar(wo[:, :, :].rearrange("p a n -> p (a n)"), wo[:, :, :].rearrange("p a n -> p (a n)"),
                                  onw[:, 0:1], None, ALU.mult).then_inc(setup, 1)
                dve.wait_ge(setup, 15)

        with nc.Block() as block:
            @block.sync
            def _(sp):
                sysv = dram["systems"].rearrange("(n m q) j i -> n q j m i", m=NM, q=NQ)

                def load_a(it, s):
                    sp.wait_ge(*on_ready.before(it, 1) if isinstance(it, int) and it < 2 else on_ready.now(it - 2))
                    sp.dma_start(pa[s][:, :], dram["packa"][it]).then_inc(pa_loaded[s].sem, 16)

                def load_b(it):
                    sp.wait_ge(*out_stored.before(it))
                    sp.dma_start(pb[:, :], dram["packb"][it]).then_inc(pb_loaded.sem, 16)

                def load_u(it):
                    sp.wait_ge(*o_ready.before(it))
                    for q in range(NQ):
                        sp.dma_start(UF[q * SC:(q + 1) * SC, :, q * SC:(q + 1) * SC], sysv[it, q]).then_inc(uf_loaded.sem, 16)

                def store(it):
                    sp.wait_ge(*acc_done.now(it))
                    sp.dma_start(out[it].rearrange("(b p) n -> p b n", b=BLK), H).then_inc(out_stored.sem, 16)

                load_a(0, 0)
                load_u(0)
                load_b(0)
                load_a(1, 1)
                load_u(1)
                store(0)
                load_b(1)
                with sp.Fori(1, NB // 2) as i:
                    for s in range(2):
                        it = i * 2 + s
                        load_a(it, s)
                        load_u(it)
                        store(it - 1)
                        load_b(it)
                store(NB - 1)
                sp.wait_ge(*out_stored.before(NB))

            @block.tensor
            def _(pe):
                with pe.Fori(0, NB // 2) as i:
                    for s in range(2):
                        it = i * 2 + s
                        qT, kT, kbT = chans(pa[s], QT), chans(pa[s], KT), chans(pa[s], KBT)
                        qkb = pa[s][:, QT:QT + 2 * HALF * T].rearrange("p (f a t) -> p f a t", f=2, a=HALF)
                        ktok = toks(pa[s], KTOK)
                        pe.wait_ge(*pa_loaded[s].now(i))
                        pe.wait_ge(*q_ready.before(it))
                        pe.wait_ge(*acc_done.before(it))
                        for e2 in range(NM // 4):
                            for odd in range(2):
                                rows = slice(odd * DH, (odd + 1) * DH)
                                for e in (2 * e2, 2 * e2 + 1):
                                    b, hh = e // 2, e % 2
                                    mm = pe.matmul(bank[2 * e2 + odd][:, (e % 2) * 2 * P:(e % 2 + 1) * 2 * P],
                                                   kT[rows, hh, b * P:(b + 1) * P], qkb[rows, :, hh, b * P:(b + 1) * P],
                                                   start=True, stop=True)
                                mm.then_inc(qk_ready.sem, 1)
                        pe.wait_ge(loaded, 1)
                        pe.wait_ge(*tdiag_ready.now(it))
                        for m in range(NM):
                            for f in (0, 2 * SC):
                                mm = pe.matmul(bank[6 + f // DH][f + SC:f + 2 * SC, m * SC:(m + 1) * SC],
                                               ATM[f:f + SC, m, P + f + SC:P + f + 2 * SC], TL[f:f + SC, m, 0:SC],
                                               start=True, stop=True, skip_group_check=True)
                        mm.then_inc(p1_ready.sem, 1)
                        pe.wait_ge(loaded, 1)
                        pe.wait_ge(*p1_copied.now(it))
                        for m in range(NM):
                            for f in (0, 2 * SC):
                                u22 = UF[f + SC:f + 2 * SC, m, f + SC:f + 2 * SC]
                                mm = pe.matmul(bank[6 + f // DH][f:f + SC, m * SC:(m + 1) * SC],
                                               P1[f + SC:f + 2 * SC, m, :], u22, start=True, stop=True, skip_group_check=True)
                                if f == 0:
                                    mm = pe.matmul(bank[6][SC:2 * SC, m * SC:(m + 1) * SC], u22, P1[SC:2 * SC, m, :],
                                                   start=True, stop=True, skip_group_check=True)
                        mm.then_inc(u12_ready.sem, 1)
                        pe.wait_ge(loaded, 1)
                        pe.wait_ge(*u12_copied.now(it))
                        for m in range(NM):
                            mm = pe.matmul(bank[6 + m // 6][DH:P, (m % 6) * DH:(m % 6 + 1) * DH],
                                           ATM[0:DH, m, P + DH:2 * P], TL[0:DH, m, :], start=True, stop=True, skip_group_check=True)
                        mm.then_inc(p1b_ready.sem, 1)
                        pe.wait_ge(loaded, 1)
                        pe.wait_ge(*p1b_copied.now(it))
                        for m in range(NM):
                            mm = pe.matmul(bank[6 + m // 6][0:DH, (m % 6) * DH:(m % 6 + 1) * DH],
                                           P1B[DH:P, m, :], UF[DH:P, m, DH:P], start=True, stop=True, skip_group_check=True)
                        mm.then_inc(u12b_ready.sem, 1)
                        pe.wait_ge(*u12b_copied.now(it))
                        pe.wait_ge(*vb_ready.now(it))
                        for b in range(BLK):
                            cols = slice(b * P, (b + 1) * P)
                            if b:
                                pe.wait_ge(*s_copied.now(it, b))
                                for h in range(NH):
                                    rows = slice((h % 2) * DH, (h % 2 + 1) * DH)
                                    mm = pe.matmul(bank[h % 2][:, (h // 2) * DH:(h // 2 + 1) * DH],
                                                   kbT[rows, h // 2, cols], S[rows, h // 2, :], start=True, stop=True)
                                mm.then_inc(r_ready.sem, 1)
                                pe.wait_ge(*d_ready.now(it, b))
                                for h in range(NH):
                                    rows = slice((h % 2) * DH, (h % 2 + 1) * DH)
                                    pe.matmul(bank[3 + h % 2][:, (h // 2) * DH:(h // 2 + 1) * DH],
                                              qT[rows, h // 2, cols], S[rows, h // 2, :],
                                              start=(h < 2), stop=False, skip_group_check=True)
                                pe.wait_ge(*r_copied.now(it, b))
                            for h in range(NH):
                                mm = pe.matmul(bank[2][:, h * DH:(h + 1) * DH], UF[:, even_heads_first(b, h), :],
                                               R[:, h, :] if b else VB[:, h, :], start=True, stop=True)
                            mm.then_inc(w_ready.sem, 1)
                            pe.wait_ge(*w_copied.now(it, b + 1))
                            if b < BLK - 1:
                                for h in range(NH):
                                    rows = slice((h % 2) * DH, (h % 2 + 1) * DH)
                                    mm = pe.matmul(bank[5][rows, (h // 2) * DH:(h // 2 + 1) * DH],
                                                   ktok[:, b, h * DH:(h + 1) * DH], W[:, h, :], start=True, stop=True)
                                mm.then_inc(s_ready.sem, 1)
                            for h in range(NH):
                                mm = pe.matmul(bank[3 + h % 2][:, (h // 2) * DH:(h // 2 + 1) * DH],
                                               ATM[:, even_heads_first(b, h), 0:P], W[:, h, :],
                                               start=(b == 0 and h < 2), stop=True, skip_group_check=True)
                            mm.then_inc(o_ready.sem, 1)
                        pe.wait_ge(*std_ready.now(it))
                        for b in range(BLK):
                            mm = pe.transpose(bank[6][0:GATE_S, b * P:(b + 1) * P],
                                              SG[:, b, :, :, :].rearrange("p r m h -> p (r m h)"), ident[:, :])
                        mm.then_inc(sgT_ready.sem, 1)
                        pe.wait_ge(*pb_loaded.now(it))
                        pe.wait_ge(*sgT_copied.now(it))
                        for m in range(MC):
                            for a in range(HALF):
                                pe.matmul(bank[m][:, 0:T], w1g[:, a, m * P:(m + 1) * P], xnT[:, a, :], start=(a == 0), stop=False)
                            pe.matmul(bank[m][:, 0:T], w1s[:, m * P:(m + 1) * P], SGT[:, :], start=False, stop=True)\
                                .then_inc(mlp_ready.sem, 1)
                        pe.wait_ge(*g1_ready.now(it))
                        for b in range(BLK):
                            for m in range(MC):
                                mm = pe.matmul(bank[4][:, b * 4 * NH:(b + 1) * 4 * NH], gated(m)[:, b, :], w2g[:, m, :],
                                               start=(m == 0), stop=(m == MC - 1))
                        mm.then_inc(logits_ready.sem, 1)
                        pe.wait_ge(*on_ready.now(it))
                        for a in range(HALF):
                            for b in range(BLK):
                                m = b * NH + a * 2
                                mm = pe.transpose(bank[a][:, b * P:(b + 1) * P],
                                                  DL[:, m:m + 2, :].rearrange("p m d -> p (m d)"), ident[:, :])
                            mm.then_inc(onT_ready.sem, 1)
                        pe.wait_ge(*onT0_copied.now(it))
                        pe.wait_ge(*onT1_copied.now(it))
                        for b in range(BLK):
                            for a in range(HALF):
                                mm = pe.matmul(bank[2 + b // 2][:, (b % 2) * D:(b % 2 + 1) * D], NT[:, a, b * P:(b + 1) * P],
                                               wo[:, a, :], start=(a == 0), stop=(a == HALF - 1))
                        mm.then_inc(wo_ready.sem, 1)
                        pe.wait_ge(*y_ready.now(it))
                        for a in range(HALF):
                            for b in range(BLK):
                                mm = pe.transpose(bank[a][:, b * P:(b + 1) * P],
                                                  tb[:, b * D + a * P:b * D + (a + 1) * P], ident[:, :])
                            mm.then_inc(yT_ready.sem, 1)
                        pe.wait_ge(*yT0_copied.now(it))
                        pe.wait_ge(*yT1_copied.now(it))
                        for b in range(BLK):
                            for a in range(HALF):
                                mm = pe.matmul(bank[4][:, b * NE:(b + 1) * NE], NT[:, a, b * P:(b + 1) * P], router[:, a, :],
                                               start=(a == 0), stop=(a == HALF - 1))
                        mm.then_inc(z_ready.sem, 1)
                        for e in range(NE + 1):
                            if e < NE:
                                if e >= 2:
                                    pe.wait_ge(*he_ready.now(it, e - 1))
                                for a in range(HALF):
                                    mm = pe.matmul(bank[e % 2][:, 0:T], w1e[:, a, e, :], NT[:, a, :],
                                                   start=(a == 0), stop=(a == HALF - 1))
                                mm.then_inc(hid_ready.sem, 1)
                            if e:
                                f = e - 1
                                pe.wait_ge(*he_ready.now(it, f + 1))
                                if f >= 2:
                                    pe.wait_ge(*acc_done.now(it, BLK * (f - 1)))
                                for b in range(BLK):
                                    mm = pe.matmul(bank[(2, 5)[f % 2] + b // 2][:, (b % 2) * D:(b % 2 + 1) * D],
                                                   HE[f % 2][:, b * P:(b + 1) * P], w2e[:, f, :], start=True, stop=True)
                                mm.then_inc(eo_ready.sem, 1)

            @block.scalar
            def _(act):
                with act.Fori(0, NB // 2) as i:
                    for s in range(2):
                        it = i * 2 + s

                        def copy(dst, src):
                            return act.activation(dst, src, ACT.Copy)

                        def blocks(n, rows, width):
                            return bank[n][rows, 0:384].rearrange("p (m c) -> p m c", c=width)

                        act.wait_ge(*p1_ready.now(it))
                        copy(P1[SC:2 * SC, :, :], blocks(6, slice(SC, 2 * SC), SC))
                        copy(P1[3 * SC:P, :, :], blocks(7, slice(3 * SC, P), SC)).then_inc(p1_copied.sem, 1)
                        act.wait_ge(*u12_ready.now(it))
                        copy(UF[0:SC, :, SC:2 * SC], blocks(6, slice(0, SC), SC))
                        copy(TL[SC:2 * SC, :, 0:SC], blocks(6, slice(SC, 2 * SC), SC))
                        copy(UF[2 * SC:3 * SC, :, 3 * SC:P], blocks(7, slice(2 * SC, 3 * SC), SC)).then_inc(u12_copied.sem, 1)
                        act.wait_ge(*p1b_ready.now(it))
                        copy(P1B[DH:P, 0:6, :], blocks(6, slice(DH, P), DH))
                        copy(P1B[DH:P, 6:NM, :], blocks(7, slice(DH, P), DH)).then_inc(p1b_copied.sem, 1)
                        act.wait_ge(*u12b_ready.now(it))
                        copy(UF[0:DH, 0:6, DH:P], blocks(6, slice(0, DH), DH))
                        copy(UF[0:DH, 6:NM, DH:P], blocks(7, slice(0, DH), DH)).then_inc(u12b_copied.sem, 1)
                        for b in range(BLK):
                            act.wait_ge(*w_ready.now(it, b + 1))
                            copy(W[:, :, :].rearrange("p h d -> p (h d)"), bank[2][:, 0:D]).then_inc(w_copied.sem, 1)
                        act.wait_ge(*vmax_ready.now(it))
                        act.activation(st2[:, :, :], st1[:, :, :], ACT.Ln).then_inc(lnv_ready.sem, 1)
                        act.wait_ge(*lnv_ready.now(it))
                        for r in range(4):
                            std = act.activation(SG[:, :, r, 1, :], st2[:, r, :].rearrange("p (b h) -> p b h", b=BLK), ACT.Exp, scale=0.5)
                        std.then_inc(std_ready.sem, 1)
                        act.wait_ge(*sgT_ready.now(it))
                        copy(SGT[:, :], bank[6][0:GATE_S, 0:T]).then_inc(sgT_copied.sem, 1)
                        for m in range(MC):
                            act.wait_ge(*mlp_ready.now(it, m + 1))
                            act.activation(gated(m), bank[m][:, 0:T].rearrange("p (b t) -> p b t", b=BLK), ACT.Gelu,
                                           bias=b1g[:, m:m + 1]).then_inc(g1_ready.sem, 1)
                        act.wait_ge(*lg_ready.now(it))
                        act.activation(WT[:, :, :], L[:, :, :], ACT.Exp).then_inc(wexp_ready.sem, 1)
                        act.wait_ge(*mix_step.now(it))
                        act.activation(ta[:, :], DL[:, :, :].rearrange("p m d -> p (m d)"), ACT.Square).then_inc(sq_ready.sem, 1)
                        act.wait_ge(*ms_ready.now(it))
                        act.activation(r12[:, :], m12[:, :], ACT.Ln).then_inc(lnr_ready.sem, 1)
                        act.wait_ge(*lnr_ready.now(it))
                        act.activation(s12[:, :], r12[:, :], ACT.Exp, scale=-0.5).then_inc(rr_ready.sem, 1)
                        act.wait_ge(*onT_ready.now(it, 1))
                        copy(NT[:, 0, :], bank[0][:, 0:T]).then_inc(onT0_copied.sem, 1)
                        act.wait_ge(*veps_ready.now(it))
                        act.activation(bl[:, :], bv[:, :], ACT.Ln).then_inc(lny_ready.sem, 1)
                        act.wait_ge(*lny_ready.now(it))
                        act.activation(br[:, :], bl[:, :], ACT.Exp, scale=-0.5).then_inc(rstd_ready.sem, 1)
                        act.wait_ge(*yT_ready.now(it, 1))
                        copy(NT[:, 0, :], bank[0][:, 0:T]).then_inc(yT0_copied.sem, 1)
                        act.wait_ge(*z_ready.now(it))
                        act.activation(qr[:, :, :].rearrange("p b e -> p (b e)"), bank[4][:, 0:BLK * NE], ACT.Tanh, scale=1.0 / 0.3)\
                            .then_inc(q_ready.sem, 1)
                        act.wait_ge(*lr_ready.now(it))
                        act.activation(ex[:, :, :], rank[:, :, :], ACT.Exp).then_inc(er_ready.sem, 1)
                        for e in range(NE):
                            act.wait_ge(*hid_ready.now(it, e + 1))
                            if e >= 2:
                                act.wait_ge(*eo_ready.now(it, e - 1))
                            act.activation(HE[e % 2], bank[e % 2][:, 0:T], ACT.Gelu_apprx_tanh).then_inc(he_ready.sem, 1)

            @block.vector
            def _(dve):
                with dve.Fori(0, NB // 2) as i:
                    for s in range(2):
                        it = i * 2 + s
                        fl = v_all[:, :, :].rearrange("p (h d) (b n) -> p n b h d", h=NH, b=BLK)[:, it]
                        rq = pa[s][:, RQ:RQ + NM].rearrange("p (b h) -> p b h", b=BLK)

                        def rows12(t):
                            return t[:, :].unsqueeze(2).broadcast_to([P, NM, DH])

                        for n in range(6):
                            e = (n % 2) * (NM // 2) + (n // 2) * 2
                            dve.wait_ge(*qk_ready.now(it, n + 1))
                            dve.tensor_tensor(ATM[:, e:e + 2, :], bank[n][:, :].rearrange("p (m c) -> p m c", m=2),
                                              upper[:, :].unsqueeze(1).broadcast_to([P, 2, 2 * P]), ALU.mult).then_inc(masked.sem, 1)
                        dve.wait_ge(*uf_loaded.now(it))
                        dve.wait_ge(*p1b_copied.before(it))
                        dve.transpose(TL[0:SC, :, 0:SC], UF[0:SC, :, 0:SC])
                        dve.transpose(TL[SC:2 * SC, :, SC:2 * SC], UF[SC:2 * SC, :, SC:2 * SC])
                        dve.transpose(TL[2 * SC:3 * SC, :, 0:SC], UF[2 * SC:3 * SC, :, 2 * SC:3 * SC]).then_inc(tdiag_ready.sem, 1)
                        dve.wait_ge(*pb_loaded.now(it))
                        for m in range(NM):
                            dve.bn_stats(ST[:, 0, m, :], heads(pb, FSF)[:, m, :])
                            dve.bn_stats(ST[:, 1, m, :], fl[:, m // NH, m % NH, :])
                            dve.bn_stats(ST[:, 3, m, :], heads(pa[s], VTOK)[:, m, :])
                        for b in range(BLK):
                            if b:
                                dve.wait_ge(*r_ready.now(it, b))
                                for odd in range(2):
                                    r = dve.tensor_tensor(R[:, odd::2, :], VB[:, b * NH + odd:(b + 1) * NH:2, :],
                                                          bank[odd][:, 0:2 * DH].rearrange("p (m d) -> p m d", m=2), ALU.subtract)
                                r.then_inc(r_copied.sem, 1)
                            if b < BLK - 1:
                                dve.wait_ge(*s_ready.now(it, b + 1))
                                new = bank[5][:, 0:2 * DH].rearrange("p (m d) -> p m d", m=2)
                                if b == 0:
                                    dve.tensor_copy(S[:, :, :], new).then_inc(s_copied.sem, 1)
                                else:
                                    dve.tensor_tensor(S[:, :, :], S[:, :, :], new, ALU.add).then_inc(s_copied.sem, 1)
                            dve.wait_ge(*o_ready.now(it, b + 1))
                            for odd in range(2):
                                d = dve.tensor_tensor(DL[:, b * NH + odd:(b + 1) * NH:2, :],
                                                      bank[3 + odd][:, 0:2 * DH].rearrange("p (m d) -> p m d", m=2),
                                                      rq[:, b, odd::2].unsqueeze(2).broadcast_to([P, 2, DH]), ALU.mult)
                            d.then_inc(d_ready.sem, 1)
                        dve.wait_ge(*d_ready.now(it))
                        for m in range(NM):
                            ins = dve.bn_stats(ST[:, 2, m, :], DL[:, m, :])
                        ins.then_inc(branch_stats.sem, 1)
                        dve.wait_ge(*branch_stats.now(it))
                        dve.tensor_tensor(st1[:, :, :], ST[:, :, :, 1], ST[:, :, :, 4], ALU.add)
                        dve.tensor_tensor(st2[:, :, :], ST[:, :, :, 1], ST[:, :, :, 4], ALU.subtract)
                        dve.tensor_tensor(st3[:, :, :], ST[:, :, :, 2], ST[:, :, :, 5], ALU.add).then_inc(stat_step.sem, 1)
                        dve.wait_ge(*stat_step.now(it, 1))
                        for r in range(4):
                            mean = dve.tensor_scalar(SG[:, :, r, 0, :], st1[:, r, :].rearrange("p (b h) -> p b h", b=BLK), 0.5, None, ALU.mult)
                        mean.then_inc(stat_step.sem, 1)
                        dve.tensor_tensor(st4[:, :, :], st2[:, :, :], st2[:, :, :], ALU.mult)
                        dve.tensor_scalar(st3[:, :, :], st3[:, :, :], 1.0 / DH, None, ALU.mult).then_inc(stat_step.sem, 1)
                        dve.wait_ge(*stat_step.now(it, 3))
                        dve.scalar_tensor_tensor(out=st2[:, :, :], in0=st4[:, :, :], scalar=0.25, in1=st3[:, :, :],
                                                 op0=ALU.mult, op1=ALU.add).then_inc(stat_step.sem, 1)
                        dve.wait_ge(*stat_step.now(it, 4))
                        dve.tensor_scalar(st1[:, :, :], st2[:, :, :], 1e-6, None, ALU.max).then_inc(vmax_ready.sem, 1)
                        dve.wait_ge(*logits_ready.now(it))
                        dve.tensor_tensor(L[:, :, :].rearrange("p (b h) r -> p b (h r)", b=BLK),
                                          bank[4][:, 0:BLK * 4 * NH].rearrange("p (b n) -> p b n", b=BLK),
                                          b2g[:, :].unsqueeze(1).broadcast_to([P, BLK, 4 * NH]), ALU.add).then_inc(gate_step.sem, 1)
                        dve.wait_ge(*gate_step.now(it, 1))
                        lv = L[:, :, :].rearrange("p (b h) r -> p b h r", b=BLK)
                        dve.tensor_tensor(lv, lv, itemp[:, :].unsqueeze(1).unsqueeze(3).broadcast_to([P, BLK, NH, 4]), ALU.mult)\
                            .then_inc(gate_step.sem, 1)
                        dve.wait_ge(*gate_step.now(it, 2))
                        dve.tensor_reduce(m12[:, :], L[:, :, :], AX.X, ALU.max).then_inc(gate_step.sem, 1)
                        dve.wait_ge(*gate_step.now(it, 3))
                        dve.tensor_tensor(L[:, :, :], L[:, :, :], m12[:, :].unsqueeze(2).broadcast_to([P, NM, 4]), ALU.subtract)\
                            .then_inc(lg_ready.sem, 1)
                        dve.wait_ge(*wexp_ready.now(it))
                        dve.tensor_reduce(s12[:, :], WT[:, :, :], AX.X, ALU.add).then_inc(wt_step.sem, 1)
                        dve.wait_ge(*wt_step.now(it, 1))
                        dve.reciprocal(r12[:, :], s12[:, :]).then_inc(wt_step.sem, 1)
                        dve.wait_ge(*wt_step.now(it, 2))
                        dve.tensor_tensor(WT[:, :, :], WT[:, :, :], r12[:, :].unsqueeze(2).broadcast_to([P, NM, 4]), ALU.mult)\
                            .then_inc(wt_step.sem, 1)
                        dve.wait_ge(*wt_step.now(it, 3))
                        ntv = NT[:, :, :].rearrange("p a t -> p (a t)").rearrange("p (m d) -> p m d", d=DH)
                        dve.tensor_tensor(DL[:, :, :], DL[:, :, :], WT[:, :, 2:3].broadcast_to([P, NM, DH]), ALU.mult).then_inc(mix_step.sem, 1)
                        for b in range(BLK):
                            ins = dve.tensor_tensor(ntv[:, b * NH:(b + 1) * NH, :], fl[:, b],
                                                    WT[:, b * NH:(b + 1) * NH, 1:2].broadcast_to([P, NH, DH]), ALU.mult)
                        ins.then_inc(mix_step.sem, 1)
                        dve.wait_ge(*mix_step.now(it, 2))
                        dve.tensor_tensor(DL[:, :, :], DL[:, :, :], ntv, ALU.add).then_inc(mix_step.sem, 1)
                        dve.wait_ge(*fsw_ready.now(it))
                        dve.wait_ge(*mix_step.now(it, 3))
                        dve.tensor_tensor(DL[:, :, :], DL[:, :, :], ta[:, :].rearrange("p (m d) -> p m d", d=DH), ALU.add)\
                            .then_inc(mix_step.sem, 1)
                        dve.wait_ge(*vw_ready.now(it))
                        dve.wait_ge(*mix_step.now(it, 4))
                        dve.tensor_tensor(DL[:, :, :], DL[:, :, :], tb[:, :].rearrange("p (m d) -> p m d", d=DH), ALU.add)\
                            .then_inc(mix_step.sem, 1)
                        dve.wait_ge(*sq_ready.now(it))
                        dve.tensor_reduce(s12[:, :], ta[:, :].rearrange("p (m d) -> p m d", d=DH), AX.X, ALU.add).then_inc(ss_ready.sem, 1)
                        dve.wait_ge(*ss_ready.now(it))
                        dve.tensor_scalar(m12[:, :], s12[:, :], 1.0 / DH, 1e-5, ALU.mult, ALU.add).then_inc(ms_ready.sem, 1)
                        dve.wait_ge(*rr_ready.now(it))
                        dve.tensor_tensor(DL[:, :, :], DL[:, :, :], rows12(s12), ALU.mult).then_inc(on_ready.sem, 1)
                        dve.wait_ge(*onT_ready.now(it, 2))
                        dve.tensor_copy(NT[:, 1, :], bank[1][:, 0:T]).then_inc(onT1_copied.sem, 1)
                        dve.wait_ge(*wo_ready.now(it))
                        hf = field(pb, HF)
                        dve.tensor_tensor(hf[:, 0:2 * D], hf[:, 0:2 * D], bank[2][:, :], ALU.add)
                        dve.tensor_tensor(hf[:, 2 * D:], hf[:, 2 * D:], bank[3][:, 0:D], ALU.add).then_inc(h2_ready.sem, 1)
                        dve.wait_ge(*h2_ready.now(it))
                        for b in range(BLK):
                            ins = dve.bn_stats(bst[:, b, :], H[:, b, :])
                        ins.then_inc(bst_ready.sem, 1)
                        dve.wait_ge(setup, 1)
                        dve.wait_ge(*bst_ready.now(it))
                        for b in range(BLK):
                            ins = dve.bn_aggr(bmv[:, b, :], bst[:, b, :])
                        ins.then_inc(bmv_ready.sem, 1)
                        dve.wait_ge(*bmv_ready.now(it))
                        dve.tensor_scalar(bv[:, :], bmv[:, :, 1], 1e-5, None, ALU.add).then_inc(veps_ready.sem, 1)
                        dve.wait_ge(*rstd_ready.now(it))
                        for b in range(BLK):
                            dve.tensor_scalar(tb[:, b * D:(b + 1) * D], H[:, b, :], bmv[:, b, 0:1], br[:, b:b + 1],
                                              ALU.subtract, ALU.mult).then_inc(y_ready.sem, 1)
                        dve.wait_ge(*yT_ready.now(it, 2))
                        dve.tensor_copy(NT[:, 1, :], bank[1][:, 0:T]).then_inc(yT1_copied.sem, 1)
                        dve.wait_ge(*q_ready.now(it))
                        dve.tensor_tensor(cmp[:, :, :, :], qr[:, :, :].unsqueeze(2).broadcast_to([P, BLK, NE, ND]),
                                          anchors[:, :, :].unsqueeze(1).broadcast_to([P, BLK, NE, ND]), ALU.mult).then_inc(route_step.sem, 1)
                        dve.wait_ge(*route_step.now(it, 1))
                        dve.tensor_reduce(lg[:, :, :], cmp[:, :, :, :], AX.X, ALU.add).then_inc(route_step.sem, 1)
                        dve.wait_ge(*route_step.now(it, 2))
                        dve.tensor_scalar(we[:, :, :], lg[:, :, :], -float(ND), 0.5, ALU.add, ALU.mult).then_inc(route_step.sem, 1)
                        dve.wait_ge(*route_step.now(it, 3))
                        dve.tensor_scalar(lg[:, :, :], we[:, :, :], rclip[:, 0:1], None, ALU.mult).then_inc(route_step.sem, 1)
                        dve.wait_ge(*route_step.now(it, 4))
                        other = lg[:, :, :].unsqueeze(2).broadcast_to([P, BLK, NE, NE])
                        own = lg[:, :, :].unsqueeze(3).broadcast_to([P, BLK, NE, NE])
                        dve.tensor_tensor(cmp[:, :, :, :], other, own, ALU.is_gt)
                        dve.tensor_tensor(eqs[:, :, :, :], other, own, ALU.is_equal)
                        dve.tensor_reduce(me[:, :], lg[:, :, :], AX.X, ALU.max).then_inc(route_step.sem, 1)
                        dve.wait_ge(*route_step.now(it, 5))
                        dve.tensor_tensor(eqs[:, :, :, :], eqs[:, :, :, :], before_e[:, :, :].unsqueeze(1).broadcast_to([P, BLK, NE, NE]), ALU.mult)\
                            .then_inc(route_step.sem, 1)
                        dve.tensor_tensor(rank[:, :, :], lg[:, :, :], me[:, :].unsqueeze(2).broadcast_to([P, BLK, NE]), ALU.subtract)\
                            .then_inc(lr_ready.sem, 1)
                        dve.wait_ge(*route_step.now(it, 6))
                        dve.tensor_tensor(cmp[:, :, :, :], cmp[:, :, :, :], eqs[:, :, :, :], ALU.add).then_inc(route_step.sem, 1)
                        dve.wait_ge(*route_step.now(it, 7))
                        dve.tensor_reduce(we[:, :, :], cmp[:, :, :, :], AX.X, ALU.add).then_inc(route_step.sem, 1)
                        dve.wait_ge(*route_step.now(it, 8))
                        dve.tensor_scalar(lg[:, :, :], we[:, :, :], 1.5, None, ALU.is_lt).then_inc(route_step.sem, 1)
                        dve.wait_ge(*er_ready.now(it))
                        dve.wait_ge(*route_step.now(it, 9))
                        dve.tensor_tensor(ex[:, :, :], ex[:, :, :], lg[:, :, :], ALU.mult).then_inc(we_step.sem, 1)
                        dve.wait_ge(*we_step.now(it, 1))
                        dve.tensor_reduce(se[:, :], ex[:, :, :], AX.X, ALU.add).then_inc(we_step.sem, 1)
                        dve.wait_ge(*we_step.now(it, 2))
                        dve.reciprocal(re[:, :], se[:, :]).then_inc(we_step.sem, 1)
                        dve.wait_ge(*we_step.now(it, 3))
                        dve.tensor_tensor(we[:, :, :], ex[:, :, :], re[:, :].unsqueeze(2).broadcast_to([P, BLK, NE]), ALU.mult)\
                            .then_inc(we_step.sem, 1)
                        dve.wait_ge(*we_step.now(it, 4))
                        for e in range(NE):
                            dve.wait_ge(*eo_ready.now(it, e + 1))
                            for b in range(BLK):
                                if e:
                                    dve.wait_ge(*acc_done.now(it, BLK * (e - 1) + b + 1))
                                dve.scalar_tensor_tensor(out=H[:, b, :], in0=bank[(2, 5)[e % 2] + b // 2][:, (b % 2) * D:(b % 2 + 1) * D],
                                                         scalar=we[:, b, e:e + 1], in1=H[:, b, :], op0=ALU.mult, op1=ALU.add)\
                                    .then_inc(acc_done.sem, 1)

            @block.gpsimd
            def _(pool):
                with pool.Fori(0, NB // 2) as i:
                    for s in range(2):
                        it = i * 2 + s
                        pool.wait_ge(*pa_loaded[s].now(i))
                        pool.wait_ge(*r_copied.before(it))
                        pool.tensor_tensor(VB[:, :, :], heads(pa[s], VTOK),
                                           pa[s][:, VBS:VBS + NM].unsqueeze(2).broadcast_to([P, NM, DH]), ALU.mult)\
                            .then_inc(vb_ready.sem, 1)
                        pool.wait_ge(*wt_step.now(it))
                        pool.tensor_tensor(ta[:, :].rearrange("p (m d) -> p m d", d=DH), heads(pb, FSF),
                                           WT[:, :, 0:1].broadcast_to([P, NM, DH]), ALU.mult).then_inc(fsw_ready.sem, 1)
                        pool.tensor_tensor(tb[:, :].rearrange("p (m d) -> p m d", d=DH), heads(pa[s], VTOK),
                                           WT[:, :, 3:4].broadcast_to([P, NM, DH]), ALU.mult).then_inc(vw_ready.sem, 1)


_ATTN = ["Wq", "Wk", "Wv", "Wb", "conv_q_w", "conv_k_w", "conv_v_w", "fir_short_w", "fir_long_w", "mlp_w1", "mlp_b1",
         "mlp_w2", "mlp_b2", "gate_log_temp", "o_norm_w", "Wo"]
_FFN = ["proj_w", "anchors", "routing_temp", "w1", "w2"]


def kernel(**inputs):
    import numpy as _np
    import concourse.bacc as _bacc
    from concourse import mybir as _mybir
    from concourse.bass_utils import run_bass_kernel_spmd as _run

    nc = _bacc.Bacc("TRN2", target_bir_lowering=False, num_devices=1)
    arrays = {}

    def give(name):
        a = _np.ascontiguousarray(inputs[name])
        a = a.reshape(1) if a.ndim == 0 else a
        arrays[f"in_{name}_dram"] = a
        return nc.dram_tensor(f"in_{name}_dram", a.shape, _mybir.dt.from_np(a.dtype), kind="ExternalInput").ap()

    x = give("x")
    w = {n: give(f"L0_attn_{n}") for n in _ATTN}
    w |= {f"ffn_{n}": give(f"L0_ffn_{n}") for n in _FFN}
    out = nc.dram_tensor("out_0_dram", (x.shape[0], T, D), F32, kind="ExternalOutput").ap()
    audio_tower(nc, x, w, out)
    r = _run(nc, [arrays], core_ids=[0])
    return r.results[0]["out_0_dram"]
```

```python
from contextlib import ExitStack

import concourse.bass as bass
from concourse import mybir

F32 = mybir.dt.float32
ALU = mybir.AluOpType
ACT = mybir.ActivationFunctionType
AX = mybir.AxisListType

P = 128
D = 256
HALF = D // P
SEG, STEP = 256, 2
BLK = 3
T = BLK * P
NH, DH = 4, 64
NM = BLK * NH
CK, FS, FL = 4, 3, 63
TW = P + FL - 1
GATE_S = 8 * NH
MLP = 2 * D
NE, DE, ND = 6, 128, 6
SC = 32
NQ = P // SC

QT, KBT, KT, KTOK, VTOK = (n * HALF * T for n in range(5))
RQ = 5 * HALF * T
VBS = RQ + NM
AW = VBS + NM
HF, XNT, FSF = (n * HALF * T for n in range(3))
BW = 3 * HALF * T


class Signal:

    def __init__(self, sem, per, primed=1):
        self.sem, self.per, self.primed = sem, per, primed

    def now(self, it, k=None):
        return self.sem, (it + self.primed) * self.per + (self.per if k is None else k)

    def before(self, it, back=1):
        return self.sem, (it + (self.primed - back + 1)) * self.per


def even_heads_first(blk, h):
    return (h % 2) * (NM // 2) + blk * (NH // 2) + h // 2


def audio_tower(nc, x, w, out):
    NB = x.shape[0]
    NSYS = NB * NM * NQ // P
    with ExitStack() as ctx:
        def sem(name):
            return ctx.enter_context(nc.semaphore(name))

        def banks():
            return [c.enter_context(nc.psum_tensor(f"bank{n}", [P, 512], F32)) for n in range(8)]

        signals = []

        def signal(name, per=1, primed=1):
            signals.append(Signal(sem(name), per, primed))
            return signals[-1]

        dram = {
            "packa": nc.dram_tensor("packa", [NB, P, AW], F32, kind="Internal").ap(),
            "packb": nc.dram_tensor("packb", [NB, P, BW], F32, kind="Internal").ap(),
            "systems": nc.dram_tensor("systems", [NB * NM * NQ, SC, SC], F32, kind="Internal").ap(),
            "fl": nc.dram_tensor("fl", [NB, P, BLK * D], F32, kind="Internal").ap(),
            "taps": nc.dram_tensor("taps", [D, 512], F32, kind="Internal").ap(),
            "toeplitz": nc.dram_tensor("toeplitz", [P, D, TW], F32, kind="Internal").ap(),
        }
        c = ctx
        bank = banks()

        def sb(name, shape):
            return ctx.enter_context(nc.sbuf_tensor(name, shape, F32))

        ident = sb("ident", [P, P])
        upper = sb("upper", [P, 2 * P])
        expanded = ctx.enter_context(nc.semaphore("expanded"))
        shared = dict(expanded=expanded, NB=NB, NSYS=NSYS, dram=dram, bank=bank, ident=ident, upper=upper)
        make_constants(nc, ctx, ident, upper)
        with nc.sbuf_tensor("v_all", [P, D, BLK * NB], F32) as v_all:
            first_phase(nc, x, w, shared, v_all)
            second_phase(nc, shared, v_all)
        third_phase(nc, w, out, shared)


def make_constants(nc, ctx, ident, upper):
    made = ctx.enter_context(nc.semaphore("made"))
    with nc.Block() as block:
        @block.gpsimd
        def _(pool):
            pool.memset(ident[:, :], 0.0).then_inc(made, 1)
            pool.memset(upper[:, 0:P], 1.0).then_inc(made, 1)
            pool.memset(upper[:, P:], -1.0).then_inc(made, 1)
            pool.wait_ge(made, 3)
            pool.affine_select(out=ident[:, :], in_=ident[:, :], compare_op=ALU.not_equal, fill=1.0,
                               base=0, pattern=[[-1, P]], channel_multiplier=1).then_inc(made, 1)
            pool.affine_select(out=upper[:, 0:P], in_=upper[:, 0:P], compare_op=ALU.is_ge, fill=0.0,
                               base=0, pattern=[[1, P]], channel_multiplier=-1).then_inc(made, 1)
            pool.affine_select(out=upper[:, P:], in_=upper[:, P:], compare_op=ALU.is_gt, fill=0.0,
                               base=0, pattern=[[1, P]], channel_multiplier=-1).then_inc(made, 1)
            pool.wait_ge(made, 6)


def prime(nc, signals):
    with nc.Block() as block:
        @block.sync
        def _(sp):
            for g in signals:
                sp.sem_inc(g.sem, g.per * g.primed)


def first_phase(nc, x, w, shared, v_all):
    NB, dram, bank, ident, upper, expanded = (shared[k] for k in ("NB", "dram", "bank", "ident", "upper", "expanded"))
    with ExitStack() as c:
        def sb(name, shape):
            return c.enter_context(nc.sbuf_tensor(name, shape, F32))

        signals = []

        def signal(name, per=1, primed=1):
            signals.append(Signal(c.enter_context(nc.semaphore(name)), per, primed))
            return signals[-1]

        loaded = c.enter_context(nc.semaphore("p1_weights"))
        setup = c.enter_context(nc.semaphore("p1_setup"))
        started = c.enter_context(nc.semaphore("p1_started"))
        wqkv = sb("wqkv", [P, HALF, 3 * D])
        wb = sb("wb", [P, HALF, NH])
        convw = sb("convw", [P, 3 * HALF, CK])
        firw = sb("firw", [P, HALF, FS])
        flw = sb("flw", [P, HALF, FL])
        flr = sb("flr", [P, HALF, 512])
        headsel = sb("headsel", [P, 2])
        xs = [sb(f"x{s}", [P, BLK, D]) for s in range(2)]
        pa = [sb(f"pa{s}", [P, AW]) for s in range(2)]
        pb = [sb(f"pb{s}", [P, BW]) for s in range(2)]
        xT = sb("xT", [P, BLK, HALF, P])
        E = sb("E", [P, BLK, P])
        PT = sb("PT", [P, BLK, P])
        xn = sb("xn", [P, BLK, D])
        Y = sb("Y", [P, 3 * HALF, T])
        VT = sb("VT", [P, HALF, T])
        SQ = sb("SQ", [P, 2 * HALF, T])
        fsT = sb("fsT", [P, HALF, T])
        KB = sb("KB", [P, BLK, D])
        AT = sb("AT", [P, NM, P])
        mx, negmax, rs, rinv, veps, rstd = (sb(f"s{n}", [P, BLK]) for n in range(6))
        minus_half = sb("minus_half", [P, 2 * NM])
        st = sb("st", [P, BLK, 6])
        mv = sb("mv", [P, BLK, 2])
        eb, b1, kbs = (sb(f"t{n}", [P, NM]) for n in range(3))
        beta = [sb(f"beta{s}", [P, NM]) for s in range(2)]
        RS = sb("RS", [P, 2 * NM])
        RR = sb("RR", [P, BLK, 2, NH])

        def field(buf, at):
            return buf[:, at:at + HALF * T]

        def chans(buf, at):
            return field(buf, at).rearrange("p (a t) -> p a t", a=HALF)

        def toks(buf, at):
            return field(buf, at).rearrange("p (b c) -> p b c", b=BLK)

        x_loaded = [signal(f"x_loaded{s}", 32) for s in range(2)]
        packs_stored = [signal(f"packs_stored{s}", 32) for s in range(2)]
        at_stored = signal("at_stored", 16 * NQ)
        xT_ready = signal("xT_ready", 2)
        scores_ready = signal("scores_ready")
        probsT_ready = signal("probsT_ready")
        attn_ready = signal("attn_ready", 1, primed=2)
        xnT_ready = signal("xnT_ready", 2)
        beta_ready = signal("beta_ready")
        proj_ready = signal("proj_ready", 6)
        ssq_ready = signal("ssq_ready")
        ktok_ready = signal("ktok_ready")
        vtok_ready = signal("vtok_ready")
        fs_ready = signal("fs_ready")
        kbT_ready = signal("kbT_ready", 2)
        at_ready = signal("at_ready", 2)
        xT01_copied = signal("xT01_copied")
        xT2_copied = signal("xT2_copied")
        max_found = signal("max_found")
        negmax_ready = signal("negmax_ready")
        probs_ready = signal("probs_ready", BLK)
        rinv_ready = signal("rinv_ready")
        probsT_copied = signal("probsT_copied")
        h_ready = signal("h_ready", BLK)
        stats_done = signal("stats_done", BLK)
        mv_ready = signal("mv_ready", BLK)
        rstd_ready = signal("rstd_ready")
        xn_ready = signal("xn_ready", BLK)
        xnT0_copied = signal("xnT0_copied")
        xnT1_copied = signal("xnT1_copied")
        eb_ready = signal("eb_ready")
        beta_step = signal("beta_step", 2)
        tap_done = signal("tap_done", 6)
        conv_step = signal("conv_step", 18)
        silu_done = signal("silu_done", 6)
        sq_ready = signal("sq_ready", 2)
        rs_ready = signal("rs_ready")
        veps_ready = signal("veps_ready")
        rr_ready = signal("rr_ready")
        vbs_ready = signal("vbs_ready")
        scales_ready = signal("scales_ready")
        ktok_copied = signal("ktok_copied")
        vtok_copied = signal("vtok_copied")
        fir_step = signal("fir_step", 6)
        fs_copied = signal("fs_copied")
        kb_ready = signal("kb_ready")
        kbT0_copied = signal("kbT0_copied")
        kbT1_copied = signal("kbT1_copied")
        at_copied = signal("at_copied", 4)
        v_kept = signal("v_kept")
        prime(nc, signals)

        proj_bank = [bank[n] for n in (3, 4, 5, 6, 7, 3)]
        attn_bank = (bank[0], bank[2])
        at_bank = [bank[n] for n in (4, 5, 7, 6)]

        with nc.Block() as block:
            @block.vector
            def _(dve):
                for half in range(2):
                    for head in range(2):
                        dve.memset(headsel[half * DH:(half + 1) * DH, head:head + 1], float(half == head)).then_inc(started, 1)
                dve.memset(minus_half[:, :], -0.5).then_inc(started, 1)
                dve.wait_ge(started, 5)

            @block.sync
            def _(sp):
                for n, name in enumerate(("Wq", "Wk", "Wv")):
                    sp.dma_start(wqkv[:, :, n * D:(n + 1) * D],
                                 w[name].rearrange("(a p) n -> p a n", a=HALF)).then_inc(loaded, 16)
                    sp.dma_start(convw[:, n * HALF:(n + 1) * HALF, :],
                                 w[f"conv_{name[1]}_w"].rearrange("(a p) k -> p a k", a=HALF)).then_inc(loaded, 16)
                sp.dma_start(wb[:, :, :], w["Wb"].rearrange("(a p) n -> p a n", a=HALF)).then_inc(loaded, 16)
                sp.dma_start(firw[:, :, :], w["fir_short_w"].rearrange("(a g) v k -> (g v) a k", a=HALF)).then_inc(loaded, 16)
                sp.dma_start(flw[:, :, :], w["fir_long_w"].rearrange("(a g) v k -> (g v) a k", a=HALF)).then_inc(loaded, 16)
                sp.wait_ge(loaded, 16 * 9)
                sp.wait_ge(setup, 5)
                sp.dma_start(dram["taps"].rearrange("(a p) n -> p a n", a=HALF), flr[:, :, :]).then_inc(loaded, 16)
                sp.wait_ge(loaded, 16 * 10)

            @block.gpsimd
            def _(pool):
                pool.memset(flr[:, :, :], 0.0).then_inc(setup, 1)
                pool.memset(xs[0][:, BLK - 1, :], 0.0).then_inc(setup, 1)
                pool.memset(xs[1][:, BLK - 1, :], 0.0).then_inc(setup, 1)
                pool.wait_ge(loaded, 16 * 9)
                pool.wait_ge(setup, 3)
                for a in range(HALF):
                    pool.tensor_copy(flr[:, a, P - 1:P - 1 + FL], flw[:, a, ::-1]).then_inc(setup, 1)
                pool.wait_ge(setup, 5)

        with nc.Block() as block:
            @block.sync
            def _(sp):
                def load_x(n, s):
                    sp.wait_ge(*attn_ready.before(n, 2))
                    sp.dma_start(xs[s][:, 0:2, :], x[n, 0:2 * SEG, :].rearrange(
                        "(b p two) n -> p b two n", b=2, two=STEP)[:, :, 0, :]).then_inc(x_loaded[s].sem, 16)
                    rows = (x.shape[1] - 2 * SEG) // STEP
                    sp.dma_start(xs[s][0:rows, 2, :], x[n, 2 * SEG:2 * SEG + rows * STEP, :].rearrange(
                        "(p two) n -> p two n", two=STEP)[:, 0, :]).then_inc(x_loaded[s].sem, 16)

                def store_packs(it, s):
                    sp.wait_ge(*fs_copied.now(it))
                    sp.wait_ge(*kbT0_copied.now(it))
                    sp.wait_ge(*kbT1_copied.now(it))
                    sp.wait_ge(*xnT1_copied.now(it))
                    sp.dma_start(dram["packa"][it], pa[s][:, :]).then_inc(packs_stored[s].sem, 16)
                    sp.dma_start(dram["packb"][it], pb[s][:, :]).then_inc(packs_stored[s].sem, 16)
                    sp.wait_ge(*at_copied.now(it))
                    sysv = dram["systems"].rearrange("(n m q) j i -> n q j m i", m=NM, q=NQ)
                    for q in range(NQ):
                        sp.dma_start(sysv[it, q], AT[q * SC:(q + 1) * SC, :, q * SC:(q + 1) * SC])\
                            .then_inc(at_stored.sem, 16)

                def expand(it):
                    for k in range(P // NB):
                        p = it * (P // NB) + k
                        sp.dma_start(dram["toeplitz"][p], dram["taps"][:, bass.ds(P - 1 - p, TW)]).then_inc(expanded, 16)

                load_x(0, 0)
                load_x(1, 1)
                with sp.Fori(0, NB // 2 - 1) as i:
                    for s in range(2):
                        expand(2 * i + s)
                        load_x(2 * i + s + 2, s)
                        store_packs(2 * i + s, s)
                for s in range(2):
                    expand(NB - 2 + s)
                    store_packs(NB - 2 + s, s)
                for s in range(2):
                    sp.wait_ge(*packs_stored[s].before(NB // 2))
                sp.wait_ge(*at_stored.before(NB))

            @block.tensor
            def _(pe):
                def transpose_x(n, s, pair):
                    pe.wait_ge(*x_loaded[s].now(pair))
                    pe.wait_ge(*xnT0_copied.before(n))
                    pe.wait_ge(*xnT1_copied.before(n))
                    for b in range(BLK):
                        for a in range(HALF):
                            o = (b % 2) * D + a * P
                            mm = pe.transpose(bank[b // 2][:, o:o + P], xs[s][:, b, a * P:(a + 1) * P], ident[:, :])
                        if b:
                            mm.then_inc(xT_ready.sem, 1)

                def scores(n):
                    pe.wait_ge(*xT01_copied.now(n))
                    pe.wait_ge(*xT2_copied.now(n))
                    pe.wait_ge(*eb_ready.before(n))
                    for b in range(BLK):
                        for a in range(HALF):
                            mm = pe.matmul(bank[2][:, b * P:(b + 1) * P], xT[:, b, a, :], xT[:, b, a, :],
                                           start=(a == 0), stop=(a == HALF - 1))
                    mm.then_inc(scores_ready.sem, 1)

                def transpose_probs(n):
                    pe.wait_ge(*probs_ready.now(n))
                    for b in range(BLK):
                        mm = pe.transpose(bank[1][:, b * P:(b + 1) * P], E[:, b, :], ident[:, :])
                    mm.then_inc(probsT_ready.sem, 1)

                def attend(n, s):
                    pe.wait_ge(*probsT_copied.now(n))
                    for b in range(BLK):
                        mm = pe.matmul(attn_bank[b // 2][:, (b % 2) * D:(b % 2 + 1) * D], PT[:, b, :], xs[s][:, b, :],
                                       start=True, stop=True)
                    mm.then_inc(attn_ready.sem, 1)

                def transpose_normed(n):
                    pe.wait_ge(*xn_ready.now(n))
                    for a in range(HALF):
                        for b in range(BLK):
                            mm = pe.transpose(bank[1 - a][:, b * P:(b + 1) * P], xn[:, b, a * P:(a + 1) * P], ident[:, :])
                        mm.then_inc(xnT_ready.sem, 1)

                def project_beta(n, s):
                    xnT = chans(pb[s], XNT)
                    pe.wait_ge(*xnT0_copied.now(n))
                    pe.wait_ge(*xnT1_copied.now(n))
                    for b in range(BLK):
                        for a in range(HALF):
                            mm = pe.matmul(bank[2][:, b * NH:(b + 1) * NH], xnT[:, a, b * P:(b + 1) * P], wb[:, a, :],
                                           start=(a == 0), stop=(a == HALF - 1))
                    mm.then_inc(beta_ready.sem, 1)

                def project(it, s, j):
                    xnT = chans(pb[s], XNT)
                    if j == 0:
                        pe.wait_ge(*fs_copied.before(it))
                    elif j < 5:
                        pe.wait_ge(*at_copied.now(it - 1, (1, 2, 4, 3)[j - 1]))
                    else:
                        pe.wait_ge(*conv_step.now(it, 5))
                    for a in range(HALF):
                        mm = pe.matmul(proj_bank[j][:, 0:T], wqkv[:, a, j * P:(j + 1) * P], xnT[:, a, :],
                                       start=(a == 0), stop=(a == HALF - 1))
                    mm.then_inc(proj_ready.sem, 1)

                def sum_squares(it):
                    pe.wait_ge(*sq_ready.now(it))
                    for b in range(BLK):
                        for n in range(2 * HALF):
                            o = b * 2 * NH + n * 2
                            mm = pe.matmul(bank[4][:, o:o + 2], SQ[:, n, b * P:(b + 1) * P], headsel[:, :],
                                           start=True, stop=True)
                    mm.then_inc(ssq_ready.sem, 1)

                def to_tokens(src, near, far):
                    for b in range(BLK):
                        for a in range(HALF):
                            o = (b % 2) * D + a * P
                            mm = pe.transpose(bank[(near, far)[b // 2]][:, o:o + P], src[:, a, b * P:(b + 1) * P], ident[:, :])
                    return mm

                def transpose_kb(it):
                    pe.wait_ge(*kb_ready.now(it))
                    for a in range(HALF):
                        for b in range(BLK):
                            mm = pe.transpose(bank[4 + a][:, b * P:(b + 1) * P], KB[:, b, a * P:(a + 1) * P], ident[:, :])
                        mm.then_inc(kbT_ready.sem, 1)

                def k_kb(it, s):
                    kT, kbT = chans(pa[s], KT), chans(pa[s], KBT)
                    pe.wait_ge(*kbT0_copied.now(it))
                    pe.wait_ge(*kbT1_copied.now(it))
                    for b in range(BLK):
                        if b == 2:
                            pe.wait_ge(*fs_copied.now(it))
                        for hh in range(NH // 2):
                            for odd in range(2):
                                e = b * (NH // 2) + hh
                                rows = slice(odd * DH, (odd + 1) * DH)
                                mm = pe.matmul(at_bank[2 * (e // 4) + odd][:, (e % 4) * P:(e % 4 + 1) * P],
                                               kT[rows, hh, b * P:(b + 1) * P], kbT[rows, hh, b * P:(b + 1) * P],
                                               start=True, stop=True)
                        if b:
                            mm.then_inc(at_ready.sem, 1)

                def body(it, s, n=None, pair=None):
                    if n is not None:
                        transpose_x(n, 1 - s, pair)
                    project(it, s, 0)
                    project(it, s, 1)
                    if n is not None:
                        scores(n)
                    for j in (2, 3, 4):
                        project(it, s, j)
                    if n is not None:
                        transpose_probs(n)
                    project(it, s, 5)
                    if n is not None:
                        attend(n, 1 - s)
                    sum_squares(it)
                    to_tokens(chans(pa[s], KT), 5, 6).then_inc(ktok_ready.sem, 1)
                    if n is not None:
                        transpose_normed(n)
                    pe.wait_ge(*silu_done.now(it, 6))
                    to_tokens(VT, 7, 3).then_inc(vtok_ready.sem, 1)
                    if n is not None:
                        project_beta(n, 1 - s)
                    transpose_kb(it)
                    pe.wait_ge(*fir_step.now(it))
                    pe.wait_ge(*vtok_copied.now(it))
                    pe.wait_ge(*ktok_copied.now(it))
                    to_tokens(fsT, 6, 3).then_inc(fs_ready.sem, 1)
                    k_kb(it, s)

                transpose_x(0, 0, 0)
                scores(0)
                transpose_probs(0)
                attend(0, 0)
                transpose_normed(0)
                project_beta(0, 0)
                with pe.Fori(0, NB // 2 - 1) as i:
                    body(2 * i, 0, 2 * i + 1, i)
                    body(2 * i + 1, 1, 2 * i + 2, i + 1)
                body(NB - 2, 0, NB - 1, NB // 2 - 1)
                body(NB - 1, 1)

            @block.scalar
            def _(act):
                def copy(dst, src):
                    return act.activation(dst, src, ACT.Copy)

                def copy_xT(n):
                    act.wait_ge(*xT_ready.now(n, 1))
                    copy(xT[:, 0:2, :, :].rearrange("p b a t -> p (b a t)"), bank[0][:, :]).then_inc(xT01_copied.sem, 1)

                def exp_scores(n):
                    act.wait_ge(*negmax_ready.now(n))
                    for b in range(BLK):
                        act.activation(E[:, b, :], bank[2][:, b * P:(b + 1) * P], ACT.Exp, bias=negmax[:, b:b + 1],
                                       scale=float(D) ** -0.5, accum_out=rs[:, b:b + 1]).then_inc(probs_ready.sem, 1)

                def copy_probsT(n):
                    act.wait_ge(*probsT_ready.now(n))
                    copy(PT[:, :, :].rearrange("p b t -> p (b t)"), bank[1][:, 0:T]).then_inc(probsT_copied.sem, 1)

                def divide_attn(n, s, pair):
                    H = toks(pb[s], HF)
                    act.wait_ge(*attn_ready.now(n))
                    act.wait_ge(*rinv_ready.now(n))
                    act.wait_ge(*packs_stored[s].before(pair))
                    for b in range(BLK):
                        act.activation(H[:, b, :], attn_bank[b // 2][:, (b % 2) * D:(b % 2 + 1) * D], ACT.Copy,
                                       scale=rinv[:, b:b + 1]).then_inc(h_ready.sem, 1)

                def copy_xnT(n, s):
                    act.wait_ge(*xnT_ready.now(n, 1))
                    copy(chans(pb[s], XNT)[:, 0, :], bank[1][:, 0:T]).then_inc(xnT0_copied.sem, 1)

                def exp_beta(n):
                    act.wait_ge(*beta_ready.now(n))
                    act.wait_ge(*beta_step.before(n))
                    act.activation(eb[:, :], bank[2][:, 0:NM], ACT.Exp, scale=-1.0).then_inc(eb_ready.sem, 1)

                def last_tap(it, j):
                    act.wait_ge(*proj_ready.now(it, j + 1))
                    act.activation(Y[:, j, :], proj_bank[j][:, 0:T], ACT.Copy, scale=convw[:, j, CK - 1:CK])\
                        .then_inc(tap_done.sem, 1)

                def silu(it, s, j):
                    dst = (chans(pa[s], QT), chans(pa[s], KT), VT)[j // 2]
                    act.wait_ge(*conv_step.now(it, 6 * (j // 2) + 5 + j % 2))
                    if j == 4:
                        act.wait_ge(*fir_step.before(it))
                        act.wait_ge(*vtok_ready.before(it))
                    act.activation(dst[:, j % 2, :], Y[:, j, :], ACT.Silu).then_inc(silu_done.sem, 1)

                def body(it, s, own, n=None, pair=None):
                    if n is not None:
                        copy_xT(n)
                    last_tap(it, 0)
                    last_tap(it, 1)
                    if n is not None:
                        exp_scores(n)
                    last_tap(it, 2)
                    last_tap(it, 3)
                    last_tap(it, 4)
                    if n is not None:
                        copy_probsT(n)
                    last_tap(it, 5)
                    if n is not None:
                        divide_attn(n, 1 - s, pair)
                    act.wait_ge(*packs_stored[s].before(own))
                    for j in range(4):
                        silu(it, s, j)
                    act.wait_ge(*silu_done.now(it, 4))
                    for f in range(2):
                        act.activation(SQ[:, 2 * f:2 * f + 2, :].rearrange("p a t -> p (a t)"),
                                       field(pa[s], (QT, KT)[f]), ACT.Square).then_inc(sq_ready.sem, 1)
                    silu(it, s, 4)
                    silu(it, s, 5)
                    act.wait_ge(*ktok_ready.now(it))
                    copy(field(pa[s], KTOK)[:, 0:2 * D], bank[5][:, :])
                    copy(field(pa[s], KTOK)[:, 2 * D:], bank[6][:, 0:D]).then_inc(ktok_copied.sem, 1)
                    if n is not None:
                        copy_xnT(n, 1 - s)
                        exp_beta(n)
                    act.wait_ge(*kbT_ready.now(it, 1))
                    copy(chans(pa[s], KBT)[:, 0, :], bank[4][:, 0:T]).then_inc(kbT0_copied.sem, 1)
                    act.wait_ge(*fs_ready.now(it))
                    copy(field(pb[s], FSF)[:, 0:2 * D], bank[6][:, :])
                    copy(field(pb[s], FSF)[:, 2 * D:], bank[3][:, 0:D]).then_inc(fs_copied.sem, 1)

                copy_xT(0)
                exp_scores(0)
                copy_probsT(0)
                divide_attn(0, 0, 0)
                copy_xnT(0, 0)
                exp_beta(0)
                with act.Fori(0, NB // 2 - 1) as i:
                    body(2 * i, 0, i, 2 * i + 1, i)
                    body(2 * i + 1, 1, i, 2 * i + 2, i + 1)
                body(NB - 2, 0, NB // 2 - 1, NB - 1, NB // 2 - 1)
                body(NB - 1, 1, NB // 2 - 1)

            @block.vector
            def _(dve):
                def copy_xT(n):
                    dve.wait_ge(*xT_ready.now(n, 2))
                    dve.tensor_copy(xT[:, 2, :, :].rearrange("p a t -> p (a t)"), bank[1][:, 0:D]).then_inc(xT2_copied.sem, 1)

                def find_max(n):
                    dve.wait_ge(*scores_ready.now(n))
                    dve.tensor_reduce(mx[:, :], bank[2][:, 0:T].rearrange("p (b t) -> p b t", b=BLK), AX.X, ALU.max)\
                        .then_inc(max_found.sem, 1)
                    dve.wait_ge(*max_found.now(n))
                    dve.tensor_scalar(negmax[:, :], mx[:, :], -float(D) ** -0.5, None, ALU.mult).then_inc(negmax_ready.sem, 1)

                def invert_sums(n):
                    dve.wait_ge(*probs_ready.now(n))
                    dve.reciprocal(rinv[:, :], rs[:, :]).then_inc(rinv_ready.sem, 1)

                def norm_stats(n, s):
                    H = toks(pb[s], HF)
                    for b in range(BLK):
                        dve.wait_ge(*h_ready.now(n, b + 1))
                        dve.bn_stats(st[:, b, :], H[:, b, :]).then_inc(stats_done.sem, 1)
                    dve.wait_ge(started, 1)
                    dve.wait_ge(*stats_done.now(n))
                    for b in range(BLK):
                        dve.bn_aggr(mv[:, b, :], st[:, b, :]).then_inc(mv_ready.sem, 1)
                    dve.wait_ge(*mv_ready.now(n))
                    dve.tensor_scalar(veps[:, :], mv[:, :, 1], 1e-5, None, ALU.add).then_inc(veps_ready.sem, 1)

                def normalise(n, s):
                    H = toks(pb[s], HF)
                    dve.wait_ge(*rstd_ready.now(n))
                    for b in range(BLK):
                        dve.tensor_scalar(xn[:, b, :], H[:, b, :], mv[:, b, 0:1], rstd[:, b:b + 1],
                                          ALU.subtract, ALU.mult).then_inc(xn_ready.sem, 1)

                def copy_xnT(n, s):
                    dve.wait_ge(*xnT_ready.now(n, 2))
                    dve.tensor_copy(chans(pb[s], XNT)[:, 1, :], bank[0][:, 0:T]).then_inc(xnT1_copied.sem, 1)

                def finish_beta(n, s):
                    dve.wait_ge(*eb_ready.now(n))
                    dve.tensor_scalar(b1[:, :], eb[:, :], 1.0, None, ALU.add).then_inc(beta_step.sem, 1)
                    dve.wait_ge(*beta_step.now(n, 1))
                    dve.reciprocal(beta[s][:, :], b1[:, :]).then_inc(beta_step.sem, 1)

                def other_taps(it, n):
                    for lag in range(1, CK):
                        for a in range(HALF):
                            j = 2 * n + a
                            if lag == 1:
                                dve.wait_ge(*tap_done.now(it, j + 1))
                            else:
                                dve.wait_ge(*conv_step.now(it, 6 * n + 2 * (lag - 2) + a + 1))
                            dve.scalar_tensor_tensor(out=Y[:, j, lag:T], in0=proj_bank[j][:, 0:T - lag],
                                                     scalar=convw[:, j, CK - 1 - lag:CK - lag], in1=Y[:, j, lag:T],
                                                     op0=ALU.mult, op1=ALU.add).then_inc(conv_step.sem, 1)

                def scales(it, s):
                    dve.wait_ge(*rr_ready.now(it))
                    dve.wait_ge(*beta_step.now(it, 2))
                    vbs = pa[s][:, VBS:VBS + NM]
                    dve.tensor_tensor(vbs.rearrange("p (b h) -> p b h", b=BLK),
                                      beta[s][:, :].rearrange("p (b h) -> p b h", b=BLK), RR[:, :, 1, :], ALU.mult)\
                        .then_inc(vbs_ready.sem, 1)
                    dve.tensor_copy(pa[s][:, RQ:RQ + NM].rearrange("p (b h) -> p b h", b=BLK), RR[:, :, 0, :])
                    dve.wait_ge(*vbs_ready.now(it))
                    dve.tensor_tensor(kbs[:, :].rearrange("p (b h) -> p b h", b=BLK),
                                      vbs.rearrange("p (b h) -> p b h", b=BLK), RR[:, :, 1, :], ALU.mult)\
                        .then_inc(scales_ready.sem, 1)

                def short_fir(it):
                    dve.wait_ge(*silu_done.now(it, 6))
                    dve.wait_ge(*fs_ready.before(it))
                    for a in range(HALF):
                        dve.tensor_scalar(fsT[:, a, :], VT[:, a, :], firw[:, a, FS - 1:FS], None, ALU.mult).then_inc(fir_step.sem, 1)
                    for lag in range(1, FS):
                        for a in range(HALF):
                            dve.wait_ge(*fir_step.now(it, 2 * (lag - 1) + a + 1))
                            dve.scalar_tensor_tensor(out=fsT[:, a, lag:T], in0=VT[:, a, 0:T - lag],
                                                     scalar=firw[:, a, FS - 1 - lag:FS - lag], in1=fsT[:, a, lag:T],
                                                     op0=ALU.mult, op1=ALU.add).then_inc(fir_step.sem, 1)

                def mask_a(it):
                    dve.wait_ge(*at_stored.before(it))
                    for n in range(4):
                        odd, far = n % 2, n // 2
                        m = 2 if far else 4
                        o = odd * NM // 2 + far * 4
                        dve.wait_ge(*at_ready.now(it, far + 1))
                        dve.tensor_tensor(AT[:, o:o + m, :], at_bank[n][:, 0:m * P].rearrange("p (m t) -> p m t", m=m),
                                          upper[:, P:].unsqueeze(1).broadcast_to([P, m, P]), ALU.mult).then_inc(at_copied.sem, 1)

                def body(it, s, n=None):
                    if n is not None:
                        copy_xT(n)
                    other_taps(it, 0)
                    if n is not None:
                        find_max(n)
                    other_taps(it, 1)
                    if n is not None:
                        invert_sums(n)
                    other_taps(it, 2)
                    if n is not None:
                        norm_stats(n, 1 - s)
                    dve.wait_ge(*ssq_ready.now(it))
                    dve.tensor_scalar(RS[:, :], bank[4][:, 0:2 * NM], 1e-6, None, ALU.add).then_inc(rs_ready.sem, 1)
                    if n is not None:
                        normalise(n, 1 - s)
                    short_fir(it)
                    if n is not None:
                        copy_xnT(n, 1 - s)
                    scales(it, s)
                    dve.wait_ge(*vtok_ready.now(it))
                    dve.tensor_copy(field(pa[s], VTOK)[:, 0:2 * D], bank[7][:, :])
                    dve.tensor_copy(field(pa[s], VTOK)[:, 2 * D:], bank[3][:, 0:D]).then_inc(vtok_copied.sem, 1)
                    if n is not None:
                        finish_beta(n, 1 - s)
                    dve.wait_ge(*kbT_ready.now(it, 2))
                    dve.tensor_copy(chans(pa[s], KBT)[:, 1, :], bank[5][:, 0:T]).then_inc(kbT1_copied.sem, 1)
                    mask_a(it)

                copy_xT(0)
                find_max(0)
                invert_sums(0)
                norm_stats(0, 0)
                normalise(0, 0)
                copy_xnT(0, 0)
                finish_beta(0, 0)
                with dve.Fori(0, NB // 2 - 1) as i:
                    body(2 * i, 0, 2 * i + 1)
                    body(2 * i + 1, 1, 2 * i + 2)
                body(NB - 2, 0, NB - 1)
                body(NB - 1, 1)

            @block.gpsimd
            def _(pool):
                def inverse_std(n):
                    pool.wait_ge(*veps_ready.now(n))
                    pool.tensor_tensor(rstd[:, :], veps[:, :], minus_half[:, 0:BLK], ALU.pow).then_inc(rstd_ready.sem, 1)

                def body(it, s, n=None):
                    if n is not None:
                        inverse_std(n)
                    pool.wait_ge(*rs_ready.now(it))
                    pool.tensor_tensor(RR[:, :, :, :].rearrange("p b n h -> p (b n h)"), RS[:, :], minus_half[:, :], ALU.pow)\
                        .then_inc(rr_ready.sem, 1)
                    pool.wait_ge(*scales_ready.now(it))
                    pool.wait_ge(*ktok_copied.now(it))
                    pool.tensor_tensor(KB[:, :, :].rearrange("p b (h d) -> p (b h) d", h=NH),
                                       field(pa[s], KTOK).rearrange("p (m d) -> p m d", d=DH),
                                       kbs[:, :].unsqueeze(2).broadcast_to([P, NM, DH]), ALU.mult).then_inc(kb_ready.sem, 1)
                    pool.wait_ge(*vtok_copied.now(it))
                    for b in range(BLK):
                        keep = pool.tensor_copy(v_all[:, :, it + b * NB], toks(pa[s], VTOK)[:, b, :])
                    keep.then_inc(v_kept.sem, 1)

                inverse_std(0)
                with pool.Fori(0, NB // 2 - 1) as i:
                    body(2 * i, 0, 2 * i + 1)
                    body(2 * i + 1, 1, 2 * i + 2)
                body(NB - 2, 0, NB - 1)
                body(NB - 1, 1)


def second_phase(nc, shared, v_all):
    NB, NSYS, dram, bank, expanded = (shared[k] for k in ("NB", "NSYS", "dram", "bank", "expanded"))
    CG = 8
    SG = 6 if NSYS % 6 == 0 else NSYS
    with ExitStack() as c:
        def sb(name, shape):
            return c.enter_context(nc.sbuf_tensor(name, shape, F32))

        signals = []

        def signal(name, per=1, primed=1):
            signals.append(Signal(c.enter_context(nc.semaphore(name)), per, primed))
            return signals[-1]

        toep = [sb(f"toep{s}", [P, CG, TW]) for s in range(2)]
        X = sb("X", [P, SG, SC, SC])
        GC = 64
        GI = GC // CG
        stage = [sb(f"stage{s}", [P, BLK * NB, GC]) for s in range(2)]
        fl_stored = [signal(f"fl_stored{s}", 16 * BLK) for s in range(2)]
        prod = sb("prod", [P, SG * (SC // 2) * (SC // 2 - 1)])
        toep_loaded = [signal(f"toep_loaded{s}", 16) for s in range(2)]
        fl_ready = signal("fl_ready", 2, primed=2)
        fl_copied = signal("fl_copied", 2, primed=2)
        sys_loaded = c.enter_context(nc.semaphore("sys_loaded"))
        sys_stored = c.enter_context(nc.semaphore("sys_stored"))
        solve_step = c.enter_context(nc.semaphore("solve_step"))
        prime(nc, signals)
        systems = dram["systems"].rearrange("(p s) j i -> p s j i", s=NSYS)
        steps = 1 + 2 * (SC - 2)

        with nc.Block() as block:
            @block.sync
            def _(sp):
                sp.wait_ge(expanded, 16 * P)
                with sp.Fori(0, D // CG // 2) as i:
                    for s in range(2):
                        it = i * 2 + s
                        sp.wait_ge(*fl_ready.before(it, 2))
                        sp.dma_start(toep[s][:, :, :], dram["toeplitz"][:, bass.ds(it * CG, CG), :]).then_inc(toep_loaded[s].sem, 16)

            @block.tensor
            def _(pe):
                with pe.Fori(0, D // CG // 2) as i:
                    for s in range(2):
                        it = i * 2 + s
                        pe.wait_ge(*toep_loaded[s].now(i))
                        pe.wait_ge(*fl_copied.before(it, 2))
                        for ch in range(CG):
                            o = (ch % 4) * BLK * NB
                            acc = bank[2 * s + ch // 4]
                            pe.matmul(acc[:, o:o + BLK * NB], toep[s][:, ch, 0:P], v_all[:, it * CG + ch, :],
                                      start=True, stop=False, skip_group_check=True)
                            mm = pe.matmul(acc[0:TW - P, o + NB:o + BLK * NB], toep[s][:, ch, P:], v_all[:, it * CG + ch, 0:(BLK - 1) * NB],
                                           start=False, stop=True, skip_group_check=True)
                            if ch % 4 == 3:
                                mm.then_inc(fl_ready.sem, 1)

            @block.scalar
            def _(act):
                with act.Fori(0, D // GC // 2) as i:
                    for g in range(2):
                        act.wait_ge(*fl_stored[g].before(i))
                        for j in range(GI):
                            it = (i * 2 + g) * GI + j
                            for half in range(2):
                                act.wait_ge(*fl_ready.now(it, half + 1))
                                c0 = j * CG + half * 4
                                act.activation(stage[g][:, :, c0:c0 + 4].rearrange("p n c -> p c n"),
                                               bank[2 * (j % 2) + half][:, 0:4 * BLK * NB].rearrange("p (c n) -> p c n", c=4), ACT.Copy)\
                                    .then_inc(fl_copied.sem, 1)
                        act.wait_ge(*fl_copied.now((i * 2 + g) * GI + GI - 1))
                        for b in range(BLK):
                            act.dma_start(dram["fl"][:, :, bass.ds(b * D + (i * 2 + g) * GC, GC)].rearrange("n p c -> p n c"),
                                          stage[g][:, b * NB:(b + 1) * NB, :]).then_inc(fl_stored[g].sem, 16)
                for g in range(2):
                    act.wait_ge(*fl_stored[g].before(D // GC // 2))

            @block.gpsimd
            def _(pool):
                for g in range(NSYS // SG):
                    pool.wait_ge(solve_step, steps * g)
                    if g:
                        pool.wait_ge(sys_stored, 16 * g)
                    pool.dma_start(X[:, :, :, :], systems[:, g * SG:(g + 1) * SG]).then_inc(sys_loaded, 16)
                    pool.wait_ge(solve_step, steps * (g + 1))
                    pool.dma_start(systems[:, g * SG:(g + 1) * SG], X[:, :, :, :]).then_inc(sys_stored, 16)
                pool.wait_ge(sys_stored, 16 * (NSYS // SG))

            @block.vector
            def _(dve):
                for g in range(NSYS // SG):
                    done = steps * g + 1
                    dve.wait_ge(sys_loaded, 16 * (g + 1))
                    dve.memset(X[:, :, :, :].rearrange("p s j i -> p s (j i)")[:, :, ::SC + 1], 1.0).then_inc(solve_step, 1)
                    dve.wait_ge(solve_step, done)
                    for j in range(1, SC - 1):
                        n = SC - 1 - j
                        pr = prod[:, 0:SG * j * n].rearrange("p (s j n) -> p s j n", s=SG, j=j)
                        dve.tensor_tensor(pr, X[:, :, 0:j, j:j + 1].broadcast_to([P, SG, j, n]),
                                          X[:, :, j:j + 1, j + 1:].broadcast_to([P, SG, j, n]), ALU.mult).then_inc(solve_step, 1)
                        done += 1
                        dve.wait_ge(solve_step, done)
                        dve.tensor_tensor(X[:, :, 0:j, j + 1:], X[:, :, 0:j, j + 1:], pr, ALU.add).then_inc(solve_step, 1)
                        done += 1
                        dve.wait_ge(solve_step, done)


def third_phase(nc, w, out, shared):
    NB, dram, bank, ident, upper = (shared[k] for k in ("NB", "dram", "bank", "ident", "upper"))
    with ExitStack() as c:
        def sb(name, shape):
            return c.enter_context(nc.sbuf_tensor(name, shape, F32))

        signals = []

        def signal(name, per=1, primed=1):
            signals.append(Signal(c.enter_context(nc.semaphore(name)), per, primed))
            return signals[-1]

        loaded = c.enter_context(nc.semaphore("p3_weights"))
        setup = c.enter_context(nc.semaphore("p3_setup"))
        setup_act = c.enter_context(nc.semaphore("p3_setup_act"))
        MC = MLP // P
        w1g = sb("w1g", [P, HALF, MLP])
        w1s = sb("w1s", [GATE_S, MLP])
        b1g = sb("b1g", [P, MC])
        w2g = sb("w2g", [P, MC, 4 * NH])
        b2g = sb("b2g", [P, 4 * NH])
        wo = sb("wo", [P, HALF, D])
        onw = sb("onw", [P, 1])
        router = sb("router", [P, HALF, NE])
        anchors = sb("anchors", [P, NE, ND])
        before_e = sb("before_e", [P, NE, NE])
        rclip = sb("rclip", [P, 1])
        w1e = sb("w1e", [P, HALF, NE, DE])
        w2e = sb("w2e", [P, NE, D])
        temp = sb("temp", [P, 4, NH])
        itemp = sb("itemp", [P, NH])
        pa = [sb(f"qa{s}", [P, AW]) for s in range(2)]
        pb = [sb(f"qb{s}", [P, BW]) for s in range(2)]
        fl = [sb(f"fl{s}", [P, HALF * T]) for s in range(2)]
        ATM = sb("ATM", [P, NM, 2 * P])
        UF = sb("UF", [P, NM, P])
        TL = sb("TL", [P, NM, DH])
        P1 = sb("P1", [P, NM, SC])
        P1B = sb("P1B", [P, NM, DH])
        VB = sb("VB", [P, NM, DH])
        R = sb("R", [P, NH, DH])
        W = sb("W", [P, NH, DH])
        S = sb("S", [P, NH // 2, DH])
        DL = [sb(f"DL{s}", [P, NM, DH]) for s in range(2)]
        HA = [sb(f"HA{s}", [P, BLK, D]) for s in range(2)]
        ta = sb("ta", [P, BLK * D])
        tb = sb("tb", [P, BLK * D])
        tc_ = sb("tc", [P, NM, DH])
        y = sb("y", [P, BLK * D])
        ONT = sb("ONT", [P, HALF, T])
        YT = sb("YT", [P, HALF, T])
        GH = sb("GH", [P, MC, T])
        HE = [sb(f"HE{s}", [P, T]) for s in range(2)]
        minus_half = sb("minus_half_q", [P, NM])
        SGT = sb("SGT", [GATE_S, T])
        ST = sb("ST", [P, 4, NM, 6])
        SG = sb("SG", [P, BLK, 4, 2, NH])
        st1, st2, st3, st4 = (sb(f"st{n}", [P, 4, NM]) for n in range(4))
        L = sb("L", [P, NM, 4])
        WT = sb("WT", [P, NM, 4])
        m12, s12, r12 = (sb(f"m{n}", [P, NM]) for n in range(3))
        bst = sb("bst", [P, BLK, 6])
        bmv = sb("bmv", [P, BLK, 2])
        bv, br = (sb(f"b{n}", [P, BLK]) for n in range(2))
        qr, lg, rank, ex, we = (sb(f"e{n}", [P, BLK, NE]) for n in range(5))
        cmp, eqs = (sb(f"c{n}", [P, BLK, NE, NE]) for n in range(2))
        me, se, re = (sb(f"g{n}", [P, BLK]) for n in range(3))

        def field(buf, at):
            return buf[:, at:at + HALF * T]

        def chans(buf, at):
            return field(buf, at).rearrange("p (a t) -> p a t", a=HALF)

        def toks(buf, at):
            return field(buf, at).rearrange("p (b c) -> p b c", b=BLK)

        def heads(buf, at):
            return field(buf, at).rearrange("p (m d) -> p m d", d=DH)

        mlp_bank = [bank[n] for n in (4, 5, 3, 4)]

        def expert_bank(b):
            return bank[7][:, b * D:(b + 1) * D] if b < 2 else bank[2][:, D:2 * D]

        pa_loaded = [signal(f"pa_loaded{s}", 16) for s in range(2)]
        pb_loaded = [signal(f"pb_loaded{s}", 16) for s in range(2)]
        fl_loaded = [signal(f"fl_loaded{s}", 16) for s in range(2)]
        uf_loaded = signal("uf_loaded", 16 * NQ)
        out_stored = signal("out_stored", 16, primed=2)
        qk_ready = signal("qk_ready", 6)
        masked = signal("masked", 6)
        tdiag_ready = signal("tdiag_ready")
        p1_ready, p1_copied = signal("p1_ready"), signal("p1_copied")
        u12_ready, u12_copied = signal("u12_ready"), signal("u12_copied")
        p1b_ready, p1b_copied = signal("p1b_ready"), signal("p1b_copied")
        u12b_ready, u12b_copied = signal("u12b_ready"), signal("u12b_copied")
        vb_ready = signal("vb_ready")
        r_ready, r_copied = signal("r_ready", 2), signal("r_copied", 2)
        w_ready, w_copied = signal("w_ready", 3), signal("w_copied", 3)
        s_ready, s_copied = signal("s_ready", 2), signal("s_copied", 2)
        o_ready, d_ready = signal("o_ready", 3), signal("d_ready", 3)
        branch_stats = signal("branch_stats")
        stat_step = signal("stat_step", 4)
        vmax_ready = signal("vmax_ready")
        std_ready = signal("std_ready")
        sgT_ready, sgT_copied = signal("sgT_ready"), signal("sgT_copied")
        mlp_ready, g1_ready = signal("mlp_ready", 4), signal("g1_ready", 4)
        logits_ready = signal("logits_ready")
        gate_step = signal("gate_step", 3)
        lg_ready, wexp_ready = signal("lg_ready"), signal("wexp_ready")
        wt_step = signal("wt_step", 3)
        fsw_ready, vw_ready = signal("fsw_ready"), signal("vw_ready")
        mix_step = signal("mix_step", 5)
        sq_ready, ss_ready, ms_ready = signal("q_sq_ready"), signal("ss_ready"), signal("ms_ready")
        rr_ready = signal("q_rr_ready")
        on_ready = signal("on_ready")
        onT_ready, onT0_copied, onT1_copied = signal("onT_ready", 2), signal("onT0_copied"), signal("onT1_copied")
        wo_ready, h2_ready = signal("wo_ready"), signal("h2_ready")
        bst_ready, bmv_ready, veps_ready = signal("bst_ready"), signal("bmv_ready"), signal("q_veps_ready")
        rstd_ready = signal("q_rstd_ready")
        y_ready = signal("y_ready", BLK)
        yT_ready, yT0_copied, yT1_copied = signal("yT_ready", 2), signal("yT0_copied"), signal("yT1_copied")
        z_ready, q_ready = signal("z_ready"), signal("q_ready", primed=2)
        route_step = signal("route_step", 9)
        lr_ready, er_ready = signal("q_lr_ready"), signal("er_ready")
        we_step = signal("we_step", 4)
        hid_ready, he_ready = signal("hid_ready", NE), signal("he_ready", NE)
        eo_ready = signal("eo_ready", NE)
        acc_done = signal("acc_done", NE * BLK)
        prime(nc, signals)

        with nc.Block() as block:
            @block.sync
            def _(sp):
                def load(dst, src):
                    sp.dma_start(dst, src).then_inc(loaded, 16)
                load(w1g[:, :, :], w["mlp_w1"][0:D].rearrange("(a p) n -> p a n", a=HALF))
                load(w1s[:, :], w["mlp_w1"][D:])
                load(w2g[:, :, :], w["mlp_w2"].rearrange("(m p) n -> p m n", m=MC))
                load(wo[:, :, :], w["Wo"].rearrange("(a p) n -> p a n", a=HALF))
                for e in range(NE):
                    load(w1e[:, :, e, :], w["ffn_w1"][e].rearrange("(a p) n -> p a n", a=HALF))
                load(w2e[:, :, :], w["ffn_w2"].rearrange("e p n -> p e n"))
                load(b2g[:, :], w["mlp_b2"].partition_broadcast(P))
                load(anchors[:, :, :].rearrange("p e d -> p (e d)"), w["ffn_anchors"].rearrange("e d -> (e d)").partition_broadcast(P))
                load(rclip[:, :], w["ffn_routing_temp"].partition_broadcast(P))
                load(itemp[:, :], w["gate_log_temp"].partition_broadcast(P))
                for half in range(2):
                    load(onw[half * DH:(half + 1) * DH, :], w["o_norm_w"].unsqueeze(1))
                with nc.allow_non_contiguous_dma(reason="a few columns, once"):
                    load(b1g[:, :], w["mlp_b1"].rearrange("(m p) -> p m", m=MC))
                    for a in range(HALF):
                        load(router[:, a, :], w["ffn_proj_w"][:, a * P:(a + 1) * P].rearrange("e p -> p e"))
                sp.wait_ge(loaded, 16 * 20)

            @block.scalar
            def _(act):
                act.wait_ge(loaded, 16 * 20)
                act.activation(s12[:, 0:NH], itemp[:, :], ACT.Abs).then_inc(setup_act, 1)
                act.wait_ge(setup_act, 1)
                act.activation(r12[:, 0:NH], s12[:, 0:NH], ACT.Exp, scale=-1.0).then_inc(setup_act, 1)
                act.wait_ge(setup, 1)
                act.activation(r12[:, NH:2 * NH], m12[:, 0:NH], ACT.Ln).then_inc(setup_act, 1)

            @block.vector
            def _(dve):
                dve.wait_ge(setup_act, 2)
                dve.tensor_scalar(m12[:, 0:NH], r12[:, 0:NH], 1.0, None, ALU.add).then_inc(setup, 1)
                dve.tensor_scalar(m12[:, NH:2 * NH], itemp[:, :], 0.0, 1e-4, ALU.max, ALU.add).then_inc(setup, 1)
                dve.wait_ge(setup_act, 3)
                dve.wait_ge(setup, 2)
                dve.tensor_tensor(s12[:, 0:NH], m12[:, NH:2 * NH], r12[:, NH:2 * NH], ALU.add).then_inc(setup, 1)
                dve.wait_ge(setup, 3)
                dve.reciprocal(itemp[:, :], s12[:, 0:NH]).then_inc(setup, 1)
                dve.tensor_scalar(bv[:, 0:1], rclip[:, :], 0.1, None, ALU.max).then_inc(setup, 1)
                dve.wait_ge(setup, 5)
                dve.reciprocal(rclip[:, :], bv[:, 0:1]).then_inc(setup, 1)
                dve.memset(TL[:, :, :], 0.0).then_inc(setup, 1)
                dve.memset(UF[:, :, :], 0.0).then_inc(setup, 1)
                dve.memset(before_e[:, :, :], 0.0).then_inc(setup, 1)
                dve.wait_ge(setup, 9)
                for e in range(1, NE):
                    dve.memset(before_e[:, e, 0:e], 1.0).then_inc(setup, 1)
                dve.tensor_scalar(wo[:, :, :].rearrange("p a n -> p (a n)"), wo[:, :, :].rearrange("p a n -> p (a n)"),
                                  onw[:, 0:1], None, ALU.mult).then_inc(setup, 1)
                dve.memset(minus_half[:, :], -0.5).then_inc(setup, 1)
                dve.wait_ge(setup, 16)

        with nc.Block() as block:
            @block.sync
            def _(sp):
                sysv = dram["systems"].rearrange("(n m q) j i -> n q j m i", m=NM, q=NQ)

                def load_u(n):
                    for q in range(NQ):
                        sp.dma_start(UF[q * SC:(q + 1) * SC, :, q * SC:(q + 1) * SC], sysv[n, q]).then_inc(uf_loaded.sem, 16)

                def load_a(n, s):
                    sp.dma_start(pa[s][:, :], dram["packa"][n]).then_inc(pa_loaded[s].sem, 16)

                def load_fl(n, s):
                    sp.dma_start(fl[s][:, :], dram["fl"][n]).then_inc(fl_loaded[s].sem, 16)

                def load_b(n, s):
                    sp.dma_start(pb[s][:, :], dram["packb"][n]).then_inc(pb_loaded[s].sem, 16)

                def store(e, s):
                    sp.wait_ge(*acc_done.now(e))
                    sp.dma_start(out[e].rearrange("(b p) n -> p b n", b=BLK), HA[s][:, :, :]).then_inc(out_stored.sem, 16)

                def body(it, s, stores=True):
                    n = it + 2
                    sp.wait_ge(*vw_ready.now(it))
                    load_a(n, s)
                    sp.wait_ge(*mix_step.now(it, 2))
                    load_fl(n, s)
                    sp.wait_ge(*w_ready.now(it + 1))
                    load_u(n)
                    sp.wait_ge(*h2_ready.now(it))
                    load_b(n, s)
                    if stores:
                        store(it - 1, 1 - s)

                load_a(0, 0)
                load_u(0)
                for s in range(2):
                    load_b(s, s)
                    load_fl(s, s)
                load_a(1, 1)
                sp.wait_ge(*w_ready.now(0))
                load_u(1)
                body(0, 0, False)
                with sp.Fori(0, NB // 2 - 2) as i:
                    body(2 * i + 1, 1)
                    body(2 * i + 2, 0)
                body(NB - 3, 1)
                store(NB - 3, 1)
                store(NB - 2, 0)
                store(NB - 1, 1)
                sp.wait_ge(*out_stored.before(NB))

            @block.tensor
            def _(pe):
                def head_rows(h):
                    return slice((h % 2) * DH, (h % 2 + 1) * DH)

                def products(n, s, k):
                    kT = chans(pa[s], KT)
                    qkb = pa[s][:, QT:QT + 2 * HALF * T].rearrange("p (f a t) -> p f a t", f=2, a=HALF)
                    if k < 2:
                        pe.wait_ge(*d_ready.before(n))
                    else:
                        pe.wait_ge(*masked.now(n, k - 1))
                    rows = slice((k % 2) * DH, (k % 2 + 1) * DH)
                    for j in range(2):
                        e = k // 2 * 2 + j
                        b, hh = e // 2, e % 2
                        mm = pe.matmul(bank[k % 2][:, j * 2 * P:(j + 1) * 2 * P],
                                       kT[rows, hh, b * P:(b + 1) * P], qkb[rows, :, hh, b * P:(b + 1) * P], start=True, stop=True)
                    mm.then_inc(qk_ready.sem, 1)

                def merge_a(n):
                    pe.wait_ge(loaded, 1)
                    pe.wait_ge(*tdiag_ready.now(n))
                    for m in range(NM):
                        for f in (0, 2 * SC):
                            mm = pe.matmul(bank[f // DH][f + SC:f + 2 * SC, m * SC:(m + 1) * SC],
                                           ATM[f:f + SC, m, P + f + SC:P + f + 2 * SC], TL[f:f + SC, m, 0:SC],
                                           start=True, stop=True, skip_group_check=True)
                    mm.then_inc(p1_ready.sem, 1)

                def merge_b(n):
                    pe.wait_ge(loaded, 1)
                    pe.wait_ge(*p1_copied.now(n))
                    for m in range(NM):
                        for f in (0, 2 * SC):
                            u22 = UF[f + SC:f + 2 * SC, m, f + SC:f + 2 * SC]
                            mm = pe.matmul(bank[f // DH][f:f + SC, m * SC:(m + 1) * SC],
                                           P1[f + SC:f + 2 * SC, m, :], u22, start=True, stop=True, skip_group_check=True)
                            if f == 0:
                                mm = pe.matmul(bank[0][SC:2 * SC, m * SC:(m + 1) * SC], u22, P1[SC:2 * SC, m, :],
                                               start=True, stop=True, skip_group_check=True)
                    mm.then_inc(u12_ready.sem, 1)

                def merge_c(n):
                    pe.wait_ge(loaded, 1)
                    pe.wait_ge(*u12_copied.now(n))
                    for m in range(NM):
                        mm = pe.matmul(bank[m // 6][DH:P, (m % 6) * DH:(m % 6 + 1) * DH],
                                       ATM[0:DH, m, P + DH:2 * P], TL[0:DH, m, :], start=True, stop=True, skip_group_check=True)
                    mm.then_inc(p1b_ready.sem, 1)

                def merge_d(n):
                    pe.wait_ge(loaded, 1)
                    pe.wait_ge(*p1b_copied.now(n))
                    for m in range(NM):
                        mm = pe.matmul(bank[m // 6][0:DH, (m % 6) * DH:(m % 6 + 1) * DH],
                                       P1B[DH:P, m, :], UF[DH:P, m, DH:P], start=True, stop=True, skip_group_check=True)
                    mm.then_inc(u12b_ready.sem, 1)

                def kb_state(n, s, b):
                    kbT = chans(pa[s], KBT)
                    cols = slice(b * P, (b + 1) * P)
                    pe.wait_ge(*s_copied.now(n, b))
                    pe.wait_ge(*d_ready.now(n, b))
                    for h in range(NH):
                        mm = pe.matmul(bank[h % 2][:, (h // 2) * DH:(h // 2 + 1) * DH],
                                       kbT[head_rows(h), h // 2, cols], S[head_rows(h), h // 2, :], start=True, stop=True)
                    mm.then_inc(r_ready.sem, 1)

                def q_state(n, s, b):
                    qT = chans(pa[s], QT)
                    cols = slice(b * P, (b + 1) * P)
                    pe.wait_ge(*r_copied.now(n, b))
                    for h in range(NH):
                        pe.matmul(bank[h % 2][:, P + (h // 2) * DH:P + (h // 2 + 1) * DH],
                                  qT[head_rows(h), h // 2, cols], S[head_rows(h), h // 2, :],
                                  start=(h < 2), stop=False, skip_group_check=True)

                def updates(n, b, e=None, k=None):
                    if b == 0:
                        pe.wait_ge(*u12b_copied.now(n))
                    if k is not None:
                        pe.wait_ge(*acc_done.now(e, BLK * k))
                    for h in range(NH):
                        mm = pe.matmul(bank[2][:, h * DH:(h + 1) * DH], UF[:, even_heads_first(b, h), :],
                                       R[:, h, :] if b else VB[:, h, :], start=True, stop=True)
                    mm.then_inc(w_ready.sem, 1)

                def state_update(n, s, b, e=None, k=None):
                    ktok = toks(pa[s], KTOK)
                    if k is not None:
                        pe.wait_ge(*he_ready.now(e, k + 1))
                    pe.wait_ge(*w_copied.now(n, b + 1))
                    for h in range(NH):
                        mm = pe.matmul(bank[6][head_rows(h), T + (h // 2) * DH:T + (h // 2 + 1) * DH],
                                       ktok[:, b, h * DH:(h + 1) * DH], W[:, h, :], start=True, stop=True)
                    mm.then_inc(s_ready.sem, 1)

                def outputs(n, b):
                    if b == 0:
                        pe.wait_ge(*u12b_copied.now(n))
                    pe.wait_ge(*w_copied.now(n, b + 1))
                    for h in range(NH):
                        mm = pe.matmul(bank[h % 2][:, P + (h // 2) * DH:P + (h // 2 + 1) * DH],
                                       ATM[:, even_heads_first(b, h), 0:P], W[:, h, :],
                                       start=(b == 0 and h < 2), stop=True, skip_group_check=True)
                    mm.then_inc(o_ready.sem, 1)

                def transpose_stats(it):
                    pe.wait_ge(*std_ready.now(it))
                    pe.wait_ge(*q_ready.before(it))
                    for b in range(BLK):
                        mm = pe.transpose(bank[3][0:GATE_S, b * P:(b + 1) * P],
                                          SG[:, b, :, :, :].rearrange("p r m h -> p (r m h)"), ident[:, :])
                    mm.then_inc(sgT_ready.sem, 1)

                def gate_x(s, m):
                    for a in range(HALF):
                        pe.matmul(mlp_bank[m][:, 0:T], w1g[:, a, m * P:(m + 1) * P], chans(pb[s], XNT)[:, a, :], start=(a == 0), stop=False)

                def gate_s(m):
                    pe.matmul(mlp_bank[m][:, 0:T], w1s[:, m * P:(m + 1) * P], SGT[:, :], start=False, stop=True)\
                        .then_inc(mlp_ready.sem, 1)

                def gate_out(it):
                    pe.wait_ge(*g1_ready.now(it))
                    for b in range(BLK):
                        for m in range(MC):
                            mm = pe.matmul(bank[5][:, b * 4 * NH:(b + 1) * 4 * NH], GH[:, m, b * P:(b + 1) * P], w2g[:, m, :],
                                           start=(m == 0), stop=(m == MC - 1))
                    mm.then_inc(logits_ready.sem, 1)

                def transpose_mixture(it, s):
                    pe.wait_ge(*on_ready.now(it))
                    for a in range(HALF):
                        for b in range(BLK):
                            m = b * NH + a * 2
                            mm = pe.transpose(bank[3 + a][:, b * P:(b + 1) * P],
                                              DL[s][:, m:m + 2, :].rearrange("p m d -> p (m d)"), ident[:, :])
                        mm.then_inc(onT_ready.sem, 1)

                def project_out(it):
                    pe.wait_ge(*onT0_copied.now(it))
                    pe.wait_ge(*onT1_copied.now(it))
                    for b in range(BLK):
                        for a in range(HALF):
                            mm = pe.matmul((bank[5], bank[3])[b // 2][:, (b % 2) * D:(b % 2 + 1) * D], ONT[:, a, b * P:(b + 1) * P],
                                           wo[:, a, :], start=(a == 0), stop=(a == HALF - 1))
                    mm.then_inc(wo_ready.sem, 1)

                def transpose_y(e):
                    pe.wait_ge(*y_ready.now(e))
                    for a in range(HALF):
                        for b in range(BLK):
                            mm = pe.transpose(bank[4 + a][:, b * P:(b + 1) * P],
                                              y[:, b * D + a * P:b * D + (a + 1) * P], ident[:, :])
                        mm.then_inc(yT_ready.sem, 1)

                def route(e):
                    pe.wait_ge(*yT0_copied.now(e))
                    pe.wait_ge(*yT1_copied.now(e))
                    for b in range(BLK):
                        for a in range(HALF):
                            mm = pe.matmul(bank[3][:, b * NE:(b + 1) * NE], YT[:, a, b * P:(b + 1) * P], router[:, a, :],
                                           start=(a == 0), stop=(a == HALF - 1))
                    mm.then_inc(z_ready.sem, 1)

                def hidden(e, k, n=None, b=None):
                    if b is not None:
                        pe.wait_ge(*s_copied.now(n, b + 1))
                    if k:
                        pe.wait_ge(*he_ready.now(e, k))
                    else:
                        pe.wait_ge(*he_ready.before(e))
                    for a in range(HALF):
                        mm = pe.matmul(bank[6][:, 0:T], w1e[:, a, k, :], YT[:, a, :], start=(a == 0), stop=(a == HALF - 1))
                    mm.then_inc(hid_ready.sem, 1)

                def expert_out(e, k, n=None, b=None):
                    if b is not None:
                        pe.wait_ge(*w_copied.now(n, b + 1))
                    pe.wait_ge(*he_ready.now(e, k + 1))
                    if k:
                        pe.wait_ge(*acc_done.now(e, BLK * k))
                    else:
                        pe.wait_ge(*acc_done.before(e))
                    for b in range(BLK):
                        mm = pe.matmul(expert_bank(b), HE[k % 2][:, b * P:(b + 1) * P], w2e[:, k, :], start=True, stop=True)
                    mm.then_inc(eo_ready.sem, 1)

                def body(n=None, it=None, e=None, s=0, npair=None, ipair=None):
                    o = 1 - s
                    if n is not None:
                        pe.wait_ge(*pa_loaded[o].now(npair))
                        products(n, o, 0)
                        products(n, o, 1)
                    if e is not None:
                        transpose_y(e)
                    if n is not None:
                        products(n, o, 2)
                        products(n, o, 3)
                    if e is not None:
                        route(e)
                    if n is not None:
                        products(n, o, 4)
                        pe.wait_ge(*vb_ready.now(n))
                        products(n, o, 5)
                    if e is not None:
                        hidden(e, 0)
                    if it is not None:
                        pe.wait_ge(*pb_loaded[s].now(ipair))
                        gate_x(s, 0)
                        gate_x(s, 1)
                        transpose_stats(it)
                    if n is not None:
                        merge_a(n)
                    if it is not None:
                        pe.wait_ge(*sgT_copied.now(it))
                        gate_s(0)
                        gate_s(1)
                        gate_x(s, 2)
                        gate_s(2)
                    if n is not None:
                        merge_b(n)
                    if it is not None:
                        pe.wait_ge(*g1_ready.now(it, 1))
                        gate_x(s, 3)
                        gate_s(3)
                    if n is not None:
                        merge_c(n)
                        merge_d(n)
                    if it is not None:
                        gate_out(it)
                    have_n, have_e = n is not None, e is not None
                    for b in range(BLK):
                        k = 2 * b
                        if have_n:
                            if have_e and b:
                                updates(n, b, e, k)
                            else:
                                updates(n, b)
                        if have_e:
                            hidden(e, k + 1)
                            if have_n:
                                expert_out(e, k, n, b)
                            else:
                                expert_out(e, k)
                        if b == 2 and it is not None:
                            transpose_mixture(it, s)
                        if have_n:
                            if b < 2 and have_e:
                                state_update(n, o, b, e, k + 1)
                            elif b < 2:
                                state_update(n, o, b)
                            outputs(n, b)
                        if b < 2 and have_n:
                            kb_state(n, o, b + 1)
                        if b == 2 and it is not None:
                            project_out(it)
                        if have_e:
                            if b < 2 and have_n:
                                hidden(e, k + 2, n, b)
                            elif b < 2:
                                hidden(e, k + 2)
                            expert_out(e, k + 1)
                        if b < 2 and have_n:
                            q_state(n, o, b + 1)

                body(n=0, s=1, npair=0)
                body(n=1, it=0, s=0, npair=0, ipair=0)
                with pe.Fori(0, NB // 2 - 1) as i:
                    body(2 * i + 2, 2 * i + 1, 2 * i, 1, i + 1, i)
                    body(2 * i + 3, 2 * i + 2, 2 * i + 1, 0, i + 1, i + 1)
                body(it=NB - 1, e=NB - 2, s=1, ipair=NB // 2 - 1)
                body(e=NB - 1, s=0)

            @block.scalar
            def _(act):
                def copy(dst, src):
                    return act.activation(dst, src, ACT.Copy)

                def blocks(n, rows, width):
                    return bank[n][rows, 0:384].rearrange("p (m c) -> p m c", c=width)

                def copy_update(n, b):
                    act.wait_ge(*w_ready.now(n, b + 1))
                    if b == 0:
                        act.wait_ge(*o_ready.before(n))
                    else:
                        act.wait_ge(*o_ready.now(n, b))
                    copy(W[:, :, :].rearrange("p h d -> p (h d)"), bank[2][:, 0:D]).then_inc(w_copied.sem, 1)

                def gelu_gate(it, m):
                    act.wait_ge(*mlp_ready.now(it, m + 1))
                    act.activation(GH[:, m, :], mlp_bank[m][:, 0:T], ACT.Gelu, bias=b1g[:, m:m + 1]).then_inc(g1_ready.sem, 1)

                def gelu_expert(e, k):
                    act.wait_ge(*hid_ready.now(e, k + 1))
                    if k >= 2:
                        act.wait_ge(*eo_ready.now(e, k - 1))
                    else:
                        act.wait_ge(*eo_ready.before(e))
                    act.activation(HE[k % 2][:, :], bank[6][:, 0:T], ACT.Gelu_apprx_tanh).then_inc(he_ready.sem, 1)

                def body(n=None, it=None, e=None, s=0):
                    if e is not None:
                        act.wait_ge(*yT_ready.now(e, 1))
                        act.wait_ge(*hid_ready.before(e))
                        copy(YT[:, 0, :], bank[4][:, 0:T]).then_inc(yT0_copied.sem, 1)
                    if it is not None:
                        act.wait_ge(*vmax_ready.now(it))
                        act.activation(SG[:, :, :, 1, :].rearrange("p b r h -> p r b h"),
                                       st1[:, :, :].rearrange("p r (b h) -> p r b h", b=BLK), ACT.Sqrt).then_inc(std_ready.sem, 1)
                    if e is not None:
                        act.wait_ge(*z_ready.now(e))
                        act.activation(qr[:, :, :].rearrange("p b e -> p (b e)"), bank[3][:, 0:BLK * NE], ACT.Tanh, scale=1.0 / 0.3)\
                            .then_inc(q_ready.sem, 1)
                        act.wait_ge(*lr_ready.now(e))
                        act.activation(ex[:, :, :], rank[:, :, :], ACT.Exp).then_inc(er_ready.sem, 1)
                    if it is not None:
                        act.wait_ge(*sgT_ready.now(it))
                        copy(SGT[:, :], bank[3][0:GATE_S, 0:T]).then_inc(sgT_copied.sem, 1)
                    if n is not None:
                        act.wait_ge(*p1_ready.now(n))
                        copy(P1[SC:2 * SC, :, :], blocks(0, slice(SC, 2 * SC), SC))
                        copy(P1[3 * SC:P, :, :], blocks(1, slice(3 * SC, P), SC)).then_inc(p1_copied.sem, 1)
                    if it is not None:
                        gelu_gate(it, 0)
                        gelu_gate(it, 1)
                        gelu_gate(it, 2)
                    if n is not None:
                        act.wait_ge(*u12_ready.now(n))
                        copy(UF[0:SC, :, SC:2 * SC], blocks(0, slice(0, SC), SC))
                        copy(TL[SC:2 * SC, :, 0:SC], blocks(0, slice(SC, 2 * SC), SC))
                        copy(UF[2 * SC:3 * SC, :, 3 * SC:P], blocks(1, slice(2 * SC, 3 * SC), SC)).then_inc(u12_copied.sem, 1)
                    if it is not None:
                        gelu_gate(it, 3)
                    if n is not None:
                        act.wait_ge(*p1b_ready.now(n))
                        copy(P1B[DH:P, 0:6, :], blocks(0, slice(DH, P), DH))
                        copy(P1B[DH:P, 6:NM, :], blocks(1, slice(DH, P), DH)).then_inc(p1b_copied.sem, 1)
                        act.wait_ge(*u12b_ready.now(n))
                        copy(UF[0:DH, 0:6, DH:P], blocks(0, slice(0, DH), DH))
                        copy(UF[0:DH, 6:NM, DH:P], blocks(1, slice(0, DH), DH)).then_inc(u12b_copied.sem, 1)
                    if e is not None:
                        gelu_expert(e, 0)
                    if it is not None:
                        act.wait_ge(*lg_ready.now(it))
                        act.activation(WT[:, :, :], L[:, :, :], ACT.Exp).then_inc(wexp_ready.sem, 1)
                    if n is not None:
                        copy_update(n, 0)
                    if e is not None:
                        gelu_expert(e, 1)
                        gelu_expert(e, 2)
                    if n is not None:
                        copy_update(n, 1)
                    if it is not None:
                        act.wait_ge(*mix_step.now(it))
                        act.activation(ta[:, :], DL[s][:, :, :].rearrange("p m d -> p (m d)"), ACT.Square).then_inc(sq_ready.sem, 1)
                    if e is not None:
                        gelu_expert(e, 3)
                        gelu_expert(e, 4)
                    if n is not None:
                        copy_update(n, 2)
                    if e is not None:
                        gelu_expert(e, 5)
                    if it is not None:
                        act.wait_ge(*onT_ready.now(it, 1))
                        copy(ONT[:, 0, :], bank[3][:, 0:T]).then_inc(onT0_copied.sem, 1)

                body(n=0, s=1)
                body(n=1, it=0, s=0)
                with act.Fori(0, NB // 2 - 1) as i:
                    body(2 * i + 2, 2 * i + 1, 2 * i, 1)
                    body(2 * i + 3, 2 * i + 2, 2 * i + 1, 0)
                body(it=NB - 1, e=NB - 2, s=1)
                body(e=NB - 1, s=0)

            @block.vector
            def _(dve):
                def mask(n, k):
                    e = (k % 2) * (NM // 2) + (k // 2) * 2
                    dve.wait_ge(*qk_ready.now(n, k + 1))
                    dve.tensor_tensor(ATM[:, e:e + 2, :], bank[k % 2][:, :].rearrange("p (m c) -> p m c", m=2),
                                      upper[:, :].unsqueeze(1).broadcast_to([P, 2, 2 * P]), ALU.mult).then_inc(masked.sem, 1)

                def transpose_diagonals(n):
                    dve.wait_ge(*uf_loaded.now(n))
                    dve.wait_ge(*p1b_copied.before(n))
                    dve.transpose(TL[0:SC, :, 0:SC], UF[0:SC, :, 0:SC])
                    dve.transpose(TL[SC:2 * SC, :, SC:2 * SC], UF[SC:2 * SC, :, SC:2 * SC])
                    dve.transpose(TL[2 * SC:3 * SC, :, 0:SC], UF[2 * SC:3 * SC, :, 2 * SC:3 * SC]).then_inc(tdiag_ready.sem, 1)

                def input_stats(n, s, pair):
                    dve.wait_ge(*pb_loaded[s].now(pair))
                    dve.wait_ge(*fl_loaded[s].now(pair))
                    for m in range(NM):
                        dve.bn_stats(ST[:, 0, m, :], heads(pb[s], FSF)[:, m, :])
                        dve.bn_stats(ST[:, 1, m, :], heads(fl[s], 0)[:, m, :])
                        dve.bn_stats(ST[:, 3, m, :], heads(pa[s], VTOK)[:, m, :])

                def remainder(n, b):
                    dve.wait_ge(*r_ready.now(n, b))
                    for odd in range(2):
                        r = dve.tensor_tensor(R[:, odd::2, :], VB[:, b * NH + odd:(b + 1) * NH:2, :],
                                              bank[odd][:, 0:2 * DH].rearrange("p (m d) -> p m d", m=2), ALU.subtract)
                    r.then_inc(r_copied.sem, 1)

                def state(n, b):
                    dve.wait_ge(*s_ready.now(n, b + 1))
                    new = bank[6][:, T:T + 2 * DH].rearrange("p (m d) -> p m d", m=2)
                    if b == 0:
                        dve.tensor_copy(S[:, :, :], new).then_inc(s_copied.sem, 1)
                    else:
                        dve.tensor_tensor(S[:, :, :], S[:, :, :], new, ALU.add).then_inc(s_copied.sem, 1)

                def delta_out(n, s, b):
                    rq = pa[s][:, RQ:RQ + NM].rearrange("p (b h) -> p b h", b=BLK)
                    dve.wait_ge(*o_ready.now(n, b + 1))
                    for odd in range(2):
                        d = dve.tensor_tensor(DL[s][:, b * NH + odd:(b + 1) * NH:2, :],
                                              bank[odd][:, P:P + 2 * DH].rearrange("p (m d) -> p m d", m=2),
                                              rq[:, b, odd::2].unsqueeze(2).broadcast_to([P, 2, DH]), ALU.mult)
                    d.then_inc(d_ready.sem, 1)

                def branch_statistics(n, s):
                    dve.wait_ge(*d_ready.now(n))
                    for m in range(NM):
                        ins = dve.bn_stats(ST[:, 2, m, :], DL[s][:, m, :])
                    ins.then_inc(branch_stats.sem, 1)
                    dve.wait_ge(*branch_stats.now(n))
                    dve.wait_ge(*sgT_ready.before(n))
                    dve.tensor_tensor(st1[:, :, :], ST[:, :, :, 1], ST[:, :, :, 4], ALU.add)
                    dve.tensor_tensor(st2[:, :, :], ST[:, :, :, 1], ST[:, :, :, 4], ALU.subtract)
                    dve.tensor_tensor(st3[:, :, :], ST[:, :, :, 2], ST[:, :, :, 5], ALU.add).then_inc(stat_step.sem, 1)
                    dve.wait_ge(*stat_step.now(n, 1))
                    dve.tensor_scalar(SG[:, :, :, 0, :].rearrange("p b r h -> p r b h"),
                                      st1[:, :, :].rearrange("p r (b h) -> p r b h", b=BLK), 0.5, None, ALU.mult).then_inc(stat_step.sem, 1)
                    dve.tensor_tensor(st4[:, :, :], st2[:, :, :], st2[:, :, :], ALU.mult)
                    dve.tensor_scalar(st3[:, :, :], st3[:, :, :], 1.0 / DH, None, ALU.mult).then_inc(stat_step.sem, 1)
                    dve.wait_ge(*stat_step.now(n, 3))
                    dve.scalar_tensor_tensor(out=st2[:, :, :], in0=st4[:, :, :], scalar=0.25, in1=st3[:, :, :],
                                             op0=ALU.mult, op1=ALU.add).then_inc(stat_step.sem, 1)
                    dve.wait_ge(*stat_step.now(n, 4))
                    dve.tensor_scalar(st1[:, :, :], st2[:, :, :], 1e-6, None, ALU.max).then_inc(vmax_ready.sem, 1)

                def gate_logits(it):
                    dve.wait_ge(*logits_ready.now(it))
                    dve.tensor_tensor(L[:, :, :].rearrange("p (b h) r -> p b (h r)", b=BLK),
                                      bank[5][:, 0:BLK * 4 * NH].rearrange("p (b n) -> p b n", b=BLK),
                                      b2g[:, :].unsqueeze(1).broadcast_to([P, BLK, 4 * NH]), ALU.add).then_inc(gate_step.sem, 1)
                    dve.wait_ge(*gate_step.now(it, 1))
                    lv = L[:, :, :].rearrange("p (b h) r -> p b h r", b=BLK)
                    dve.tensor_tensor(lv, lv, itemp[:, :].unsqueeze(1).unsqueeze(3).broadcast_to([P, BLK, NH, 4]), ALU.mult)\
                        .then_inc(gate_step.sem, 1)
                    dve.wait_ge(*gate_step.now(it, 2))
                    dve.tensor_reduce(m12[:, :], L[:, :, :], AX.X, ALU.max).then_inc(gate_step.sem, 1)
                    dve.wait_ge(*gate_step.now(it, 3))
                    dve.tensor_tensor(L[:, :, :], L[:, :, :], m12[:, :].unsqueeze(2).broadcast_to([P, NM, 4]), ALU.subtract)\
                        .then_inc(lg_ready.sem, 1)

                def gate_weights(it):
                    dve.wait_ge(*wexp_ready.now(it))
                    dve.tensor_reduce(s12[:, :], WT[:, :, :], AX.X, ALU.add).then_inc(wt_step.sem, 1)
                    dve.wait_ge(*wt_step.now(it, 1))
                    dve.reciprocal(r12[:, :], s12[:, :]).then_inc(wt_step.sem, 1)
                    dve.wait_ge(*wt_step.now(it, 2))
                    dve.tensor_tensor(WT[:, :, :], WT[:, :, :], r12[:, :].unsqueeze(2).broadcast_to([P, NM, 4]), ALU.mult)\
                        .then_inc(wt_step.sem, 1)

                def mix_own(it, s):
                    dve.wait_ge(*wt_step.now(it, 3))
                    dve.tensor_tensor(DL[s][:, :, :], DL[s][:, :, :], WT[:, :, 2:3].broadcast_to([P, NM, DH]), ALU.mult)\
                        .then_inc(mix_step.sem, 1)
                    dve.tensor_tensor(tc_[:, :, :], heads(fl[s], 0), WT[:, :, 1:2].broadcast_to([P, NM, DH]), ALU.mult)\
                        .then_inc(mix_step.sem, 1)

                def mix_add(it, s, step, other):
                    dve.wait_ge(*mix_step.now(it, step))
                    dve.tensor_tensor(DL[s][:, :, :], DL[s][:, :, :], other, ALU.add).then_inc(mix_step.sem, 1)

                def mean_squares(it):
                    dve.wait_ge(*sq_ready.now(it))
                    dve.tensor_reduce(s12[:, :], ta[:, :].rearrange("p (m d) -> p m d", d=DH), AX.X, ALU.add).then_inc(ss_ready.sem, 1)
                    dve.wait_ge(*ss_ready.now(it))
                    dve.tensor_scalar(m12[:, :], s12[:, :], 1.0 / DH, 1e-5, ALU.mult, ALU.add).then_inc(ms_ready.sem, 1)

                def normed_mixture(it, s):
                    dve.wait_ge(*rr_ready.now(it))
                    dve.tensor_tensor(DL[s][:, :, :], DL[s][:, :, :], r12[:, :].unsqueeze(2).broadcast_to([P, NM, DH]), ALU.mult)\
                        .then_inc(on_ready.sem, 1)

                def residual(it, s):
                    hf = field(pb[s], HF)
                    ha = HA[s][:, :, :].rearrange("p b n -> p (b n)")
                    dve.wait_ge(*wo_ready.now(it))
                    dve.wait_ge(*out_stored.before(it, 2))
                    dve.tensor_tensor(ha[:, 0:2 * D], hf[:, 0:2 * D], bank[5][:, :], ALU.add)
                    dve.tensor_tensor(ha[:, 2 * D:], hf[:, 2 * D:], bank[3][:, 0:D], ALU.add).then_inc(h2_ready.sem, 1)
                    dve.wait_ge(*h2_ready.now(it))
                    for b in range(BLK):
                        ins = dve.bn_stats(bst[:, b, :], HA[s][:, b, :])
                    ins.then_inc(bst_ready.sem, 1)
                    dve.wait_ge(setup, 1)
                    dve.wait_ge(*bst_ready.now(it))
                    for b in range(BLK):
                        ins = dve.bn_aggr(bmv[:, b, :], bst[:, b, :])
                    ins.then_inc(bmv_ready.sem, 1)
                    dve.wait_ge(*bmv_ready.now(it))
                    dve.tensor_scalar(bv[:, :], bmv[:, :, 1], 1e-5, None, ALU.add).then_inc(veps_ready.sem, 1)

                def second_norm(e, s):
                    dve.wait_ge(*rstd_ready.now(e))
                    for b in range(BLK):
                        dve.tensor_scalar(y[:, b * D:(b + 1) * D], HA[s][:, b, :], bmv[:, b, 0:1], br[:, b:b + 1],
                                          ALU.subtract, ALU.mult).then_inc(y_ready.sem, 1)

                def routing_logits(e):
                    dve.wait_ge(*q_ready.now(e))
                    dve.tensor_tensor(cmp[:, :, :, :], qr[:, :, :].unsqueeze(2).broadcast_to([P, BLK, NE, ND]),
                                      anchors[:, :, :].unsqueeze(1).broadcast_to([P, BLK, NE, ND]), ALU.mult).then_inc(route_step.sem, 1)
                    dve.wait_ge(*route_step.now(e, 1))
                    dve.tensor_reduce(lg[:, :, :], cmp[:, :, :, :], AX.X, ALU.add).then_inc(route_step.sem, 1)
                    dve.wait_ge(*route_step.now(e, 2))
                    dve.tensor_scalar(we[:, :, :], lg[:, :, :], -float(ND), 0.5, ALU.add, ALU.mult).then_inc(route_step.sem, 1)
                    dve.wait_ge(*route_step.now(e, 3))
                    dve.tensor_scalar(lg[:, :, :], we[:, :, :], rclip[:, 0:1], None, ALU.mult).then_inc(route_step.sem, 1)
                    dve.wait_ge(*route_step.now(e, 4))
                    other = lg[:, :, :].unsqueeze(2).broadcast_to([P, BLK, NE, NE])
                    own = lg[:, :, :].unsqueeze(3).broadcast_to([P, BLK, NE, NE])
                    dve.tensor_tensor(cmp[:, :, :, :], other, own, ALU.is_gt)
                    dve.tensor_tensor(eqs[:, :, :, :], other, own, ALU.is_equal)
                    dve.tensor_reduce(me[:, :], lg[:, :, :], AX.X, ALU.max).then_inc(route_step.sem, 1)
                    dve.wait_ge(*route_step.now(e, 5))
                    dve.tensor_tensor(eqs[:, :, :, :], eqs[:, :, :, :], before_e[:, :, :].unsqueeze(1).broadcast_to([P, BLK, NE, NE]), ALU.mult)\
                        .then_inc(route_step.sem, 1)
                    dve.tensor_tensor(rank[:, :, :], lg[:, :, :], me[:, :].unsqueeze(2).broadcast_to([P, BLK, NE]), ALU.subtract)\
                        .then_inc(lr_ready.sem, 1)
                    dve.wait_ge(*route_step.now(e, 6))
                    dve.tensor_tensor(cmp[:, :, :, :], cmp[:, :, :, :], eqs[:, :, :, :], ALU.add).then_inc(route_step.sem, 1)
                    dve.wait_ge(*route_step.now(e, 7))
                    dve.tensor_reduce(we[:, :, :], cmp[:, :, :, :], AX.X, ALU.add).then_inc(route_step.sem, 1)
                    dve.wait_ge(*route_step.now(e, 8))
                    dve.tensor_scalar(lg[:, :, :], we[:, :, :], 1.5, None, ALU.is_lt).then_inc(route_step.sem, 1)

                def routing_weights(e):
                    dve.wait_ge(*er_ready.now(e))
                    dve.wait_ge(*route_step.now(e, 9))
                    dve.tensor_tensor(ex[:, :, :], ex[:, :, :], lg[:, :, :], ALU.mult).then_inc(we_step.sem, 1)
                    dve.wait_ge(*we_step.now(e, 1))
                    dve.tensor_reduce(se[:, :], ex[:, :, :], AX.X, ALU.add).then_inc(we_step.sem, 1)
                    dve.wait_ge(*we_step.now(e, 2))
                    dve.reciprocal(re[:, :], se[:, :]).then_inc(we_step.sem, 1)
                    dve.wait_ge(*we_step.now(e, 3))
                    dve.tensor_tensor(we[:, :, :], ex[:, :, :], re[:, :].unsqueeze(2).broadcast_to([P, BLK, NE]), ALU.mult)\
                        .then_inc(we_step.sem, 1)

                def add_expert(e, s, k):
                    if k == 0:
                        dve.wait_ge(*we_step.now(e, 4))
                    dve.wait_ge(*eo_ready.now(e, k + 1))
                    for b in range(BLK):
                        if k:
                            dve.wait_ge(*acc_done.now(e, BLK * (k - 1) + b + 1))
                        dve.scalar_tensor_tensor(out=HA[s][:, b, :], in0=expert_bank(b),
                                                 scalar=we[:, b, k:k + 1], in1=HA[s][:, b, :], op0=ALU.mult, op1=ALU.add)\
                            .then_inc(acc_done.sem, 1)

                def body(n=None, it=None, e=None, s=0, npair=None):
                    o = 1 - s
                    if n is not None:
                        mask(n, 0)
                        mask(n, 1)
                    if e is not None:
                        second_norm(e, o)
                    if n is not None:
                        mask(n, 2)
                    if e is not None:
                        dve.wait_ge(*yT_ready.now(e, 2))
                        dve.tensor_copy(YT[:, 1, :], bank[5][:, 0:T]).then_inc(yT1_copied.sem, 1)
                    if n is not None:
                        mask(n, 3)
                        mask(n, 4)
                        mask(n, 5)
                    if e is not None:
                        routing_logits(e)
                    if n is not None:
                        transpose_diagonals(n)
                    if e is not None:
                        routing_weights(e)
                    if n is not None:
                        input_stats(n, o, npair)
                    if it is not None:
                        gate_logits(it)
                    if it is not None:
                        gate_weights(it)
                        mix_own(it, s)
                    if e is not None:
                        add_expert(e, o, 0)
                    if n is not None:
                        state(n, 0)
                        delta_out(n, o, 0)
                        remainder(n, 1)
                    if it is not None:
                        mix_add(it, s, 2, tc_[:, :, :])
                    if e is not None:
                        add_expert(e, o, 1)
                    if it is not None:
                        dve.wait_ge(*fsw_ready.now(it))
                        mix_add(it, s, 3, ta[:, :].rearrange("p (m d) -> p m d", d=DH))
                        dve.wait_ge(*vw_ready.now(it))
                        mix_add(it, s, 4, tb[:, :].rearrange("p (m d) -> p m d", d=DH))
                    if e is not None:
                        add_expert(e, o, 2)
                    if n is not None:
                        state(n, 1)
                        delta_out(n, o, 1)
                        remainder(n, 2)
                    if it is not None:
                        mean_squares(it)
                    if e is not None:
                        add_expert(e, o, 3)
                    if it is not None:
                        normed_mixture(it, s)
                    if e is not None:
                        add_expert(e, o, 4)
                    if it is not None:
                        dve.wait_ge(*onT_ready.now(it, 2))
                        dve.tensor_copy(ONT[:, 1, :], bank[4][:, 0:T]).then_inc(onT1_copied.sem, 1)
                    if n is not None:
                        delta_out(n, o, 2)
                    if it is not None:
                        residual(it, s)
                    if e is not None:
                        add_expert(e, o, 5)
                    if n is not None:
                        branch_statistics(n, o)

                body(n=0, s=1, npair=0)
                body(n=1, it=0, s=0, npair=0)
                with dve.Fori(0, NB // 2 - 1) as i:
                    body(2 * i + 2, 2 * i + 1, 2 * i, 1, i + 1)
                    body(2 * i + 3, 2 * i + 2, 2 * i + 1, 0, i + 1)
                body(it=NB - 1, e=NB - 2, s=1)
                body(e=NB - 1, s=0)

            @block.gpsimd
            def _(pool):
                def body(n=None, it=None, e=None, s=0, npair=None):
                    o = 1 - s
                    if e is not None:
                        pool.wait_ge(*veps_ready.now(e))
                        pool.tensor_tensor(br[:, :], bv[:, :], minus_half[:, 0:BLK], ALU.pow).then_inc(rstd_ready.sem, 1)
                    if n is not None:
                        pool.wait_ge(*pa_loaded[o].now(npair))
                        pool.wait_ge(*r_copied.before(n))
                        pool.tensor_tensor(VB[:, :, :], heads(pa[o], VTOK),
                                           pa[o][:, VBS:VBS + NM].unsqueeze(2).broadcast_to([P, NM, DH]), ALU.mult)\
                            .then_inc(vb_ready.sem, 1)
                    if it is not None:
                        pool.wait_ge(*wt_step.now(it))
                        pool.tensor_tensor(ta[:, :].rearrange("p (m d) -> p m d", d=DH), heads(pb[s], FSF),
                                           WT[:, :, 0:1].broadcast_to([P, NM, DH]), ALU.mult).then_inc(fsw_ready.sem, 1)
                        pool.tensor_tensor(tb[:, :].rearrange("p (m d) -> p m d", d=DH), heads(pa[s], VTOK),
                                           WT[:, :, 3:4].broadcast_to([P, NM, DH]), ALU.mult).then_inc(vw_ready.sem, 1)
                        pool.wait_ge(*ms_ready.now(it))
                        pool.tensor_tensor(r12[:, :], m12[:, :], minus_half[:, :], ALU.pow).then_inc(rr_ready.sem, 1)

                body(n=0, s=1, npair=0)
                body(n=1, it=0, s=0, npair=0)
                with pool.Fori(0, NB // 2 - 1) as i:
                    body(2 * i + 2, 2 * i + 1, 2 * i, 1, i + 1)
                    body(2 * i + 3, 2 * i + 2, 2 * i + 1, 0, i + 1)
                body(it=NB - 1, e=NB - 2, s=1)
                body(e=NB - 1, s=0)


_ATTN = ["Wq", "Wk", "Wv", "Wb", "conv_q_w", "conv_k_w", "conv_v_w", "fir_short_w", "fir_long_w", "mlp_w1", "mlp_b1",
         "mlp_w2", "mlp_b2", "gate_log_temp", "o_norm_w", "Wo"]
_FFN = ["proj_w", "anchors", "routing_temp", "w1", "w2"]


def kernel(**inputs):
    import numpy as _np
    import concourse.bacc as _bacc
    from concourse import mybir as _mybir
    from concourse.bass_utils import run_bass_kernel_spmd as _run

    nc = _bacc.Bacc("TRN2", target_bir_lowering=False, num_devices=1)
    arrays = {}

    def give(name):
        a = _np.ascontiguousarray(inputs[name])
        a = a.reshape(1) if a.ndim == 0 else a
        arrays[f"in_{name}_dram"] = a
        return nc.dram_tensor(f"in_{name}_dram", a.shape, _mybir.dt.from_np(a.dtype), kind="ExternalInput").ap()

    x = give("x")
    w = {n: give(f"L0_attn_{n}") for n in _ATTN}
    w |= {f"ffn_{n}": give(f"L0_ffn_{n}") for n in _FFN}
    out = nc.dram_tensor("out_0_dram", (x.shape[0], T, D), F32, kind="ExternalOutput").ap()
    audio_tower(nc, x, w, out)
    r = _run(nc, [arrays], core_ids=[0])
    return r.results[0]["out_0_dram"]
```

```python
from contextlib import ExitStack

import concourse.bass as bass
from concourse import mybir

F32 = mybir.dt.float32
ALU = mybir.AluOpType
ACT = mybir.ActivationFunctionType
AX = mybir.AxisListType

P = 128
D = 256
HALF = D // P
SEG, STEP = 256, 2
BLK = 3
T = BLK * P
NH, DH = 4, 64
NM = BLK * NH
CK, FS, FL = 4, 3, 63
MC = 2 * D // P
TW = P + FL - 1
GATE_S = 8 * NH
MLP = 2 * D
NE, DE, ND = 6, 128, 6
SC = 32
NQ = P // SC

QT, KBT, KT, KTOK, VTOK = (n * HALF * T for n in range(5))
RQ = 5 * HALF * T
VBS = RQ + NM
AW = VBS + NM
HF, XNT, FSF = (n * HALF * T for n in range(3))
BW = 3 * HALF * T


class Signal:

    def __init__(self, sem, per, primed=1):
        self.sem, self.per, self.primed = sem, per, primed

    def now(self, it, k=None):
        return self.sem, (it + self.primed) * self.per + (self.per if k is None else k)

    def before(self, it, back=1):
        return self.sem, (it + (self.primed - back + 1)) * self.per


def even_heads_first(blk, h):
    return (h % 2) * (NM // 2) + blk * (NH // 2) + h // 2


def audio_tower(nc, x, w, out):
    NB = x.shape[0]
    NSYS = NB * NM * NQ // P
    with ExitStack() as ctx:
        def sem(name):
            return ctx.enter_context(nc.semaphore(name))

        def banks():
            return [c.enter_context(nc.psum_tensor(f"bank{n}", [P, 512], F32)) for n in range(8)]

        signals = []

        def signal(name, per=1, primed=1):
            signals.append(Signal(sem(name), per, primed))
            return signals[-1]

        dram = {
            "packa": nc.dram_tensor("packa", [NB, P, AW], F32, kind="Internal").ap(),
            "packb": nc.dram_tensor("packb", [NB, P, BW], F32, kind="Internal").ap(),
            "systems": nc.dram_tensor("systems", [NB * NM * NQ, SC, SC], F32, kind="Internal").ap(),
            "fl": nc.dram_tensor("fl", [NB, P, BLK * D], F32, kind="Internal").ap(),
            "taps": nc.dram_tensor("taps", [D, 512], F32, kind="Internal").ap(),
            "toeplitz": nc.dram_tensor("toeplitz", [P, D, TW], F32, kind="Internal").ap(),
        }
        c = ctx
        bank = banks()

        def sb(name, shape):
            return ctx.enter_context(nc.sbuf_tensor(name, shape, F32))

        ident = sb("ident", [P, P])
        upper = sb("upper", [P, 2 * P])
        expanded = ctx.enter_context(nc.semaphore("expanded"))
        shared = dict(expanded=expanded, NB=NB, NSYS=NSYS, dram=dram, bank=bank, ident=ident, upper=upper)
        make_constants(nc, ctx, ident, upper)
        with nc.sbuf_tensor("v_all", [P, D, BLK * NB], F32) as v_all:
            first_phase(nc, x, w, shared, v_all)
            second_phase(nc, shared, v_all)
        third_phase(nc, w, out, shared, third_phase_weights(nc, ctx))


def make_constants(nc, ctx, ident, upper):
    made = ctx.enter_context(nc.semaphore("made"))
    with nc.Block() as block:
        @block.gpsimd
        def _(pool):
            pool.memset(ident[:, :], 0.0).then_inc(made, 1)
            pool.memset(upper[:, 0:P], 1.0).then_inc(made, 1)
            pool.memset(upper[:, P:], -1.0).then_inc(made, 1)
            pool.wait_ge(made, 3)
            pool.affine_select(out=ident[:, :], in_=ident[:, :], compare_op=ALU.not_equal, fill=1.0,
                               base=0, pattern=[[-1, P]], channel_multiplier=1).then_inc(made, 1)
            pool.affine_select(out=upper[:, 0:P], in_=upper[:, 0:P], compare_op=ALU.is_ge, fill=0.0,
                               base=0, pattern=[[1, P]], channel_multiplier=-1).then_inc(made, 1)
            pool.affine_select(out=upper[:, P:], in_=upper[:, P:], compare_op=ALU.is_gt, fill=0.0,
                               base=0, pattern=[[1, P]], channel_multiplier=-1).then_inc(made, 1)
            pool.wait_ge(made, 6)


def prime(nc, signals):
    with nc.Block() as block:
        @block.sync
        def _(sp):
            for g in signals:
                sp.sem_inc(g.sem, g.per * g.primed)


def first_phase(nc, x, w, shared, v_all):
    NB, dram, bank, ident, upper, expanded = (shared[k] for k in ("NB", "dram", "bank", "ident", "upper", "expanded"))
    with ExitStack() as c:
        def sb(name, shape):
            return c.enter_context(nc.sbuf_tensor(name, shape, F32))

        signals = []

        def signal(name, per=1, primed=1):
            signals.append(Signal(c.enter_context(nc.semaphore(name)), per, primed))
            return signals[-1]

        loaded = c.enter_context(nc.semaphore("p1_weights"))
        setup = c.enter_context(nc.semaphore("p1_setup"))
        started = c.enter_context(nc.semaphore("p1_started"))
        wqkv = sb("wqkv", [P, HALF, 3 * D])
        HV = 3 * NH
        wb = sb("wb", [P, HALF, HV])
        convw = sb("convw", [P, 3 * HALF, CK])
        firw = sb("firw", [P, HALF, FS])
        flw = sb("flw", [P, HALF, FL])
        flr = sb("flr", [P, HALF, 512])
        headsel = sb("headsel", [P, 2 * HALF, HV])
        HVT = sb("HVT", [HV, T])
        hvk = sb("hvk", [P, BLK, HV])
        xs = [sb(f"x{s}", [P, BLK, D]) for s in range(2)]
        pa = [sb(f"pa{s}", [P, AW]) for s in range(2)]
        pb = [sb(f"pb{s}", [P, 2 * HALF * T]) for s in range(2)]
        fsk = sb("fsk", [P, HALF * T])
        xT = sb("xT", [P, BLK, HALF, P])
        E = sb("E", [P, BLK, P])
        PT = sb("PT", [P, BLK, P])
        xn = sb("xn", [P, BLK, D])
        Y = sb("Y", [P, 3 * HALF, T])
        VT = sb("VT", [P, HALF, T])
        SQ = sb("SQ", [P, 2 * HALF, T])
        fsT = sb("fsT", [P, HALF, T])
        KB = sb("KB", [P, BLK, D])
        AT = sb("AT", [P, NM, P])
        mx, negmax, rs, rinv, veps, rstd = (sb(f"s{n}", [P, BLK]) for n in range(6))
        minus_half = sb("minus_half", [P, 2 * NM])
        st = sb("st", [P, BLK, 6])
        mv = sb("mv", [P, BLK, 2])
        eb, b1, kbs = (sb(f"t{n}", [P, NM]) for n in range(3))
        beta = sb("beta", [P, NM])
        RS = sb("RS", [P, 2 * NM])
        RR = sb("RR", [P, BLK, 2, NH])

        def field(buf, at):
            return buf[:, at:at + HALF * T]

        def chans(buf, at):
            return field(buf, at).rearrange("p (a t) -> p a t", a=HALF)

        def toks(buf, at):
            return field(buf, at).rearrange("p (b c) -> p b c", b=BLK)

        x_loaded = [signal(f"x_loaded{s}", 32) for s in range(2)]
        pack_stored = [signal(f"pack_stored{s}", 16) for s in range(2)]
        h_stored = [signal(f"h_stored{s}", 16) for s in range(2)]
        fs_stored = signal("fs_stored", 16)
        at_stored = signal("at_stored", 16 * NQ)
        xT_ready = signal("xT_ready", 2)
        scores_ready = signal("scores_ready")
        probsT_ready = signal("probsT_ready")
        attn_ready = signal("attn_ready", 1, primed=2)
        xnT_ready = signal("xnT_ready", 2)
        hv_ready = signal("hv_ready")
        hv_copied = signal("hv_copied")
        hvk_ready = signal("hvk_ready")
        proj_ready = signal("proj_ready", 6)
        ssq_ready = signal("ssq_ready")
        ktok_ready = signal("ktok_ready")
        vtok_ready = signal("vtok_ready")
        fs_ready = signal("fs_ready")
        kbT_ready = signal("kbT_ready", 2)
        at_ready = signal("at_ready", 4)
        xT01_copied = signal("xT01_copied")
        xT2_copied = signal("xT2_copied")
        max_found = signal("max_found")
        negmax_ready = signal("negmax_ready")
        probs_ready = signal("probs_ready", BLK)
        rinv_ready = signal("rinv_ready")
        probsT_copied = signal("probsT_copied")
        h_ready = signal("h_ready", BLK)
        stats_done = signal("stats_done", BLK)
        mv_ready = signal("mv_ready", BLK)
        rstd_ready = signal("rstd_ready")
        xn_ready = signal("xn_ready", BLK)
        xnT0_copied = signal("xnT0_copied")
        xnT1_copied = signal("xnT1_copied")
        eb_ready = signal("eb_ready")
        beta_step = signal("beta_step", 2)
        tap_done = signal("tap_done", 6)
        conv_step = signal("conv_step", 18)
        silu_done = signal("silu_done", 6)
        sq_ready = signal("sq_ready", 2)
        rs_ready = signal("rs_ready")
        veps_ready = signal("veps_ready")
        rr_ready = signal("rr_ready")
        vbs_ready = signal("vbs_ready")
        scales_ready = signal("scales_ready")
        ktok_copied = signal("ktok_copied")
        vtok_copied = signal("vtok_copied")
        fir_step = signal("fir_step", 6)
        fs_copied = signal("fs_copied")
        kb_ready = signal("kb_ready")
        kbT0_copied = signal("kbT0_copied")
        kbT1_copied = signal("kbT1_copied")
        at_copied = signal("at_copied", 4)
        v_kept = signal("v_kept")
        prime(nc, signals)

        proj_bank = [bank[n] for n in (3, 4, 5, 3, 4, 5)]
        attn_bank = (bank[0], bank[2])

        with nc.Block() as block:
            @block.vector
            def _(dve):
                dve.memset(wb[:, :, :], 0.0).then_inc(started, 1)
                dve.memset(headsel[:, :, :], 0.0).then_inc(started, 1)
                dve.wait_ge(started, 2)
                for n in range(2 * HALF):
                    for head in range(2):
                        dve.memset(headsel[head * DH:(head + 1) * DH, n, 2 * n + head:2 * n + head + 1], 1.0).then_inc(started, 1)
                dve.memset(minus_half[:, :], -0.5).then_inc(started, 1)
                dve.wait_ge(started, 11)

            @block.sync
            def _(sp):
                for n, name in enumerate(("Wq", "Wk", "Wv")):
                    sp.dma_start(wqkv[:, :, n * D:(n + 1) * D],
                                 w[name].rearrange("(a p) n -> p a n", a=HALF)).then_inc(loaded, 16)
                    sp.dma_start(convw[:, n * HALF:(n + 1) * HALF, :],
                                 w[f"conv_{name[1]}_w"].rearrange("(a p) k -> p a k", a=HALF)).then_inc(loaded, 16)
                sp.wait_ge(started, 2)
                sp.dma_start(wb[:, :, 2 * NH:], w["Wb"].rearrange("(a p) n -> p a n", a=HALF)).then_inc(loaded, 16)
                sp.dma_start(firw[:, :, :], w["fir_short_w"].rearrange("(a g) v k -> (g v) a k", a=HALF)).then_inc(loaded, 16)
                sp.dma_start(flw[:, :, :], w["fir_long_w"].rearrange("(a g) v k -> (g v) a k", a=HALF)).then_inc(loaded, 16)
                sp.wait_ge(loaded, 16 * 9)
                sp.wait_ge(setup, 5)
                sp.dma_start(dram["taps"].rearrange("(a p) n -> p a n", a=HALF), flr[:, :, :]).then_inc(loaded, 16)
                sp.wait_ge(loaded, 16 * 10)

            @block.gpsimd
            def _(pool):
                pool.memset(flr[:, :, :], 0.0).then_inc(setup, 1)
                pool.memset(xs[0][:, BLK - 1, :], 0.0).then_inc(setup, 1)
                pool.memset(xs[1][:, BLK - 1, :], 0.0).then_inc(setup, 1)
                pool.wait_ge(loaded, 16 * 9)
                pool.wait_ge(setup, 3)
                for a in range(HALF):
                    pool.tensor_copy(flr[:, a, P - 1:P - 1 + FL], flw[:, a, ::-1]).then_inc(setup, 1)
                pool.wait_ge(setup, 5)

        with nc.Block() as block:
            @block.sync
            def _(sp):
                def load_x(n, s):
                    sp.wait_ge(*attn_ready.before(n, 2))
                    sp.dma_start(xs[s][:, 0:2, :], x[n, 0:2 * SEG, :].rearrange(
                        "(b p two) n -> p b two n", b=2, two=STEP)[:, :, 0, :]).then_inc(x_loaded[s].sem, 16)
                    rows = (x.shape[1] - 2 * SEG) // STEP
                    sp.dma_start(xs[s][0:rows, 2, :], x[n, 2 * SEG:2 * SEG + rows * STEP, :].rearrange(
                        "(p two) n -> p two n", two=STEP)[:, 0, :]).then_inc(x_loaded[s].sem, 16)

                def store_fs(c):
                    sp.wait_ge(*fs_copied.now(c))
                    sp.dma_start(dram["packb"][c][:, FSF:FSF + HALF * T], fsk[:, :]).then_inc(fs_stored.sem, 16)

                def store_h(a, s):
                    sp.wait_ge(*xnT0_copied.now(a))
                    sp.wait_ge(*xnT1_copied.now(a))
                    sp.dma_start(dram["packb"][a][:, 0:2 * HALF * T], pb[s][:, :]).then_inc(h_stored[s].sem, 16)

                def store_pack(c, s):
                    sp.wait_ge(*kbT0_copied.now(c))
                    sp.wait_ge(*kbT1_copied.now(c))
                    sp.dma_start(dram["packa"][c], pa[s][:, :]).then_inc(pack_stored[s].sem, 16)

                def store_systems(c):
                    sp.wait_ge(*at_copied.now(c))
                    sysv = dram["systems"].rearrange("(n m q) j i -> n q j m i", m=NM, q=NQ)
                    for q in range(NQ):
                        sp.dma_start(sysv[c, q], AT[q * SC:(q + 1) * SC, :, q * SC:(q + 1) * SC])\
                            .then_inc(at_stored.sem, 16)

                def expand(c):
                    for k in range(P // NB):
                        p = c * (P // NB) + k
                        sp.dma_start(dram["toeplitz"][p], dram["taps"][:, bass.ds(P - 1 - p, TW)]).then_inc(expanded, 16)

                def body(a=None, c=None, s=0, ahead=True):
                    if a is not None and ahead:
                        load_x(a + 1, 1 - s)
                    if c is not None:
                        expand(c)
                        store_pack(c, s)
                        store_fs(c)
                    if a is not None:
                        store_h(a, s)
                    if c is not None:
                        store_systems(c)

                load_x(0, 0)
                body(a=0, s=0)
                body(a=1, s=1)
                with sp.Fori(0, NB // 2 - 2) as i:
                    body(2 * i + 2, 2 * i, 0)
                    body(2 * i + 3, 2 * i + 1, 1)
                body(NB - 2, NB - 4, 0)
                body(NB - 1, NB - 3, 1, ahead=False)
                body(c=NB - 2, s=0)
                body(c=NB - 1, s=1)
                for s in range(2):
                    sp.wait_ge(*pack_stored[s].before(NB // 2))
                    sp.wait_ge(*h_stored[s].before(NB // 2))
                sp.wait_ge(*fs_stored.before(NB))
                sp.wait_ge(*at_stored.before(NB))

            @block.tensor
            def _(pe):
                def transpose_x(n, s, pair):
                    pe.wait_ge(*x_loaded[s].now(pair))
                    pe.wait_ge(*xnT0_copied.before(n))
                    pe.wait_ge(*xnT1_copied.before(n))
                    for b in range(BLK):
                        for a in range(HALF):
                            o = (b % 2) * D + a * P
                            mm = pe.transpose(bank[b // 2][:, o:o + P], xs[s][:, b, a * P:(a + 1) * P], ident[:, :])
                        if b:
                            mm.then_inc(xT_ready.sem, 1)

                def scores(n):
                    pe.wait_ge(*xT01_copied.now(n))
                    pe.wait_ge(*xT2_copied.now(n))
                    pe.wait_ge(*h_ready.before(n))
                    for b in range(BLK):
                        for a in range(HALF):
                            mm = pe.matmul(bank[2][:, b * P:(b + 1) * P], xT[:, b, a, :], xT[:, b, a, :],
                                           start=(a == 0), stop=(a == HALF - 1))
                    mm.then_inc(scores_ready.sem, 1)

                def transpose_probs(n):
                    pe.wait_ge(*probs_ready.now(n))
                    for b in range(BLK):
                        mm = pe.transpose(bank[1][:, b * P:(b + 1) * P], E[:, b, :], ident[:, :])
                    mm.then_inc(probsT_ready.sem, 1)

                def attend(n, s):
                    pe.wait_ge(*probsT_copied.now(n))
                    for b in range(BLK):
                        mm = pe.matmul(attn_bank[b // 2][:, (b % 2) * D:(b % 2 + 1) * D], PT[:, b, :], xs[s][:, b, :],
                                       start=True, stop=True)
                    mm.then_inc(attn_ready.sem, 1)

                def transpose_normed(n):
                    pe.wait_ge(*xn_ready.now(n))
                    for a in range(HALF):
                        for b in range(BLK):
                            mm = pe.transpose(bank[1 - a][:, b * P:(b + 1) * P], xn[:, b, a * P:(a + 1) * P], ident[:, :])
                        mm.then_inc(xnT_ready.sem, 1)

                def project(it, s, j):
                    xnT = chans(pb[s], XNT)
                    if j == 0:
                        pe.wait_ge(*xnT0_copied.now(it))
                        pe.wait_ge(*xnT1_copied.now(it))
                    if j < 3:
                        pe.wait_ge(*conv_step.now(it - 1, (12, 17, 18)[j]))
                    else:
                        pe.wait_ge(*conv_step.now(it, (5, 6, 11)[j - 3]))
                    for a in range(HALF):
                        mm = pe.matmul(proj_bank[j][:, 0:T], wqkv[:, a, j * P:(j + 1) * P], xnT[:, a, :],
                                       start=(a == 0), stop=(a == HALF - 1))
                    mm.then_inc(proj_ready.sem, 1)

                def head_values(it, s):
                    pe.wait_ge(*sq_ready.now(it))
                    pe.wait_ge(*at_copied.before(it))
                    pe.wait_ge(*probsT_copied.now(it))
                    for n in range(2 * HALF):
                        pe.matmul(bank[6][0:HV, 0:T], headsel[:, n, :], SQ[:, n, :], start=(n == 0), stop=False)
                    for a in range(HALF):
                        mm = pe.matmul(bank[6][0:HV, 0:T], wb[:, a, :], chans(pb[s], XNT)[:, a, :], start=False, stop=(a == HALF - 1))
                    mm.then_inc(hv_ready.sem, 1)

                def transpose_head_values(it):
                    pe.wait_ge(started, 1)
                    pe.wait_ge(*hv_copied.now(it))
                    for b in range(BLK):
                        mm = pe.transpose(bank[7][:, b * HV:(b + 1) * HV], HVT[:, b * P:(b + 1) * P], ident[0:HV, 0:HV])
                    mm.then_inc(ssq_ready.sem, 1)

                def to_tokens(src):
                    for b in range(BLK):
                        for a in range(HALF):
                            o = (b % 2) * D + a * P
                            mm = pe.transpose(bank[6 + b // 2][:, o:o + P], src[:, a, b * P:(b + 1) * P], ident[:, :])
                    return mm

                def transpose_kb(it):
                    pe.wait_ge(*kb_ready.now(it))
                    pe.wait_ge(*vtok_copied.now(it))
                    for a in range(HALF):
                        for b in range(BLK):
                            mm = pe.transpose(bank[6 + a][:, b * P:(b + 1) * P], KB[:, b, a * P:(a + 1) * P], ident[:, :])
                        mm.then_inc(kbT_ready.sem, 1)

                def k_kb(it, s, part):
                    kT, kbT = chans(pa[s], KT), chans(pa[s], KBT)
                    for odd in range(2):
                        if part:
                            pe.wait_ge(*at_copied.now(it, odd + 1))
                        elif odd == 0:
                            pe.wait_ge(*fs_copied.now(it))
                        rows = slice(odd * DH, (odd + 1) * DH)
                        for b in (range(2), (2,))[part]:
                            for hh in range(NH // 2):
                                e = b * (NH // 2) + hh
                                mm = pe.matmul(bank[6 + odd][:, (e % 4) * P:(e % 4 + 1) * P],
                                               kT[rows, hh, b * P:(b + 1) * P], kbT[rows, hh, b * P:(b + 1) * P],
                                               start=True, stop=True)
                        mm.then_inc(at_ready.sem, 1)

                def body(a=None, b=None, c=None, s=0, apair=None):
                    if a is not None:
                        transpose_x(a, s, apair)
                    if c is not None:
                        head_values(c, s)
                    if b is not None:
                        project(b, 1 - s, 0)
                    if c is not None:
                        transpose_head_values(c)
                    if b is not None:
                        project(b, 1 - s, 1)
                    if c is not None:
                        pe.wait_ge(*hvk_ready.now(c))
                        to_tokens(chans(pa[s], KT)).then_inc(ktok_ready.sem, 1)
                    if a is not None:
                        scores(a)
                    if b is not None:
                        project(b, 1 - s, 2)
                    if c is not None:
                        pe.wait_ge(*silu_done.now(c, 6))
                        pe.wait_ge(*ktok_copied.now(c))
                        to_tokens(VT).then_inc(vtok_ready.sem, 1)
                    if b is not None:
                        project(b, 1 - s, 3)
                    if a is not None:
                        transpose_probs(a)
                    if b is not None:
                        project(b, 1 - s, 4)
                    if c is not None:
                        transpose_kb(c)
                    if a is not None:
                        attend(a, s)
                    if b is not None:
                        project(b, 1 - s, 5)
                    if c is not None:
                        pe.wait_ge(*fir_step.now(c))
                        pe.wait_ge(*kbT0_copied.now(c))
                        pe.wait_ge(*kbT1_copied.now(c))
                        to_tokens(fsT).then_inc(fs_ready.sem, 1)
                        k_kb(c, s, 0)
                        k_kb(c, s, 1)
                    if a is not None:
                        transpose_normed(a)

                body(a=0, s=0, apair=0)
                body(a=1, b=0, s=1, apair=0)
                with pe.Fori(0, NB // 2 - 1) as i:
                    body(2 * i + 2, 2 * i + 1, 2 * i, 0, i + 1)
                    body(2 * i + 3, 2 * i + 2, 2 * i + 1, 1, i + 1)
                body(b=NB - 1, c=NB - 2, s=0)
                body(c=NB - 1, s=1)

            @block.scalar
            def _(act):
                def copy(dst, src):
                    return act.activation(dst, src, ACT.Copy)

                def copy_xT(n):
                    act.wait_ge(*xT_ready.now(n, 1))
                    copy(xT[:, 0:2, :, :].rearrange("p b a t -> p (b a t)"), bank[0][:, :]).then_inc(xT01_copied.sem, 1)

                def exp_scores(n):
                    act.wait_ge(*negmax_ready.now(n))
                    for b in range(BLK):
                        act.activation(E[:, b, :], bank[2][:, b * P:(b + 1) * P], ACT.Exp, bias=negmax[:, b:b + 1],
                                       scale=float(D) ** -0.5, accum_out=rs[:, b:b + 1]).then_inc(probs_ready.sem, 1)

                def copy_probsT(n):
                    act.wait_ge(*probsT_ready.now(n))
                    copy(PT[:, :, :].rearrange("p b t -> p (b t)"), bank[1][:, 0:T]).then_inc(probsT_copied.sem, 1)

                def divide_attn(n, s, pair):
                    H = toks(pb[s], HF)
                    act.wait_ge(*attn_ready.now(n))
                    act.wait_ge(*rinv_ready.now(n))
                    act.wait_ge(*h_stored[s].before(pair))
                    for b in range(BLK):
                        act.activation(H[:, b, :], attn_bank[b // 2][:, (b % 2) * D:(b % 2 + 1) * D], ACT.Copy,
                                       scale=rinv[:, b:b + 1]).then_inc(h_ready.sem, 1)

                def copy_xnT(n, s):
                    act.wait_ge(*xnT_ready.now(n, 1))
                    copy(chans(pb[s], XNT)[:, 0, :], bank[1][:, 0:T]).then_inc(xnT0_copied.sem, 1)

                def exp_beta(n):
                    act.wait_ge(*hvk_ready.now(n))
                    act.wait_ge(*beta_step.before(n))
                    act.activation(eb[:, :].rearrange("p (b h) -> p b h", b=BLK),
                                   hvk[:, :, 2 * NH:],
                                   ACT.Exp, scale=-1.0).then_inc(eb_ready.sem, 1)

                def last_tap(it, j):
                    act.wait_ge(*proj_ready.now(it, j + 1))
                    act.activation(Y[:, j, :], proj_bank[j][:, 0:T], ACT.Copy, scale=convw[:, j, CK - 1:CK])\
                        .then_inc(tap_done.sem, 1)

                def silu(it, s, j):
                    dst = (chans(pa[s], QT), chans(pa[s], KT), VT)[j // 2]
                    act.wait_ge(*conv_step.now(it, 6 * (j // 2) + 5 + j % 2))
                    if j == 4:
                        act.wait_ge(*fir_step.before(it))
                        act.wait_ge(*vtok_ready.before(it))
                    act.activation(dst[:, j % 2, :], Y[:, j, :], ACT.Silu).then_inc(silu_done.sem, 1)

                def body(a=None, b=None, c=None, s=0, apair=None, bpair=None):
                    if a is not None:
                        copy_xT(a)
                    if c is not None:
                        act.wait_ge(*hv_ready.now(c))
                        copy(HVT[:, :], bank[6][0:HV, 0:T]).then_inc(hv_copied.sem, 1)
                    if b is not None:
                        last_tap(b, 0)
                        last_tap(b, 1)
                    if c is not None:
                        exp_beta(c)
                        act.wait_ge(*ktok_ready.now(c))
                        copy(field(pa[s], KTOK)[:, 0:2 * D], bank[6][:, :])
                        copy(field(pa[s], KTOK)[:, 2 * D:], bank[7][:, 0:D]).then_inc(ktok_copied.sem, 1)
                    if a is not None:
                        exp_scores(a)
                    if b is not None:
                        last_tap(b, 2)
                        last_tap(b, 3)
                    if a is not None:
                        copy_probsT(a)
                    if b is not None:
                        last_tap(b, 4)
                    if c is not None:
                        act.wait_ge(*kbT_ready.now(c, 1))
                        copy(chans(pa[s], KBT)[:, 0, :], bank[6][:, 0:T]).then_inc(kbT0_copied.sem, 1)
                    if a is not None:
                        divide_attn(a, s, apair)
                    if b is not None:
                        last_tap(b, 5)
                    if c is not None:
                        act.wait_ge(*fs_ready.now(c))
                        act.wait_ge(*fs_stored.before(c))
                        copy(fsk[:, 0:2 * D], bank[6][:, :])
                        copy(fsk[:, 2 * D:], bank[7][:, 0:D]).then_inc(fs_copied.sem, 1)
                    if b is not None:
                        act.wait_ge(*pack_stored[1 - s].before(bpair))
                        for j in range(4):
                            silu(b, 1 - s, j)
                        act.wait_ge(*silu_done.now(b, 4))
                        act.wait_ge(*ssq_ready.before(b))
                        for f in range(2):
                            act.activation(SQ[:, 2 * f:2 * f + 2, :].rearrange("p a t -> p (a t)"),
                                           field(pa[1 - s], (QT, KT)[f]), ACT.Square).then_inc(sq_ready.sem, 1)
                    if a is not None:
                        copy_xnT(a, s)
                    if b is not None:
                        silu(b, 1 - s, 4)
                        silu(b, 1 - s, 5)

                body(a=0, s=0, apair=0)
                body(a=1, b=0, s=1, apair=0, bpair=0)
                with act.Fori(0, NB // 2 - 1) as i:
                    body(2 * i + 2, 2 * i + 1, 2 * i, 0, i + 1, i)
                    body(2 * i + 3, 2 * i + 2, 2 * i + 1, 1, i + 1, i + 1)
                body(b=NB - 1, c=NB - 2, s=0, bpair=NB // 2 - 1)
                body(c=NB - 1, s=1)

            @block.vector
            def _(dve):
                def copy_xT(n):
                    dve.wait_ge(*xT_ready.now(n, 2))
                    dve.tensor_copy(xT[:, 2, :, :].rearrange("p a t -> p (a t)"), bank[1][:, 0:D]).then_inc(xT2_copied.sem, 1)

                def find_max(n):
                    dve.wait_ge(*scores_ready.now(n))
                    dve.tensor_reduce(mx[:, :], bank[2][:, 0:T].rearrange("p (b t) -> p b t", b=BLK), AX.X, ALU.max)\
                        .then_inc(max_found.sem, 1)
                    dve.wait_ge(*max_found.now(n))
                    dve.tensor_scalar(negmax[:, :], mx[:, :], -float(D) ** -0.5, None, ALU.mult).then_inc(negmax_ready.sem, 1)

                def invert_sums(n):
                    dve.wait_ge(*probs_ready.now(n))
                    dve.reciprocal(rinv[:, :], rs[:, :]).then_inc(rinv_ready.sem, 1)

                def norm_stats(n, s):
                    H = toks(pb[s], HF)
                    for b in range(BLK):
                        dve.wait_ge(*h_ready.now(n, b + 1))
                        dve.bn_stats(st[:, b, :], H[:, b, :]).then_inc(stats_done.sem, 1)
                    dve.wait_ge(started, 1)
                    dve.wait_ge(*stats_done.now(n))
                    for b in range(BLK):
                        dve.bn_aggr(mv[:, b, :], st[:, b, :]).then_inc(mv_ready.sem, 1)
                    dve.wait_ge(*mv_ready.now(n))
                    dve.tensor_scalar(veps[:, :], mv[:, :, 1], 1e-5, None, ALU.add).then_inc(veps_ready.sem, 1)

                def normalise(n, s):
                    H = toks(pb[s], HF)
                    dve.wait_ge(*rstd_ready.now(n))
                    for b in range(BLK):
                        dve.tensor_scalar(xn[:, b, :], H[:, b, :], mv[:, b, 0:1], rstd[:, b:b + 1],
                                          ALU.subtract, ALU.mult).then_inc(xn_ready.sem, 1)

                def copy_xnT(n, s):
                    dve.wait_ge(*xnT_ready.now(n, 2))
                    dve.tensor_copy(chans(pb[s], XNT)[:, 1, :], bank[0][:, 0:T]).then_inc(xnT1_copied.sem, 1)

                def finish_beta(n):
                    dve.wait_ge(*eb_ready.now(n))
                    dve.tensor_scalar(b1[:, :], eb[:, :], 1.0, None, ALU.add).then_inc(beta_step.sem, 1)
                    dve.wait_ge(*beta_step.now(n, 1))
                    dve.reciprocal(beta[:, :], b1[:, :]).then_inc(beta_step.sem, 1)

                def other_taps(it, n, lags=range(1, CK)):
                    for lag in lags:
                        for a in range(HALF):
                            j = 2 * n + a
                            if lag == 1:
                                dve.wait_ge(*tap_done.now(it, j + 1))
                            else:
                                dve.wait_ge(*conv_step.now(it, 6 * n + 2 * (lag - 2) + a + 1))
                            dve.scalar_tensor_tensor(out=Y[:, j, lag:T], in0=proj_bank[j][:, 0:T - lag],
                                                     scalar=convw[:, j, CK - 1 - lag:CK - lag], in1=Y[:, j, lag:T],
                                                     op0=ALU.mult, op1=ALU.add).then_inc(conv_step.sem, 1)

                def scales(it, s):
                    dve.wait_ge(*rr_ready.now(it))
                    dve.wait_ge(*beta_step.now(it, 2))
                    vbs = pa[s][:, VBS:VBS + NM]
                    dve.tensor_tensor(vbs.rearrange("p (b h) -> p b h", b=BLK),
                                      beta[:, :].rearrange("p (b h) -> p b h", b=BLK), RR[:, :, 1, :], ALU.mult)\
                        .then_inc(vbs_ready.sem, 1)
                    dve.tensor_copy(pa[s][:, RQ:RQ + NM].rearrange("p (b h) -> p b h", b=BLK), RR[:, :, 0, :])
                    dve.wait_ge(*vbs_ready.now(it))
                    dve.tensor_tensor(kbs[:, :].rearrange("p (b h) -> p b h", b=BLK),
                                      vbs.rearrange("p (b h) -> p b h", b=BLK), RR[:, :, 1, :], ALU.mult)\
                        .then_inc(scales_ready.sem, 1)

                def short_fir(it):
                    dve.wait_ge(*silu_done.now(it, 6))
                    dve.wait_ge(*fs_ready.before(it))
                    for a in range(HALF):
                        dve.tensor_scalar(fsT[:, a, :], VT[:, a, :], firw[:, a, FS - 1:FS], None, ALU.mult).then_inc(fir_step.sem, 1)
                    for lag in range(1, FS):
                        for a in range(HALF):
                            dve.wait_ge(*fir_step.now(it, 2 * (lag - 1) + a + 1))
                            dve.scalar_tensor_tensor(out=fsT[:, a, lag:T], in0=VT[:, a, 0:T - lag],
                                                     scalar=firw[:, a, FS - 1 - lag:FS - lag], in1=fsT[:, a, lag:T],
                                                     op0=ALU.mult, op1=ALU.add).then_inc(fir_step.sem, 1)

                def mask_a(it, part):
                    if part == 0:
                        dve.wait_ge(*at_stored.before(it))
                    m = (4, 2)[part]
                    for odd in range(2):
                        dve.wait_ge(*at_ready.now(it, 2 * part + odd + 1))
                        o = odd * NM // 2 + part * 4
                        dve.tensor_tensor(AT[:, o:o + m, :], bank[6 + odd][:, 0:m * P].rearrange("p (m t) -> p m t", m=m),
                                          upper[:, P:].unsqueeze(1).broadcast_to([P, m, P]), ALU.mult).then_inc(at_copied.sem, 1)

                def body(a=None, b=None, c=None, s=0):
                    if a is not None:
                        copy_xT(a)
                    if c is not None:
                        short_fir(c)
                        dve.wait_ge(*ssq_ready.now(c))
                        dve.tensor_copy(hvk[:, :, :].rearrange("p b v -> p (b v)"), bank[7][:, 0:BLK * HV]).then_inc(hvk_ready.sem, 1)
                        dve.wait_ge(*hvk_ready.now(c))
                        dve.tensor_scalar(RS[:, :].rearrange("p (b v) -> p b v", b=BLK), hvk[:, :, 0:2 * NH], 1e-6, None,
                                          ALU.add).then_inc(rs_ready.sem, 1)
                    if b is not None:
                        other_taps(b, 0)
                    if a is not None:
                        find_max(a)
                    if c is not None:
                        dve.wait_ge(*vtok_ready.now(c))
                        dve.tensor_copy(field(pa[s], VTOK)[:, 0:2 * D], bank[6][:, :])
                        dve.tensor_copy(field(pa[s], VTOK)[:, 2 * D:], bank[7][:, 0:D]).then_inc(vtok_copied.sem, 1)
                        finish_beta(c)
                        scales(c, s)
                    if a is not None:
                        invert_sums(a)
                    if b is not None:
                        other_taps(b, 1)
                    if c is not None:
                        dve.wait_ge(*kbT_ready.now(c, 2))
                        dve.tensor_copy(chans(pa[s], KBT)[:, 1, :], bank[7][:, 0:T]).then_inc(kbT1_copied.sem, 1)
                    if a is not None:
                        norm_stats(a, s)
                    if b is not None:
                        other_taps(b, 2, (1,))
                    if c is not None:
                        mask_a(c, 0)
                    if a is not None:
                        normalise(a, s)
                    if c is not None:
                        mask_a(c, 1)
                    if a is not None:
                        copy_xnT(a, s)
                    if b is not None:
                        other_taps(b, 2, (2, 3))

                body(a=0, s=0)
                body(a=1, b=0, s=1)
                with dve.Fori(0, NB // 2 - 1) as i:
                    body(2 * i + 2, 2 * i + 1, 2 * i, 0)
                    body(2 * i + 3, 2 * i + 2, 2 * i + 1, 1)
                body(b=NB - 1, c=NB - 2, s=0)
                body(c=NB - 1, s=1)

            @block.gpsimd
            def _(pool):
                def inverse_std(n):
                    pool.wait_ge(*veps_ready.now(n))
                    pool.tensor_tensor(rstd[:, :], veps[:, :], minus_half[:, 0:BLK], ALU.pow).then_inc(rstd_ready.sem, 1)

                def body(a=None, c=None, s=0):
                    if c is not None:
                        pool.wait_ge(*rs_ready.now(c))
                        pool.tensor_tensor(RR[:, :, :, :].rearrange("p b n h -> p (b n h)"), RS[:, :], minus_half[:, :], ALU.pow)\
                            .then_inc(rr_ready.sem, 1)
                        pool.wait_ge(*scales_ready.now(c))
                        pool.wait_ge(*ktok_copied.now(c))
                        pool.tensor_tensor(KB[:, :, :].rearrange("p b (h d) -> p (b h) d", h=NH),
                                           field(pa[s], KTOK).rearrange("p (m d) -> p m d", d=DH),
                                           kbs[:, :].unsqueeze(2).broadcast_to([P, NM, DH]), ALU.mult).then_inc(kb_ready.sem, 1)
                        pool.wait_ge(*vtok_copied.now(c))
                        for b in range(BLK):
                            keep = pool.tensor_copy(v_all[:, :, c + b * NB], toks(pa[s], VTOK)[:, b, :])
                        keep.then_inc(v_kept.sem, 1)
                    if a is not None:
                        inverse_std(a)

                body(a=0)
                body(a=1)
                with pool.Fori(0, NB // 2 - 1) as i:
                    body(2 * i + 2, 2 * i, 0)
                    body(2 * i + 3, 2 * i + 1, 1)
                body(c=NB - 2, s=0)
                body(c=NB - 1, s=1)


def third_phase_weights(nc, ctx):
    def sb(name, shape):
        return ctx.enter_context(nc.sbuf_tensor(name, shape, F32))

    w1g = sb("w1g", [P, HALF, MLP])
    w1s = sb("w1s", [GATE_S, MLP])
    b1g = sb("b1g", [P, MC])
    w2g = sb("w2g", [P, MC, 4 * NH])
    b2g = sb("b2g", [P, 4 * NH])
    wo = sb("wo", [P, HALF, D])
    onw = sb("onw", [P, 1])
    router = sb("router", [P, HALF, NE])
    anchors = sb("anchors", [P, NE, ND])
    rclip = sb("rclip", [P, 1])
    w1e = sb("w1e", [P, HALF, NE, DE])
    w2e = sb("w2e", [P, NE, D])
    itemp = sb("itemp", [P, NH])
    loaded = ctx.enter_context(nc.semaphore("p3_weights"))
    return dict(w1g=w1g, w1s=w1s, b1g=b1g, w2g=w2g, b2g=b2g, wo=wo, onw=onw, router=router, anchors=anchors,
                rclip=rclip, w1e=w1e, w2e=w2e, itemp=itemp, loaded=loaded)


def load_third_phase_weights(nc, sp, w, tail):
    def load(dst, src):
        sp.dma_start(dst, src).then_inc(tail["loaded"], 16)

    load(tail["w1g"][:, :, :], w["mlp_w1"][0:D].rearrange("(a p) n -> p a n", a=HALF))
    load(tail["w1s"][:, :], w["mlp_w1"][D:])
    load(tail["w2g"][:, :, :], w["mlp_w2"].rearrange("(m p) n -> p m n", m=MC))
    load(tail["wo"][:, :, :], w["Wo"].rearrange("(a p) n -> p a n", a=HALF))
    for e in range(NE):
        load(tail["w1e"][:, :, e, :], w["ffn_w1"][e].rearrange("(a p) n -> p a n", a=HALF))
    load(tail["w2e"][:, :, :], w["ffn_w2"].rearrange("e p n -> p e n"))
    load(tail["b2g"][:, :], w["mlp_b2"].partition_broadcast(P))
    load(tail["anchors"][:, :, :].rearrange("p e d -> p (e d)"), w["ffn_anchors"].rearrange("e d -> (e d)").partition_broadcast(P))
    load(tail["rclip"][:, :], w["ffn_routing_temp"].partition_broadcast(P))
    load(tail["itemp"][:, :], w["gate_log_temp"].partition_broadcast(P))
    for half in range(2):
        load(tail["onw"][half * DH:(half + 1) * DH, :], w["o_norm_w"].unsqueeze(1))
    with nc.allow_non_contiguous_dma(reason="a few columns, once"):
        load(tail["b1g"][:, :], w["mlp_b1"].rearrange("(m p) -> p m", m=MC))
        for a in range(HALF):
            load(tail["router"][:, a, :], w["ffn_proj_w"][:, a * P:(a + 1) * P].rearrange("e p -> p e"))


def second_phase(nc, shared, v_all):
    NB, NSYS, dram, bank, expanded = (shared[k] for k in ("NB", "NSYS", "dram", "bank", "expanded"))
    CG = 8
    SG = 3
    with ExitStack() as c:
        def sb(name, shape):
            return c.enter_context(nc.sbuf_tensor(name, shape, F32))

        signals = []

        def signal(name, per=1, primed=1):
            signals.append(Signal(c.enter_context(nc.semaphore(name)), per, primed))
            return signals[-1]

        toep = [sb(f"toep{s}", [P, CG, TW]) for s in range(2)]
        Xs = [sb(f"X{s}", [P, SG, SC, SC]) for s in range(2)]
        GC = D // 2
        GI = GC // CG
        stage = [sb("stage", [P, BLK * NB, GC]),
                 v_all[:, 0:GC, :].rearrange("p c n -> p (c n)").rearrange("p (n c) -> p n c", c=GC)]
        fl_stored = c.enter_context(nc.semaphore("fl_stored"))
        prod = sb("prod", [P, SG * (SC // 2) * (SC // 2 - 1)])
        toep_loaded = [signal(f"toep_loaded{s}", 16) for s in range(2)]
        fl_ready = signal("fl_ready", 2, primed=2)
        fl_copied = signal("fl_copied", 2, primed=2)
        sys_loaded = [c.enter_context(nc.semaphore(f"sys_loaded{s}")) for s in range(2)]
        sys_stored = c.enter_context(nc.semaphore("sys_stored"))
        solve_step = c.enter_context(nc.semaphore("solve_step"))
        prime(nc, signals)
        systems = dram["systems"].rearrange("(p s) j i -> p s j i", s=NSYS)
        steps = 1 + 2 * (SC - 2)

        with nc.Block() as block:
            @block.sync
            def _(sp):
                sp.wait_ge(expanded, 16 * P)
                with sp.Fori(0, D // CG // 2) as i:
                    for s in range(2):
                        it = i * 2 + s
                        sp.wait_ge(*fl_ready.before(it, 2))
                        sp.dma_start(toep[s][:, :, :], dram["toeplitz"][:, bass.ds(it * CG, CG), :]).then_inc(toep_loaded[s].sem, 16)

            @block.tensor
            def _(pe):
                with pe.Fori(0, D // CG // 2) as i:
                    for s in range(2):
                        it = i * 2 + s
                        pe.wait_ge(*toep_loaded[s].now(i))
                        pe.wait_ge(*fl_copied.before(it, 2))
                        for ch in range(CG):
                            o = (ch % 4) * BLK * NB
                            acc = bank[2 * s + ch // 4]
                            pe.matmul(acc[:, o:o + BLK * NB], toep[s][:, ch, 0:P], v_all[:, it * CG + ch, :],
                                      start=True, stop=False, skip_group_check=True)
                            mm = pe.matmul(acc[0:TW - P, o + NB:o + BLK * NB], toep[s][:, ch, P:], v_all[:, it * CG + ch, 0:(BLK - 1) * NB],
                                           start=False, stop=True, skip_group_check=True)
                            if ch % 4 == 3:
                                mm.then_inc(fl_ready.sem, 1)

            @block.scalar
            def _(act):
                def copy_pairs(g, first, last):
                    with act.Fori(first, last) as j:
                        for s in range(2):
                            it = g * GI + j * 2 + s
                            for half in range(2):
                                act.wait_ge(*fl_ready.now(it, half + 1))
                                act.activation(stage[g][:, :, bass.ds((j * 2 + s) * CG + half * 4, 4)].rearrange("p n c -> p c n"),
                                               bank[2 * s + half][:, 0:4 * BLK * NB].rearrange("p (c n) -> p c n", c=4), ACT.Copy)\
                                    .then_inc(fl_copied.sem, 1)

                def store(g, b):
                    act.dma_start(dram["fl"][:, :, b * D + g * GC:b * D + (g + 1) * GC].rearrange("n p c -> p n c"),
                                  stage[g][:, b * NB:(b + 1) * NB, :]).then_inc(fl_stored, 16)

                copy_pairs(0, 0, GI // 2)
                act.wait_ge(*fl_copied.now(GI - 1))
                for b in range(BLK):
                    store(0, b)
                    copy_pairs(1, b * 2, b * 2 + 2 if b < BLK - 1 else GI // 2)
                act.wait_ge(*fl_copied.now(2 * GI - 1))
                for b in range(BLK):
                    store(1, b)
                act.wait_ge(fl_stored, 16 * BLK * 2)

            @block.gpsimd
            def _(pool):
                groups = NSYS // SG
                for g in range(groups + 1):
                    if g < groups:
                        if g >= 2:
                            pool.wait_ge(sys_stored, 16 * (g - 1))
                        pool.dma_start(Xs[g % 2][:, :, :, :], systems[:, g * SG:(g + 1) * SG]).then_inc(sys_loaded[g % 2], 16)
                    if g:
                        pool.wait_ge(solve_step, steps * g)
                        pool.dma_start(systems[:, (g - 1) * SG:g * SG], Xs[(g - 1) % 2][:, :, :, :]).then_inc(sys_stored, 16)
                pool.wait_ge(sys_stored, 16 * groups)

            @block.vector
            def _(dve):
                for g in range(NSYS // SG):
                    X = Xs[g % 2]
                    done = steps * g + 1
                    dve.wait_ge(sys_loaded[g % 2], 16 * (g // 2 + 1))
                    dve.memset(X[:, :, :, :].rearrange("p s j i -> p s (j i)")[:, :, ::SC + 1], 1.0).then_inc(solve_step, 1)
                    dve.wait_ge(solve_step, done)
                    for j in range(1, SC - 1):
                        n = SC - 1 - j
                        pr = prod[:, 0:SG * j * n].rearrange("p (s j n) -> p s j n", s=SG, j=j)
                        dve.tensor_tensor(pr, X[:, :, 0:j, j:j + 1].broadcast_to([P, SG, j, n]),
                                          X[:, :, j:j + 1, j + 1:].broadcast_to([P, SG, j, n]), ALU.mult).then_inc(solve_step, 1)
                        done += 1
                        dve.wait_ge(solve_step, done)
                        dve.tensor_tensor(X[:, :, 0:j, j + 1:], X[:, :, 0:j, j + 1:], pr, ALU.add).then_inc(solve_step, 1)
                        done += 1
                        dve.wait_ge(solve_step, done)


def third_phase(nc, w, out, shared, tail):
    NB, dram, bank, ident, upper = (shared[k] for k in ("NB", "dram", "bank", "ident", "upper"))
    with ExitStack() as c:
        def sb(name, shape):
            return c.enter_context(nc.sbuf_tensor(name, shape, F32))

        signals = []

        def signal(name, per=1, primed=1):
            signals.append(Signal(c.enter_context(nc.semaphore(name)), per, primed))
            return signals[-1]

        loaded = tail["loaded"]
        setup = c.enter_context(nc.semaphore("p3_setup"))
        setup_act = c.enter_context(nc.semaphore("p3_setup_act"))
        before_e = sb("before_e", [P, NE, NE])
        w1g, w1s, b1g, w2g, b2g, wo, onw, router, anchors, rclip, w1e, w2e, itemp = (
            tail[n] for n in ("w1g", "w1s", "b1g", "w2g", "b2g", "wo", "onw", "router", "anchors", "rclip", "w1e", "w2e", "itemp"))
        pa = [sb(f"qa{s}", [P, AW]) for s in range(2)]
        pb = [sb(f"qb{s}", [P, BW]) for s in range(2)]
        fl = [sb(f"fl{s}", [P, HALF * T]) for s in range(2)]
        ATM = sb("ATM", [P, NM, 2 * P])
        UF = sb("UF", [P, NM, P])
        TL = sb("TL", [P, NM, DH])
        P1 = sb("P1", [P, NM, SC])
        P1B = sb("P1B", [P, NM, DH])
        VB = sb("VB", [P, NM, DH])
        R = sb("R", [P, NH, DH])
        W = sb("W", [P, NH, DH])
        S = sb("S", [P, NH // 2, DH])
        DL = [sb(f"DL{s}", [P, NM, DH]) for s in range(2)]
        HA = [sb(f"HA{s}", [P, BLK, D]) for s in range(2)]
        ta = sb("ta", [P, BLK * D])
        tb = sb("tb", [P, BLK * D])
        tc_ = sb("tc", [P, NM, DH])
        y = sb("y", [P, BLK * D])
        ONT = sb("ONT", [P, HALF, T])
        YT = sb("YT", [P, HALF, T])
        GH = sb("GH", [P, MC, T])
        HE = [sb(f"HE{s}", [P, T]) for s in range(2)]
        minus_half = sb("minus_half_q", [P, NM])
        SGT = sb("SGT", [GATE_S, T])
        ST = sb("ST", [P, 4, NM, 6])
        SG = sb("SG", [P, BLK, 4, 2, NH])
        st1, st2, st3, st4 = (sb(f"st{n}", [P, 4, NM]) for n in range(4))
        L = sb("L", [P, NM, 4])
        WT = sb("WT", [P, NM, 4])
        m12, s12, r12 = (sb(f"m{n}", [P, NM]) for n in range(3))
        bst = sb("bst", [P, BLK, 6])
        bmv = sb("bmv", [P, BLK, 2])
        bv, br = (sb(f"b{n}", [P, BLK]) for n in range(2))
        qr, lg, rank, ex, we = (sb(f"e{n}", [P, BLK, NE]) for n in range(5))
        cmp, eqs = (sb(f"c{n}", [P, BLK, NE, NE]) for n in range(2))
        me, se, re = (sb(f"g{n}", [P, BLK]) for n in range(3))

        def field(buf, at):
            return buf[:, at:at + HALF * T]

        def chans(buf, at):
            return field(buf, at).rearrange("p (a t) -> p a t", a=HALF)

        def toks(buf, at):
            return field(buf, at).rearrange("p (b c) -> p b c", b=BLK)

        def heads(buf, at):
            return field(buf, at).rearrange("p (m d) -> p m d", d=DH)

        mlp_bank = [bank[n] for n in (4, 5, 3, 4)]

        def expert_bank(b):
            return bank[7][:, b * D:(b + 1) * D] if b < 2 else bank[2][:, D:2 * D]

        pa_loaded = [signal(f"pa_loaded{s}", 16) for s in range(2)]
        pb_loaded = [signal(f"pb_loaded{s}", 16) for s in range(2)]
        fl_loaded = [signal(f"fl_loaded{s}", 16) for s in range(2)]
        uf_loaded = signal("uf_loaded", 16 * NQ)
        out_stored = signal("out_stored", 16, primed=2)
        qk_ready = signal("qk_ready", 6)
        masked = signal("masked", 6)
        tdiag_ready = signal("tdiag_ready")
        p1_ready, p1_copied = signal("p1_ready"), signal("p1_copied")
        u12_ready, u12_copied = signal("u12_ready"), signal("u12_copied")
        p1b_ready, p1b_copied = signal("p1b_ready"), signal("p1b_copied")
        u12b_ready, u12b_copied = signal("u12b_ready"), signal("u12b_copied")
        vb_ready = signal("vb_ready")
        r_ready, r_copied = signal("r_ready", 2), signal("r_copied", 2)
        w_ready, w_copied = signal("w_ready", 3), signal("w_copied", 3)
        s_ready, s_copied = signal("s_ready", 2), signal("s_copied", 2)
        o_ready, d_ready = signal("o_ready", 3), signal("d_ready", 3)
        branch_stats = signal("branch_stats")
        stat_step = signal("stat_step", 4)
        vmax_ready = signal("vmax_ready")
        std_ready = signal("std_ready")
        sgT_ready, sgT_copied = signal("sgT_ready"), signal("sgT_copied")
        mlp_ready, g1_ready = signal("mlp_ready", 4), signal("g1_ready", 4)
        logits_ready = signal("logits_ready")
        gate_step = signal("gate_step", 3)
        lg_ready, wexp_ready = signal("lg_ready"), signal("wexp_ready")
        wt_step = signal("wt_step", 3)
        fsw_ready, vw_ready = signal("fsw_ready"), signal("vw_ready")
        mix_step = signal("mix_step", 5)
        sq_ready, ss_ready, ms_ready = signal("q_sq_ready"), signal("ss_ready"), signal("ms_ready")
        rr_ready = signal("q_rr_ready")
        on_ready = signal("on_ready")
        onT_ready, onT0_copied, onT1_copied = signal("onT_ready", 2), signal("onT0_copied"), signal("onT1_copied")
        wo_ready, h2_ready = signal("wo_ready"), signal("h2_ready")
        bst_ready, bmv_ready, veps_ready = signal("bst_ready"), signal("bmv_ready"), signal("q_veps_ready")
        rstd_ready = signal("q_rstd_ready")
        y_ready = signal("y_ready", BLK)
        yT_ready, yT0_copied, yT1_copied = signal("yT_ready", 2), signal("yT0_copied"), signal("yT1_copied")
        z_ready, q_ready = signal("z_ready"), signal("q_ready", primed=2)
        route_step = signal("route_step", 9)
        lr_ready, er_ready = signal("q_lr_ready"), signal("er_ready")
        we_step = signal("we_step", 4)
        hid_ready, he_ready = signal("hid_ready", NE), signal("he_ready", NE)
        eo_ready = signal("eo_ready", NE)
        acc_done = signal("acc_done", NE * BLK)
        prime(nc, signals)

        sysv = dram["systems"].rearrange("(n m q) j i -> n q j m i", m=NM, q=NQ)

        def load_u(sp, n):
            for q in range(NQ):
                sp.dma_start(UF[q * SC:(q + 1) * SC, :, q * SC:(q + 1) * SC], sysv[n, q]).then_inc(uf_loaded.sem, 16)

        def load_a(sp, n, s):
            sp.dma_start(pa[s][:, :], dram["packa"][n]).then_inc(pa_loaded[s].sem, 16)

        def load_fl(sp, n, s):
            sp.dma_start(fl[s][:, :], dram["fl"][n]).then_inc(fl_loaded[s].sem, 16)

        def load_b(sp, n, s):
            sp.dma_start(pb[s][:, :], dram["packb"][n]).then_inc(pb_loaded[s].sem, 16)

        with nc.Block() as block:
            @block.sync
            def _(sp):
                load_third_phase_weights(nc, sp, w, tail)
                load_a(sp, 0, 0)
                sp.wait_ge(setup, 8)
                load_u(sp, 0)
                for s in range(2):
                    load_b(sp, s, s)
                    load_fl(sp, s, s)
                load_a(sp, 1, 1)
                sp.wait_ge(loaded, 16 * 20)

            @block.scalar
            def _(act):
                act.wait_ge(loaded, 16 * 20)
                act.activation(s12[:, 0:NH], itemp[:, :], ACT.Abs).then_inc(setup_act, 1)
                act.wait_ge(setup_act, 1)
                act.activation(r12[:, 0:NH], s12[:, 0:NH], ACT.Exp, scale=-1.0).then_inc(setup_act, 1)
                act.wait_ge(setup, 1)
                act.activation(r12[:, NH:2 * NH], m12[:, 0:NH], ACT.Ln).then_inc(setup_act, 1)

            @block.vector
            def _(dve):
                dve.wait_ge(setup_act, 2)
                dve.tensor_scalar(m12[:, 0:NH], r12[:, 0:NH], 1.0, None, ALU.add).then_inc(setup, 1)
                dve.tensor_scalar(m12[:, NH:2 * NH], itemp[:, :], 0.0, 1e-4, ALU.max, ALU.add).then_inc(setup, 1)
                dve.wait_ge(setup_act, 3)
                dve.wait_ge(setup, 2)
                dve.tensor_tensor(s12[:, 0:NH], m12[:, NH:2 * NH], r12[:, NH:2 * NH], ALU.add).then_inc(setup, 1)
                dve.wait_ge(setup, 3)
                dve.reciprocal(itemp[:, :], s12[:, 0:NH]).then_inc(setup, 1)
                dve.tensor_scalar(bv[:, 0:1], rclip[:, :], 0.1, None, ALU.max).then_inc(setup, 1)
                dve.wait_ge(setup, 5)
                dve.reciprocal(rclip[:, :], bv[:, 0:1]).then_inc(setup, 1)
                dve.memset(TL[:, :, :], 0.0).then_inc(setup, 1)
                dve.memset(UF[:, :, :], 0.0).then_inc(setup, 1)
                dve.memset(before_e[:, :, :], 0.0).then_inc(setup, 1)
                dve.wait_ge(setup, 9)
                for e in range(1, NE):
                    dve.memset(before_e[:, e, 0:e], 1.0).then_inc(setup, 1)
                dve.tensor_scalar(wo[:, :, :].rearrange("p a n -> p (a n)"), wo[:, :, :].rearrange("p a n -> p (a n)"),
                                  onw[:, 0:1], None, ALU.mult).then_inc(setup, 1)
                dve.memset(minus_half[:, :], -0.5).then_inc(setup, 1)
                dve.wait_ge(setup, 16)

        with nc.Block() as block:
            @block.sync
            def _(sp):
                def store(e, s):
                    sp.wait_ge(*acc_done.now(e))
                    sp.dma_start(out[e].rearrange("(b p) n -> p b n", b=BLK), HA[s][:, :, :]).then_inc(out_stored.sem, 16)

                def body(it, s, stores=True):
                    n = it + 2
                    sp.wait_ge(*vw_ready.now(it))
                    load_a(sp, n, s)
                    sp.wait_ge(*mix_step.now(it, 2))
                    load_fl(sp, n, s)
                    sp.wait_ge(*w_ready.now(it + 1))
                    load_u(sp, n)
                    sp.wait_ge(*h2_ready.now(it))
                    load_b(sp, n, s)
                    if stores:
                        store(it - 1, 1 - s)

                sp.wait_ge(*w_ready.now(0))
                load_u(sp, 1)
                body(0, 0, False)
                with sp.Fori(0, NB // 2 - 2) as i:
                    body(2 * i + 1, 1)
                    body(2 * i + 2, 0)
                body(NB - 3, 1)
                store(NB - 3, 1)
                store(NB - 2, 0)
                store(NB - 1, 1)
                sp.wait_ge(*out_stored.before(NB))

            @block.tensor
            def _(pe):
                def head_rows(h):
                    return slice((h % 2) * DH, (h % 2 + 1) * DH)

                def products(n, s, k):
                    kT = chans(pa[s], KT)
                    qkb = pa[s][:, QT:QT + 2 * HALF * T].rearrange("p (f a t) -> p f a t", f=2, a=HALF)
                    if k < 2:
                        pe.wait_ge(*d_ready.before(n))
                    else:
                        pe.wait_ge(*masked.now(n, k - 1))
                    rows = slice((k % 2) * DH, (k % 2 + 1) * DH)
                    for j in range(2):
                        e = k // 2 * 2 + j
                        b, hh = e // 2, e % 2
                        mm = pe.matmul(bank[k % 2][:, j * 2 * P:(j + 1) * 2 * P],
                                       kT[rows, hh, b * P:(b + 1) * P], qkb[rows, :, hh, b * P:(b + 1) * P], start=True, stop=True)
                    mm.then_inc(qk_ready.sem, 1)

                def merge_a(n):
                    pe.wait_ge(loaded, 1)
                    pe.wait_ge(*tdiag_ready.now(n))
                    for m in range(NM):
                        for f in (0, 2 * SC):
                            mm = pe.matmul(bank[f // DH][f + SC:f + 2 * SC, m * SC:(m + 1) * SC],
                                           ATM[f:f + SC, m, P + f + SC:P + f + 2 * SC], TL[f:f + SC, m, 0:SC],
                                           start=True, stop=True, skip_group_check=True)
                    mm.then_inc(p1_ready.sem, 1)

                def merge_b(n):
                    pe.wait_ge(loaded, 1)
                    pe.wait_ge(*p1_copied.now(n))
                    for m in range(NM):
                        for f in (0, 2 * SC):
                            u22 = UF[f + SC:f + 2 * SC, m, f + SC:f + 2 * SC]
                            mm = pe.matmul(bank[f // DH][f:f + SC, m * SC:(m + 1) * SC],
                                           P1[f + SC:f + 2 * SC, m, :], u22, start=True, stop=True, skip_group_check=True)
                            if f == 0:
                                mm = pe.matmul(bank[0][SC:2 * SC, m * SC:(m + 1) * SC], u22, P1[SC:2 * SC, m, :],
                                               start=True, stop=True, skip_group_check=True)
                    mm.then_inc(u12_ready.sem, 1)

                def merge_c(n):
                    pe.wait_ge(loaded, 1)
                    pe.wait_ge(*u12_copied.now(n))
                    for m in range(NM):
                        mm = pe.matmul(bank[m // 6][DH:P, (m % 6) * DH:(m % 6 + 1) * DH],
                                       ATM[0:DH, m, P + DH:2 * P], TL[0:DH, m, :], start=True, stop=True, skip_group_check=True)
                    mm.then_inc(p1b_ready.sem, 1)

                def merge_d(n):
                    pe.wait_ge(loaded, 1)
                    pe.wait_ge(*p1b_copied.now(n))
                    for m in range(NM):
                        mm = pe.matmul(bank[m // 6][0:DH, (m % 6) * DH:(m % 6 + 1) * DH],
                                       P1B[DH:P, m, :], UF[DH:P, m, DH:P], start=True, stop=True, skip_group_check=True)
                    mm.then_inc(u12b_ready.sem, 1)

                def kb_state(n, s, b):
                    kbT = chans(pa[s], KBT)
                    cols = slice(b * P, (b + 1) * P)
                    pe.wait_ge(*s_copied.now(n, b))
                    pe.wait_ge(*d_ready.now(n, b))
                    for h in range(NH):
                        mm = pe.matmul(bank[h % 2][:, (h // 2) * DH:(h // 2 + 1) * DH],
                                       kbT[head_rows(h), h // 2, cols], S[head_rows(h), h // 2, :], start=True, stop=True)
                    mm.then_inc(r_ready.sem, 1)

                def q_state(n, s, b):
                    qT = chans(pa[s], QT)
                    cols = slice(b * P, (b + 1) * P)
                    pe.wait_ge(*r_copied.now(n, b))
                    for h in range(NH):
                        pe.matmul(bank[h % 2][:, P + (h // 2) * DH:P + (h // 2 + 1) * DH],
                                  qT[head_rows(h), h // 2, cols], S[head_rows(h), h // 2, :],
                                  start=(h < 2), stop=False, skip_group_check=True)

                def updates(n, b, e=None, k=None):
                    if b == 0:
                        pe.wait_ge(*u12b_copied.now(n))
                    if k is not None:
                        pe.wait_ge(*acc_done.now(e, BLK * k))
                    for h in range(NH):
                        mm = pe.matmul(bank[2][:, h * DH:(h + 1) * DH], UF[:, even_heads_first(b, h), :],
                                       R[:, h, :] if b else VB[:, h, :], start=True, stop=True)
                    mm.then_inc(w_ready.sem, 1)

                def state_update(n, s, b, e=None, k=None):
                    ktok = toks(pa[s], KTOK)
                    if k is not None:
                        pe.wait_ge(*he_ready.now(e, k + 1))
                    pe.wait_ge(*w_copied.now(n, b + 1))
                    for h in range(NH):
                        mm = pe.matmul(bank[6][head_rows(h), T + (h // 2) * DH:T + (h // 2 + 1) * DH],
                                       ktok[:, b, h * DH:(h + 1) * DH], W[:, h, :], start=True, stop=True)
                    mm.then_inc(s_ready.sem, 1)

                def outputs(n, b):
                    if b == 0:
                        pe.wait_ge(*u12b_copied.now(n))
                    pe.wait_ge(*w_copied.now(n, b + 1))
                    for h in range(NH):
                        mm = pe.matmul(bank[h % 2][:, P + (h // 2) * DH:P + (h // 2 + 1) * DH],
                                       ATM[:, even_heads_first(b, h), 0:P], W[:, h, :],
                                       start=(b == 0 and h < 2), stop=True, skip_group_check=True)
                    mm.then_inc(o_ready.sem, 1)

                def transpose_stats(it):
                    pe.wait_ge(*std_ready.now(it))
                    pe.wait_ge(*q_ready.before(it))
                    for b in range(BLK):
                        mm = pe.transpose(bank[3][0:GATE_S, b * P:(b + 1) * P],
                                          SG[:, b, :, :, :].rearrange("p r m h -> p (r m h)"), ident[:, :])
                    mm.then_inc(sgT_ready.sem, 1)

                def gate_x(s, m):
                    for a in range(HALF):
                        pe.matmul(mlp_bank[m][:, 0:T], w1g[:, a, m * P:(m + 1) * P], chans(pb[s], XNT)[:, a, :], start=(a == 0), stop=False)

                def gate_s(m):
                    pe.matmul(mlp_bank[m][:, 0:T], w1s[:, m * P:(m + 1) * P], SGT[:, :], start=False, stop=True)\
                        .then_inc(mlp_ready.sem, 1)

                def gate_out(it):
                    pe.wait_ge(*g1_ready.now(it))
                    for b in range(BLK):
                        for m in range(MC):
                            mm = pe.matmul(bank[5][:, b * 4 * NH:(b + 1) * 4 * NH], GH[:, m, b * P:(b + 1) * P], w2g[:, m, :],
                                           start=(m == 0), stop=(m == MC - 1))
                    mm.then_inc(logits_ready.sem, 1)

                def transpose_mixture(it, s):
                    pe.wait_ge(*on_ready.now(it))
                    for a in range(HALF):
                        for b in range(BLK):
                            m = b * NH + a * 2
                            mm = pe.transpose(bank[3 + a][:, b * P:(b + 1) * P],
                                              DL[s][:, m:m + 2, :].rearrange("p m d -> p (m d)"), ident[:, :])
                        mm.then_inc(onT_ready.sem, 1)

                def project_out(it):
                    pe.wait_ge(*onT0_copied.now(it))
                    pe.wait_ge(*onT1_copied.now(it))
                    for b in range(BLK):
                        for a in range(HALF):
                            mm = pe.matmul((bank[5], bank[3])[b // 2][:, (b % 2) * D:(b % 2 + 1) * D], ONT[:, a, b * P:(b + 1) * P],
                                           wo[:, a, :], start=(a == 0), stop=(a == HALF - 1))
                    mm.then_inc(wo_ready.sem, 1)

                def transpose_y(e):
                    pe.wait_ge(*y_ready.now(e))
                    for a in range(HALF):
                        for b in range(BLK):
                            mm = pe.transpose(bank[4 + a][:, b * P:(b + 1) * P],
                                              y[:, b * D + a * P:b * D + (a + 1) * P], ident[:, :])
                        mm.then_inc(yT_ready.sem, 1)

                def route(e):
                    pe.wait_ge(*yT0_copied.now(e))
                    pe.wait_ge(*yT1_copied.now(e))
                    for b in range(BLK):
                        for a in range(HALF):
                            mm = pe.matmul(bank[3][:, b * NE:(b + 1) * NE], YT[:, a, b * P:(b + 1) * P], router[:, a, :],
                                           start=(a == 0), stop=(a == HALF - 1))
                    mm.then_inc(z_ready.sem, 1)

                def hidden(e, k, n=None, b=None):
                    if b is not None:
                        pe.wait_ge(*s_copied.now(n, b + 1))
                    if k:
                        pe.wait_ge(*he_ready.now(e, k))
                    else:
                        pe.wait_ge(*he_ready.before(e))
                    for a in range(HALF):
                        mm = pe.matmul(bank[6][:, 0:T], w1e[:, a, k, :], YT[:, a, :], start=(a == 0), stop=(a == HALF - 1))
                    mm.then_inc(hid_ready.sem, 1)

                def expert_out(e, k, n=None, b=None):
                    if b is not None:
                        pe.wait_ge(*w_copied.now(n, b + 1))
                    pe.wait_ge(*he_ready.now(e, k + 1))
                    if k:
                        pe.wait_ge(*acc_done.now(e, BLK * k))
                    else:
                        pe.wait_ge(*acc_done.before(e))
                    for b in range(BLK):
                        mm = pe.matmul(expert_bank(b), HE[k % 2][:, b * P:(b + 1) * P], w2e[:, k, :], start=True, stop=True)
                    mm.then_inc(eo_ready.sem, 1)

                def body(n=None, it=None, e=None, s=0, npair=None, ipair=None):
                    o = 1 - s
                    have_n, have_it, have_e = n is not None, it is not None, e is not None
                    if have_n:
                        pe.wait_ge(*pa_loaded[o].now(npair))
                        products(n, o, 0)
                        products(n, o, 1)
                        products(n, o, 2)
                    if have_e:
                        transpose_y(e)
                    if have_n:
                        products(n, o, 3)
                    if have_e:
                        route(e)
                    if have_n:
                        products(n, o, 4)
                        pe.wait_ge(*vb_ready.now(n))
                        products(n, o, 5)
                    if have_e:
                        hidden(e, 0)
                    if have_it:
                        pe.wait_ge(*pb_loaded[s].now(ipair))
                        gate_x(s, 0)
                        gate_x(s, 1)
                        transpose_stats(it)
                    if have_n:
                        merge_a(n)
                    if have_it:
                        pe.wait_ge(*sgT_copied.now(it))
                        gate_s(0)
                        gate_s(1)
                        gate_x(s, 2)
                        gate_s(2)
                    if have_n:
                        merge_b(n)
                    if have_it:
                        pe.wait_ge(*g1_ready.now(it, 1))
                        gate_x(s, 3)
                        gate_s(3)
                    if have_n:
                        merge_c(n)
                        merge_d(n)
                    if have_it:
                        gate_out(it)
                    if have_n:
                        updates(n, 0)
                    if have_e:
                        hidden(e, 1)
                        expert_out(e, 0, n, 0) if have_n else expert_out(e, 0)
                    if have_n:
                        state_update(n, o, 0, e, 1) if have_e else state_update(n, o, 0)
                        outputs(n, 0)
                        kb_state(n, o, 1)
                    if have_e:
                        hidden(e, 2, n, 0) if have_n else hidden(e, 2)
                        expert_out(e, 1)
                    if have_n:
                        q_state(n, o, 1)
                    if have_e:
                        hidden(e, 3)
                    if have_n:
                        updates(n, 1, e, 2) if have_e else updates(n, 1)
                    if have_e:
                        expert_out(e, 2, n, 1) if have_n else expert_out(e, 2)
                    if have_n:
                        state_update(n, o, 1, e, 3) if have_e else state_update(n, o, 1)
                        outputs(n, 1)
                        kb_state(n, o, 2)
                    if have_e:
                        hidden(e, 4, n, 1) if have_n else hidden(e, 4)
                        expert_out(e, 3)
                    if have_n:
                        q_state(n, o, 2)
                        updates(n, 2, e, 4) if have_e else updates(n, 2)
                    if have_e:
                        hidden(e, 5)
                        expert_out(e, 4, n, 2) if have_n else expert_out(e, 4)
                    if have_it:
                        transpose_mixture(it, s)
                    if have_n:
                        outputs(n, 2)
                    if have_it:
                        project_out(it)
                    if have_e:
                        expert_out(e, 5)

                body(n=0, s=1, npair=0)
                body(n=1, it=0, s=0, npair=0, ipair=0)
                with pe.Fori(0, NB // 2 - 1) as i:
                    body(2 * i + 2, 2 * i + 1, 2 * i, 1, i + 1, i)
                    body(2 * i + 3, 2 * i + 2, 2 * i + 1, 0, i + 1, i + 1)
                body(it=NB - 1, e=NB - 2, s=1, ipair=NB // 2 - 1)
                body(e=NB - 1, s=0)

            @block.scalar
            def _(act):
                def copy(dst, src):
                    return act.activation(dst, src, ACT.Copy)

                def blocks(n, rows, width):
                    return bank[n][rows, 0:384].rearrange("p (m c) -> p m c", c=width)

                def copy_update(n, b):
                    act.wait_ge(*w_ready.now(n, b + 1))
                    if b == 0:
                        act.wait_ge(*o_ready.before(n))
                    else:
                        act.wait_ge(*o_ready.now(n, b))
                    copy(W[:, :, :].rearrange("p h d -> p (h d)"), bank[2][:, 0:D]).then_inc(w_copied.sem, 1)

                def gelu_gate(it, m):
                    act.wait_ge(*mlp_ready.now(it, m + 1))
                    act.activation(GH[:, m, :], mlp_bank[m][:, 0:T], ACT.Gelu, bias=b1g[:, m:m + 1]).then_inc(g1_ready.sem, 1)

                def gelu_expert(e, k):
                    act.wait_ge(*hid_ready.now(e, k + 1))
                    if k >= 2:
                        act.wait_ge(*eo_ready.now(e, k - 1))
                    else:
                        act.wait_ge(*eo_ready.before(e))
                    act.activation(HE[k % 2][:, :], bank[6][:, 0:T], ACT.Gelu_apprx_tanh).then_inc(he_ready.sem, 1)

                def body(n=None, it=None, e=None, s=0):
                    o = 1 - s
                    have_n, have_it, have_e = n is not None, it is not None, e is not None
                    if have_e:
                        act.wait_ge(*yT_ready.now(e, 1))
                        act.wait_ge(*hid_ready.before(e))
                        copy(YT[:, 0, :], bank[4][:, 0:T]).then_inc(yT0_copied.sem, 1)
                    if have_it:
                        act.wait_ge(*vmax_ready.now(it))
                        act.activation(SG[:, :, :, 1, :].rearrange("p b r h -> p r b h"),
                                       st1[:, :, :].rearrange("p r (b h) -> p r b h", b=BLK), ACT.Sqrt).then_inc(std_ready.sem, 1)
                    if have_e:
                        act.wait_ge(*z_ready.now(e))
                        act.activation(qr[:, :, :].rearrange("p b e -> p (b e)"), bank[3][:, 0:BLK * NE], ACT.Tanh, scale=1.0 / 0.3)\
                            .then_inc(q_ready.sem, 1)
                        act.wait_ge(*lr_ready.now(e))
                        act.activation(ex[:, :, :], rank[:, :, :], ACT.Exp).then_inc(er_ready.sem, 1)
                    if have_it:
                        act.wait_ge(*sgT_ready.now(it))
                        copy(SGT[:, :], bank[3][0:GATE_S, 0:T]).then_inc(sgT_copied.sem, 1)
                    if have_n:
                        act.wait_ge(*p1_ready.now(n))
                        copy(P1[SC:2 * SC, :, :], blocks(0, slice(SC, 2 * SC), SC))
                        copy(P1[3 * SC:P, :, :], blocks(1, slice(3 * SC, P), SC)).then_inc(p1_copied.sem, 1)
                    if have_it:
                        gelu_gate(it, 0)
                        gelu_gate(it, 1)
                        gelu_gate(it, 2)
                    if have_n:
                        act.wait_ge(*u12_ready.now(n))
                        copy(UF[0:SC, :, SC:2 * SC], blocks(0, slice(0, SC), SC))
                        copy(TL[SC:2 * SC, :, 0:SC], blocks(0, slice(SC, 2 * SC), SC))
                        copy(UF[2 * SC:3 * SC, :, 3 * SC:P], blocks(1, slice(2 * SC, 3 * SC), SC)).then_inc(u12_copied.sem, 1)
                    if have_it:
                        gelu_gate(it, 3)
                    if have_n:
                        act.wait_ge(*p1b_ready.now(n))
                        copy(P1B[DH:P, 0:6, :], blocks(0, slice(DH, P), DH))
                        copy(P1B[DH:P, 6:NM, :], blocks(1, slice(DH, P), DH)).then_inc(p1b_copied.sem, 1)
                        act.wait_ge(*u12b_ready.now(n))
                        copy(UF[0:DH, 0:6, DH:P], blocks(0, slice(0, DH), DH))
                        copy(UF[0:DH, 6:NM, DH:P], blocks(1, slice(0, DH), DH)).then_inc(u12b_copied.sem, 1)
                    if have_e:
                        gelu_expert(e, 0)
                    if have_it:
                        act.wait_ge(*lg_ready.now(it))
                        act.activation(WT[:, :, :], L[:, :, :], ACT.Exp).then_inc(wexp_ready.sem, 1)
                    if have_n:
                        copy_update(n, 0)
                    if have_e:
                        gelu_expert(e, 1)
                        gelu_expert(e, 2)
                    if have_n:
                        copy_update(n, 1)
                    if have_it:
                        act.wait_ge(*mix_step.now(it))
                        act.activation(ta[:, :], DL[s][:, :, :].rearrange("p m d -> p (m d)"), ACT.Square).then_inc(sq_ready.sem, 1)
                    if have_e:
                        gelu_expert(e, 3)
                        gelu_expert(e, 4)
                    if have_n:
                        copy_update(n, 2)
                    if have_e:
                        gelu_expert(e, 5)
                    if have_it:
                        act.wait_ge(*onT_ready.now(it, 1))
                        copy(ONT[:, 0, :], bank[3][:, 0:T]).then_inc(onT0_copied.sem, 1)

                body(n=0, s=1)
                body(n=1, it=0, s=0)
                with act.Fori(0, NB // 2 - 1) as i:
                    body(2 * i + 2, 2 * i + 1, 2 * i, 1)
                    body(2 * i + 3, 2 * i + 2, 2 * i + 1, 0)
                body(it=NB - 1, e=NB - 2, s=1)
                body(e=NB - 1, s=0)

            @block.vector
            def _(dve):
                def mask(n, k):
                    e = (k % 2) * (NM // 2) + (k // 2) * 2
                    dve.wait_ge(*qk_ready.now(n, k + 1))
                    dve.tensor_tensor(ATM[:, e:e + 2, :], bank[k % 2][:, :].rearrange("p (m c) -> p m c", m=2),
                                      upper[:, :].unsqueeze(1).broadcast_to([P, 2, 2 * P]), ALU.mult).then_inc(masked.sem, 1)

                def transpose_diagonals(n):
                    dve.wait_ge(*uf_loaded.now(n))
                    dve.wait_ge(*p1b_copied.before(n))
                    dve.transpose(TL[0:SC, :, 0:SC], UF[0:SC, :, 0:SC])
                    dve.transpose(TL[SC:2 * SC, :, SC:2 * SC], UF[SC:2 * SC, :, SC:2 * SC])
                    dve.transpose(TL[2 * SC:3 * SC, :, 0:SC], UF[2 * SC:3 * SC, :, 2 * SC:3 * SC]).then_inc(tdiag_ready.sem, 1)

                def input_stats(n, s, pair):
                    dve.wait_ge(*pb_loaded[s].now(pair))
                    dve.wait_ge(*fl_loaded[s].now(pair))
                    for m in range(NM):
                        dve.bn_stats(ST[:, 0, m, :], heads(pb[s], FSF)[:, m, :])
                        dve.bn_stats(ST[:, 1, m, :], heads(fl[s], 0)[:, m, :])
                        dve.bn_stats(ST[:, 3, m, :], heads(pa[s], VTOK)[:, m, :])

                def remainder(n, b):
                    dve.wait_ge(*r_ready.now(n, b))
                    for odd in range(2):
                        r = dve.tensor_tensor(R[:, odd::2, :], VB[:, b * NH + odd:(b + 1) * NH:2, :],
                                              bank[odd][:, 0:2 * DH].rearrange("p (m d) -> p m d", m=2), ALU.subtract)
                    r.then_inc(r_copied.sem, 1)

                def state(n, b):
                    dve.wait_ge(*s_ready.now(n, b + 1))
                    new = bank[6][:, T:T + 2 * DH].rearrange("p (m d) -> p m d", m=2)
                    if b == 0:
                        dve.tensor_copy(S[:, :, :], new).then_inc(s_copied.sem, 1)
                    else:
                        dve.tensor_tensor(S[:, :, :], S[:, :, :], new, ALU.add).then_inc(s_copied.sem, 1)

                def delta_out(n, s, b):
                    rq = pa[s][:, RQ:RQ + NM].rearrange("p (b h) -> p b h", b=BLK)
                    dve.wait_ge(*o_ready.now(n, b + 1))
                    for odd in range(2):
                        d = dve.tensor_tensor(DL[s][:, b * NH + odd:(b + 1) * NH:2, :],
                                              bank[odd][:, P:P + 2 * DH].rearrange("p (m d) -> p m d", m=2),
                                              rq[:, b, odd::2].unsqueeze(2).broadcast_to([P, 2, DH]), ALU.mult)
                    d.then_inc(d_ready.sem, 1)

                def branch_statistics(n, s):
                    dve.wait_ge(*d_ready.now(n))
                    for m in range(NM):
                        ins = dve.bn_stats(ST[:, 2, m, :], DL[s][:, m, :])
                    ins.then_inc(branch_stats.sem, 1)
                    dve.wait_ge(*branch_stats.now(n))
                    dve.wait_ge(*sgT_ready.before(n))
                    dve.tensor_tensor(st1[:, :, :], ST[:, :, :, 1], ST[:, :, :, 4], ALU.add)
                    dve.tensor_tensor(st2[:, :, :], ST[:, :, :, 1], ST[:, :, :, 4], ALU.subtract)
                    dve.tensor_tensor(st3[:, :, :], ST[:, :, :, 2], ST[:, :, :, 5], ALU.add).then_inc(stat_step.sem, 1)
                    dve.wait_ge(*stat_step.now(n, 1))
                    dve.tensor_scalar(SG[:, :, :, 0, :].rearrange("p b r h -> p r b h"),
                                      st1[:, :, :].rearrange("p r (b h) -> p r b h", b=BLK), 0.5, None, ALU.mult).then_inc(stat_step.sem, 1)
                    dve.tensor_tensor(st4[:, :, :], st2[:, :, :], st2[:, :, :], ALU.mult)
                    dve.tensor_scalar(st3[:, :, :], st3[:, :, :], 1.0 / DH, None, ALU.mult).then_inc(stat_step.sem, 1)
                    dve.wait_ge(*stat_step.now(n, 3))
                    dve.scalar_tensor_tensor(out=st2[:, :, :], in0=st4[:, :, :], scalar=0.25, in1=st3[:, :, :],
                                             op0=ALU.mult, op1=ALU.add).then_inc(stat_step.sem, 1)
                    dve.wait_ge(*stat_step.now(n, 4))
                    dve.tensor_scalar(st1[:, :, :], st2[:, :, :], 1e-6, None, ALU.max).then_inc(vmax_ready.sem, 1)

                def gate_logits(it):
                    dve.wait_ge(*logits_ready.now(it))
                    dve.tensor_tensor(L[:, :, :].rearrange("p (b h) r -> p b (h r)", b=BLK),
                                      bank[5][:, 0:BLK * 4 * NH].rearrange("p (b n) -> p b n", b=BLK),
                                      b2g[:, :].unsqueeze(1).broadcast_to([P, BLK, 4 * NH]), ALU.add).then_inc(gate_step.sem, 1)
                    dve.wait_ge(*gate_step.now(it, 1))
                    lv = L[:, :, :].rearrange("p (b h) r -> p b h r", b=BLK)
                    dve.tensor_tensor(lv, lv, itemp[:, :].unsqueeze(1).unsqueeze(3).broadcast_to([P, BLK, NH, 4]), ALU.mult)\
                        .then_inc(gate_step.sem, 1)
                    dve.wait_ge(*gate_step.now(it, 2))
                    dve.tensor_reduce(m12[:, :], L[:, :, :], AX.X, ALU.max).then_inc(gate_step.sem, 1)
                    dve.wait_ge(*gate_step.now(it, 3))
                    dve.tensor_tensor(L[:, :, :], L[:, :, :], m12[:, :].unsqueeze(2).broadcast_to([P, NM, 4]), ALU.subtract)\
                        .then_inc(lg_ready.sem, 1)

                def gate_weights(it):
                    dve.wait_ge(*wexp_ready.now(it))
                    dve.tensor_reduce(s12[:, :], WT[:, :, :], AX.X, ALU.add).then_inc(wt_step.sem, 1)
                    dve.wait_ge(*wt_step.now(it, 1))
                    dve.reciprocal(r12[:, :], s12[:, :]).then_inc(wt_step.sem, 1)
                    dve.wait_ge(*wt_step.now(it, 2))
                    dve.tensor_tensor(WT[:, :, :], WT[:, :, :], r12[:, :].unsqueeze(2).broadcast_to([P, NM, 4]), ALU.mult)\
                        .then_inc(wt_step.sem, 1)

                def mix_own(it, s):
                    dve.wait_ge(*wt_step.now(it, 3))
                    dve.tensor_tensor(DL[s][:, :, :], DL[s][:, :, :], WT[:, :, 2:3].broadcast_to([P, NM, DH]), ALU.mult)\
                        .then_inc(mix_step.sem, 1)
                    dve.tensor_tensor(tc_[:, :, :], heads(fl[s], 0), WT[:, :, 1:2].broadcast_to([P, NM, DH]), ALU.mult)\
                        .then_inc(mix_step.sem, 1)

                def mix_add(it, s, step, other):
                    dve.wait_ge(*mix_step.now(it, step))
                    dve.tensor_tensor(DL[s][:, :, :], DL[s][:, :, :], other, ALU.add).then_inc(mix_step.sem, 1)

                def mean_squares(it):
                    dve.wait_ge(*sq_ready.now(it))
                    dve.tensor_reduce(s12[:, :], ta[:, :].rearrange("p (m d) -> p m d", d=DH), AX.X, ALU.add).then_inc(ss_ready.sem, 1)
                    dve.wait_ge(*ss_ready.now(it))
                    dve.tensor_scalar(m12[:, :], s12[:, :], 1.0 / DH, 1e-5, ALU.mult, ALU.add).then_inc(ms_ready.sem, 1)

                def normed_mixture(it, s):
                    dve.wait_ge(*rr_ready.now(it))
                    dve.tensor_tensor(DL[s][:, :, :], DL[s][:, :, :], r12[:, :].unsqueeze(2).broadcast_to([P, NM, DH]), ALU.mult)\
                        .then_inc(on_ready.sem, 1)

                def residual(it, s):
                    hf = field(pb[s], HF)
                    ha = HA[s][:, :, :].rearrange("p b n -> p (b n)")
                    dve.wait_ge(*wo_ready.now(it))
                    dve.wait_ge(*out_stored.before(it, 2))
                    dve.tensor_tensor(ha[:, 0:2 * D], hf[:, 0:2 * D], bank[5][:, :], ALU.add)
                    dve.tensor_tensor(ha[:, 2 * D:], hf[:, 2 * D:], bank[3][:, 0:D], ALU.add).then_inc(h2_ready.sem, 1)
                    dve.wait_ge(*h2_ready.now(it))
                    for b in range(BLK):
                        ins = dve.bn_stats(bst[:, b, :], HA[s][:, b, :])
                    ins.then_inc(bst_ready.sem, 1)
                    dve.wait_ge(setup, 1)
                    dve.wait_ge(*bst_ready.now(it))
                    for b in range(BLK):
                        ins = dve.bn_aggr(bmv[:, b, :], bst[:, b, :])
                    ins.then_inc(bmv_ready.sem, 1)
                    dve.wait_ge(*bmv_ready.now(it))
                    dve.tensor_scalar(bv[:, :], bmv[:, :, 1], 1e-5, None, ALU.add).then_inc(veps_ready.sem, 1)

                def second_norm(e, s):
                    dve.wait_ge(*rstd_ready.now(e))
                    for b in range(BLK):
                        dve.tensor_scalar(y[:, b * D:(b + 1) * D], HA[s][:, b, :], bmv[:, b, 0:1], br[:, b:b + 1],
                                          ALU.subtract, ALU.mult).then_inc(y_ready.sem, 1)

                def routing_logits(e):
                    dve.wait_ge(*q_ready.now(e))
                    dve.tensor_tensor(cmp[:, :, :, :], qr[:, :, :].unsqueeze(2).broadcast_to([P, BLK, NE, ND]),
                                      anchors[:, :, :].unsqueeze(1).broadcast_to([P, BLK, NE, ND]), ALU.mult).then_inc(route_step.sem, 1)
                    dve.wait_ge(*route_step.now(e, 1))
                    dve.tensor_reduce(lg[:, :, :], cmp[:, :, :, :], AX.X, ALU.add).then_inc(route_step.sem, 1)
                    dve.wait_ge(*route_step.now(e, 2))
                    dve.tensor_scalar(we[:, :, :], lg[:, :, :], -float(ND), 0.5, ALU.add, ALU.mult).then_inc(route_step.sem, 1)
                    dve.wait_ge(*route_step.now(e, 3))
                    dve.tensor_scalar(lg[:, :, :], we[:, :, :], rclip[:, 0:1], None, ALU.mult).then_inc(route_step.sem, 1)
                    dve.wait_ge(*route_step.now(e, 4))
                    other = lg[:, :, :].unsqueeze(2).broadcast_to([P, BLK, NE, NE])
                    own = lg[:, :, :].unsqueeze(3).broadcast_to([P, BLK, NE, NE])
                    dve.tensor_tensor(cmp[:, :, :, :], other, own, ALU.is_gt)
                    dve.tensor_tensor(eqs[:, :, :, :], other, own, ALU.is_equal)
                    dve.tensor_reduce(me[:, :], lg[:, :, :], AX.X, ALU.max).then_inc(route_step.sem, 1)
                    dve.wait_ge(*route_step.now(e, 5))
                    dve.tensor_tensor(eqs[:, :, :, :], eqs[:, :, :, :], before_e[:, :, :].unsqueeze(1).broadcast_to([P, BLK, NE, NE]), ALU.mult)\
                        .then_inc(route_step.sem, 1)
                    dve.tensor_tensor(rank[:, :, :], lg[:, :, :], me[:, :].unsqueeze(2).broadcast_to([P, BLK, NE]), ALU.subtract)\
                        .then_inc(lr_ready.sem, 1)
                    dve.wait_ge(*route_step.now(e, 6))
                    dve.tensor_tensor(cmp[:, :, :, :], cmp[:, :, :, :], eqs[:, :, :, :], ALU.add).then_inc(route_step.sem, 1)
                    dve.wait_ge(*route_step.now(e, 7))
                    dve.tensor_reduce(we[:, :, :], cmp[:, :, :, :], AX.X, ALU.add).then_inc(route_step.sem, 1)
                    dve.wait_ge(*route_step.now(e, 8))
                    dve.tensor_scalar(lg[:, :, :], we[:, :, :], 1.5, None, ALU.is_lt).then_inc(route_step.sem, 1)

                def routing_weights(e):
                    dve.wait_ge(*er_ready.now(e))
                    dve.wait_ge(*route_step.now(e, 9))
                    dve.tensor_tensor(ex[:, :, :], ex[:, :, :], lg[:, :, :], ALU.mult).then_inc(we_step.sem, 1)
                    dve.wait_ge(*we_step.now(e, 1))
                    dve.tensor_reduce(se[:, :], ex[:, :, :], AX.X, ALU.add).then_inc(we_step.sem, 1)
                    dve.wait_ge(*we_step.now(e, 2))
                    dve.reciprocal(re[:, :], se[:, :]).then_inc(we_step.sem, 1)
                    dve.wait_ge(*we_step.now(e, 3))
                    dve.tensor_tensor(we[:, :, :], ex[:, :, :], re[:, :].unsqueeze(2).broadcast_to([P, BLK, NE]), ALU.mult)\
                        .then_inc(we_step.sem, 1)

                def add_expert(e, s, k):
                    if k == 0:
                        dve.wait_ge(*we_step.now(e, 4))
                    dve.wait_ge(*eo_ready.now(e, k + 1))
                    for b in range(BLK):
                        if k:
                            dve.wait_ge(*acc_done.now(e, BLK * (k - 1) + b + 1))
                        dve.scalar_tensor_tensor(out=HA[s][:, b, :], in0=expert_bank(b),
                                                 scalar=we[:, b, k:k + 1], in1=HA[s][:, b, :], op0=ALU.mult, op1=ALU.add)\
                            .then_inc(acc_done.sem, 1)

                def body(n=None, it=None, e=None, s=0, npair=None, more=True):
                    o = 1 - s
                    have_n, have_it, have_e = n is not None, it is not None, e is not None
                    if have_e:
                        dve.wait_ge(*yT_ready.now(e, 2))
                        dve.tensor_copy(YT[:, 1, :], bank[5][:, 0:T]).then_inc(yT1_copied.sem, 1)
                    if have_n:
                        mask(n, 2)
                        mask(n, 3)
                    if have_it:
                        branch_statistics(it, s)
                    if have_n:
                        mask(n, 4)
                        mask(n, 5)
                    if have_e:
                        routing_logits(e)
                    if have_n:
                        transpose_diagonals(n)
                    if have_e:
                        routing_weights(e)
                    if have_n:
                        input_stats(n, o, npair)
                    if have_it:
                        gate_logits(it)
                        gate_weights(it)
                        mix_own(it, s)
                    if have_e:
                        add_expert(e, o, 0)
                    if have_n:
                        state(n, 0)
                        delta_out(n, o, 0)
                        remainder(n, 1)
                    if have_it:
                        mix_add(it, s, 2, tc_[:, :, :])
                    if have_e:
                        add_expert(e, o, 1)
                    if have_it:
                        dve.wait_ge(*fsw_ready.now(it))
                        mix_add(it, s, 3, ta[:, :].rearrange("p (m d) -> p m d", d=DH))
                        dve.wait_ge(*vw_ready.now(it))
                        mix_add(it, s, 4, tb[:, :].rearrange("p (m d) -> p m d", d=DH))
                    if have_e:
                        add_expert(e, o, 2)
                    if have_n:
                        state(n, 1)
                        delta_out(n, o, 1)
                        remainder(n, 2)
                    if have_it:
                        mean_squares(it)
                    if have_e:
                        add_expert(e, o, 3)
                    if have_it:
                        normed_mixture(it, s)
                        dve.wait_ge(*onT_ready.now(it, 2))
                        dve.tensor_copy(ONT[:, 1, :], bank[4][:, 0:T]).then_inc(onT1_copied.sem, 1)
                    if have_e:
                        add_expert(e, o, 4)
                    if have_n:
                        delta_out(n, o, 2)
                    if have_it:
                        residual(it, s)
                    if more:
                        mask(n + 1, 0)
                        mask(n + 1, 1)
                    if have_it:
                        second_norm(it, s)
                    if have_e:
                        add_expert(e, o, 5)

                mask(0, 0)
                mask(0, 1)
                body(n=0, s=1, npair=0)
                body(n=1, it=0, s=0, npair=0)
                with dve.Fori(0, NB // 2 - 2) as i:
                    body(2 * i + 2, 2 * i + 1, 2 * i, 1, i + 1)
                    body(2 * i + 3, 2 * i + 2, 2 * i + 1, 0, i + 1)
                body(NB - 2, NB - 3, NB - 4, 1, NB // 2 - 1)
                body(NB - 1, NB - 2, NB - 3, 0, NB // 2 - 1, more=False)
                body(it=NB - 1, e=NB - 2, s=1, more=False)
                body(e=NB - 1, s=0, more=False)

            @block.gpsimd
            def _(pool):
                def body(n=None, it=None, e=None, s=0, npair=None):
                    o = 1 - s
                    if n is not None:
                        pool.wait_ge(*pa_loaded[o].now(npair))
                        pool.wait_ge(*r_copied.before(n))
                        pool.tensor_tensor(VB[:, :, :], heads(pa[o], VTOK),
                                           pa[o][:, VBS:VBS + NM].unsqueeze(2).broadcast_to([P, NM, DH]), ALU.mult)\
                            .then_inc(vb_ready.sem, 1)
                    if it is not None:
                        pool.wait_ge(*wt_step.now(it))
                        pool.tensor_tensor(ta[:, :].rearrange("p (m d) -> p m d", d=DH), heads(pb[s], FSF),
                                           WT[:, :, 0:1].broadcast_to([P, NM, DH]), ALU.mult).then_inc(fsw_ready.sem, 1)
                        pool.tensor_tensor(tb[:, :].rearrange("p (m d) -> p m d", d=DH), heads(pa[s], VTOK),
                                           WT[:, :, 3:4].broadcast_to([P, NM, DH]), ALU.mult).then_inc(vw_ready.sem, 1)
                        pool.wait_ge(*ms_ready.now(it))
                        pool.tensor_tensor(r12[:, :], m12[:, :], minus_half[:, :], ALU.pow).then_inc(rr_ready.sem, 1)
                        pool.wait_ge(*veps_ready.now(it))
                        pool.tensor_tensor(br[:, :], bv[:, :], minus_half[:, 0:BLK], ALU.pow).then_inc(rstd_ready.sem, 1)

                body(n=0, s=1, npair=0)
                body(n=1, it=0, s=0, npair=0)
                with pool.Fori(0, NB // 2 - 1) as i:
                    body(2 * i + 2, 2 * i + 1, 2 * i, 1, i + 1)
                    body(2 * i + 3, 2 * i + 2, 2 * i + 1, 0, i + 1)
                body(it=NB - 1, e=NB - 2, s=1)
                body(e=NB - 1, s=0)


_ATTN = ["Wq", "Wk", "Wv", "Wb", "conv_q_w", "conv_k_w", "conv_v_w", "fir_short_w", "fir_long_w", "mlp_w1", "mlp_b1",
         "mlp_w2", "mlp_b2", "gate_log_temp", "o_norm_w", "Wo"]
_FFN = ["proj_w", "anchors", "routing_temp", "w1", "w2"]


def kernel(**inputs):
    import numpy as _np
    import concourse.bacc as _bacc
    from concourse import mybir as _mybir
    from concourse.bass_utils import run_bass_kernel_spmd as _run

    nc = _bacc.Bacc("TRN2", target_bir_lowering=False, num_devices=1)
    arrays = {}

    def give(name):
        a = _np.ascontiguousarray(inputs[name])
        a = a.reshape(1) if a.ndim == 0 else a
        arrays[f"in_{name}_dram"] = a
        return nc.dram_tensor(f"in_{name}_dram", a.shape, _mybir.dt.from_np(a.dtype), kind="ExternalInput").ap()

    x = give("x")
    w = {n: give(f"L0_attn_{n}") for n in _ATTN}
    w |= {f"ffn_{n}": give(f"L0_ffn_{n}") for n in _FFN}
    out = nc.dram_tensor("out_0_dram", (x.shape[0], T, D), F32, kind="ExternalOutput").ap()
    audio_tower(nc, x, w, out)
    r = _run(nc, [arrays], core_ids=[0])
    return r.results[0]["out_0_dram"]
```
